# Optimizing a Trainium2 kernel written in Bass

```python
import numpy as np
import jax
import jax.numpy as jnp

def _softmax(x, axis=-1):
    return jax.nn.softmax(x, axis=axis)

def _gelu(x):
    return jax.nn.gelu(x, approximate=True)

def _silu(x):
    return jax.nn.silu(x)

def _sigmoid(x):
    return jax.nn.sigmoid(x)

def _layernorm(x, axis=-1, eps=1e-05):
    m = jnp.mean(x, axis=axis, keepdims=True)
    v = jnp.var(x, axis=axis, keepdims=True)
    return (x - m) / jnp.sqrt(v + eps)

def _scatter_add(tgt, idx, src, axis=0):
    return tgt.at[idx].add(src)

def _segment_sum(src, seg, n):
    return jax.ops.segment_sum(src, seg, n)
kernel_name = 'mk_decoder_preln_d1_seqx_r8_b1de40'

def setup_inputs(seed: int=0):
    np.random.seed(seed)
    _w = jnp.asarray

    def _rec_inputs():
        import jax
        import jax.numpy as jnp
        _rk = jax.random.key(seed)
        x = -0.000125 + 0.9999 * jax.random.normal(jax.random.fold_in(_rk, 1), (4, 256, 256), jnp.float32)
        _lenS = 256 - jax.random.randint(jax.random.fold_in(_rk, 7), (4,), 0, max(1, 256 // 4) + 1, jnp.int32)
        _lenS2 = 256 - jax.random.randint(jax.random.fold_in(_rk, 8), (4,), 0, max(1, 256 // 4) + 1, jnp.int32)
        _ctx_2048P = jax.random.normal(jax.random.fold_in(_rk, 11), (4, 16, 256), jnp.float32)
        _ctx_2048c = jax.random.dirichlet(jax.random.fold_in(_rk, 511), 0.3 * jnp.ones((16,), jnp.float32), (4, 256))
        _ctx_2048t = jnp.einsum('bsk,bkd->bsd', _ctx_2048c, _ctx_2048P)
        _ctx_2048t = _ctx_2048t * jax.lax.rsqrt(jnp.mean(jnp.square(_ctx_2048t)) + 1e-12) * 0.953939
        ctx_2048 = 1.72703e-05 + 1.00003 * (_ctx_2048t + 0.3 * jax.random.normal(jax.random.fold_in(_rk, 611), (4, 256, 256), jnp.float32))
        return (x, ctx_2048)
    x, ctx_2048 = _rec_inputs()

    def _L0_attn_setup():
        import jax, jax.numpy as jnp
        import numpy as np
        NUM_HEADS = 16
        GROUP_SIZE = 4
        RMS_EPS = 1e-06

        def _rope_cos_sin(S, head_dim):
            inv_freq = 1.0 / 10000.0 ** (jnp.arange(0, head_dim, 2, dtype=jnp.float32) / head_dim)
            t = jnp.arange(S, dtype=jnp.float32)
            angles = t[:, None] * inv_freq[None, :]
            return (jnp.cos(angles), jnp.sin(angles))

        def _apply_rope(x, cos, sin):
            B, S, h, hd = x.shape
            xr = x.reshape(B, S, h, hd // 2, 2)
            x0, x1 = (xr[..., 0], xr[..., 1])
            c = cos[None, :, None, :]
            s = sin[None, :, None, :]
            o0 = x0 * c - x1 * s
            o1 = x0 * s + x1 * c
            return jnp.stack([o0, o1], axis=-1).reshape(B, S, h, hd)
        key = jax.random.key(seed)
        k1, k2, k3 = jax.random.split(key, 3)
        B, S, H = (4, 256, 256)
        g = GROUP_SIZE
        x = jax.random.normal(k1, (B, S, H), dtype=jnp.float32)
        w_attn = jax.random.normal(k2, (H, H + 2 * H // g), dtype=jnp.float32) * 0.02
        w_proj = jax.random.normal(k3, (H, H), dtype=jnp.float32) * 0.02
        norm_w = jnp.ones((H,), dtype=jnp.float32)
        return {'x': x, 'w_attn': w_attn, 'w_proj': w_proj, 'norm_w': norm_w}
    _L0_attn_all = _L0_attn_setup()
    _L0_attn_in = {k: v for k, v in _L0_attn_all.items() if k in ('w_attn', 'w_proj', 'norm_w')}
    del _L0_attn_all

    def _L0_xattn_setup():
        import jax, jax.numpy as jnp
        import numpy as np
        DIM = 256
        NH = 16
        HD = DIM // NH
        EPS = 1e-06
        IMG_LEN = 257

        def rms_norm(x, w, eps=EPS):
            xf = x.astype(jnp.float32)
            y = xf * jax.lax.rsqrt(jnp.mean(xf * xf, axis=-1, keepdims=True) + eps)
            return y.astype(x.dtype) * w

        def linear(x, w, b):
            return jnp.einsum('blc,oc->blo', x, w) + b

        def attention(q, k, v):
            scale = 1.0 / jnp.sqrt(jnp.asarray(HD, q.dtype))
            scores = jnp.einsum('bqhd,bkhd->bhqk', q, k) * scale
            probs = jax.nn.softmax(scores, axis=-1)
            return jnp.einsum('bhqk,bkhd->bqhd', probs, v)
        key = jax.random.key(seed)
        ks = jax.random.split(key, 12)
        B, L = (2, 1024)
        s = 0.02
        inp = {'x': jax.random.normal(ks[0], (B, L, DIM), jnp.float32), 'context': jax.random.normal(ks[1], (B, 769, DIM), jnp.float32), 'q_w': jax.random.normal(ks[2], (DIM, DIM), jnp.float32) * s, 'q_b': jnp.zeros((DIM,), jnp.float32), 'k_w': jax.random.normal(ks[3], (DIM, DIM), jnp.float32) * s, 'k_b': jnp.zeros((DIM,), jnp.float32), 'v_w': jax.random.normal(ks[4], (DIM, DIM), jnp.float32) * s, 'v_b': jnp.zeros((DIM,), jnp.float32), 'k_img_w': jax.random.normal(ks[5], (DIM, DIM), jnp.float32) * s, 'k_img_b': jnp.zeros((DIM,), jnp.float32), 'v_img_w': jax.random.normal(ks[6], (DIM, DIM), jnp.float32) * s, 'v_img_b': jnp.zeros((DIM,), jnp.float32), 'o_w': jax.random.normal(ks[7], (DIM, DIM), jnp.float32) * s, 'o_b': jnp.zeros((DIM,), jnp.float32), 'norm_q_w': jnp.ones((DIM,), jnp.float32), 'norm_k_w': jnp.ones((DIM,), jnp.float32), 'norm_k_img_w': jnp.ones((DIM,), jnp.float32)}
        return inp
    _L0_xattn_all = _L0_xattn_setup()
    _L0_xattn_in = {k: v for k, v in _L0_xattn_all.items() if k in ('q_w', 'q_b', 'k_w', 'k_b', 'v_w', 'v_b', 'k_img_w', 'k_img_b', 'v_img_w', 'v_img_b', 'o_w', 'o_b', 'norm_q_w', 'norm_k_w', 'norm_k_img_w')}
    del _L0_xattn_all

    def _L0_ffn_setup():
        import jax, jax.numpy as jnp
        import numpy as np
        TOP_K = 2
        key = jax.random.key(seed)
        ks = jax.random.split(key, 6)
        B, S, H, F, E = (1, 256, 256, 176, 8)
        Fs = 2 * F
        std = jnp.float32(0.02)
        return {'hidden_states': jax.random.normal(ks[0], (B, S, H), jnp.float32), 'gate_weight': jax.random.normal(ks[1], (E, H), jnp.float32) * std, 'gate_up_weights': jax.random.normal(ks[2], (E, 2 * F, H), jnp.float32) * std, 'down_weights': jax.random.normal(ks[3], (E, H, F), jnp.float32) * std, 'shared_gate_up': jax.random.normal(ks[4], (2 * Fs, H), jnp.float32) * std, 'shared_down': jax.random.normal(ks[5], (H, Fs), jnp.float32) * std}
    _L0_ffn_all = _L0_ffn_setup()
    _L0_ffn_in = {k: v for k, v in _L0_ffn_all.items() if k in ('gate_weight', 'gate_up_weights', 'down_weights', 'shared_gate_up', 'shared_down')}
    del _L0_ffn_all
    return {'x': x, 'ctx_2048': ctx_2048, 'L0_attn_w_attn': _L0_attn_in['w_attn'], 'L0_attn_w_proj': _L0_attn_in['w_proj'], 'L0_attn_norm_w': _L0_attn_in['norm_w'], 'L0_xattn_q_w': _L0_xattn_in['q_w'], 'L0_xattn_q_b': _L0_xattn_in['q_b'], 'L0_xattn_k_w': _L0_xattn_in['k_w'], 'L0_xattn_k_b': _L0_xattn_in['k_b'], 'L0_xattn_v_w': _L0_xattn_in['v_w'], 'L0_xattn_v_b': _L0_xattn_in['v_b'], 'L0_xattn_k_img_w': _L0_xattn_in['k_img_w'], 'L0_xattn_k_img_b': _L0_xattn_in['k_img_b'], 'L0_xattn_v_img_w': _L0_xattn_in['v_img_w'], 'L0_xattn_v_img_b': _L0_xattn_in['v_img_b'], 'L0_xattn_o_w': _L0_xattn_in['o_w'], 'L0_xattn_o_b': _L0_xattn_in['o_b'], 'L0_xattn_norm_q_w': _L0_xattn_in['norm_q_w'], 'L0_xattn_norm_k_w': _L0_xattn_in['norm_k_w'], 'L0_xattn_norm_k_img_w': _L0_xattn_in['norm_k_img_w'], 'L0_ffn_gate_weight': _L0_ffn_in['gate_weight'], 'L0_ffn_gate_up_weights': _L0_ffn_in['gate_up_weights'], 'L0_ffn_down_weights': _L0_ffn_in['down_weights'], 'L0_ffn_shared_gate_up': _L0_ffn_in['shared_gate_up'], 'L0_ffn_shared_down': _L0_ffn_in['shared_down']}

def reference(x, ctx_2048, L0_attn_w_attn, L0_attn_w_proj, L0_attn_norm_w, L0_xattn_q_w, L0_xattn_q_b, L0_xattn_k_w, L0_xattn_k_b, L0_xattn_v_w, L0_xattn_v_b, L0_xattn_k_img_w, L0_xattn_k_img_b, L0_xattn_v_img_w, L0_xattn_v_img_b, L0_xattn_o_w, L0_xattn_o_b, L0_xattn_norm_q_w, L0_xattn_norm_k_w, L0_xattn_norm_k_img_w, L0_ffn_gate_weight, L0_ffn_gate_up_weights, L0_ffn_down_weights, L0_ffn_shared_gate_up, L0_ffn_shared_down):
    import jax
    import jax.numpy as jnp

    def _L0_attn_ref(x, w_attn, w_proj, norm_w):
        import jax, jax.numpy as jnp
        import numpy as np
        NUM_HEADS = 16
        GROUP_SIZE = 4
        RMS_EPS = 1e-06

        def _rope_cos_sin(S, head_dim):
            inv_freq = 1.0 / 10000.0 ** (jnp.arange(0, head_dim, 2, dtype=jnp.float32) / head_dim)
            t = jnp.arange(S, dtype=jnp.float32)
            angles = t[:, None] * inv_freq[None, :]
            return (jnp.cos(angles), jnp.sin(angles))

        def _apply_rope(x, cos, sin):
            B, S, h, hd = x.shape
            xr = x.reshape(B, S, h, hd // 2, 2)
            x0, x1 = (xr[..., 0], xr[..., 1])
            c = cos[None, :, None, :]
            s = sin[None, :, None, :]
            o0 = x0 * c - x1 * s
            o1 = x0 * s + x1 * c
            return jnp.stack([o0, o1], axis=-1).reshape(B, S, h, hd)
        B, S, H = x.shape
        nh = NUM_HEADS
        g = GROUP_SIZE
        nkv = nh // g
        hd = H // nh
        ghd = H // g
        qkv = jnp.einsum('bsh,hf->bsf', x, w_attn)
        q = qkv[..., :H].reshape(B, S, nh, hd)
        k = qkv[..., H:H + ghd].reshape(B, S, nkv, hd)
        v = qkv[..., H + ghd:].reshape(B, S, nkv, hd)
        cos, sin = _rope_cos_sin(S, hd)
        q = _apply_rope(q, cos, sin)
        k = _apply_rope(k, cos, sin)
        q = q.transpose(0, 2, 1, 3)
        k = jnp.repeat(k.transpose(0, 2, 1, 3), g, axis=1)
        v = jnp.repeat(v.transpose(0, 2, 1, 3), g, axis=1)
        scale = 1.0 / jnp.sqrt(jnp.float32(hd))
        scores = jnp.einsum('bhqd,bhkd->bhqk', q, k) * scale
        causal = jnp.tril(jnp.ones((S, S), dtype=bool))
        scores = jnp.where(causal[None, None], scores, jnp.finfo(scores.dtype).min)
        attn = jax.nn.softmax(scores, axis=-1)
        y = jnp.einsum('bhqk,bhkd->bhqd', attn, v)
        y = y.transpose(0, 2, 1, 3).reshape(B, S, H)
        y = jnp.einsum('bsh,ho->bso', y, w_proj)
        rms = jnp.sqrt(jnp.mean(jnp.square(y), axis=-1, keepdims=True) + RMS_EPS)
        return y / rms * norm_w

    def _L0_xattn_ref(x, context, q_w, q_b, k_w, k_b, v_w, v_b, k_img_w, k_img_b, v_img_w, v_img_b, o_w, o_b, norm_q_w, norm_k_w, norm_k_img_w):
        import jax, jax.numpy as jnp
        import numpy as np
        DIM = 256
        NH = 16
        HD = DIM // NH
        EPS = 1e-06
        IMG_LEN = 257

        def rms_norm(x, w, eps=EPS):
            xf = x.astype(jnp.float32)
            y = xf * jax.lax.rsqrt(jnp.mean(xf * xf, axis=-1, keepdims=True) + eps)
            return y.astype(x.dtype) * w

        def linear(x, w, b):
            return jnp.einsum('blc,oc->blo', x, w) + b

        def attention(q, k, v):
            scale = 1.0 / jnp.sqrt(jnp.asarray(HD, q.dtype))
            scores = jnp.einsum('bqhd,bkhd->bhqk', q, k) * scale
            probs = jax.nn.softmax(scores, axis=-1)
            return jnp.einsum('bhqk,bkhd->bqhd', probs, v)
        B, L, _ = x.shape
        ctx_img = context[:, :IMG_LEN]
        ctx_txt = context[:, IMG_LEN:]
        q = rms_norm(linear(x, q_w, q_b), norm_q_w).reshape(B, L, NH, HD)
        k = rms_norm(linear(ctx_txt, k_w, k_b), norm_k_w).reshape(B, -1, NH, HD)
        v = linear(ctx_txt, v_w, v_b).reshape(B, -1, NH, HD)
        k_img = rms_norm(linear(ctx_img, k_img_w, k_img_b), norm_k_img_w).reshape(B, -1, NH, HD)
        v_img = linear(ctx_img, v_img_w, v_img_b).reshape(B, -1, NH, HD)
        img_x = attention(q, k_img, v_img)
        txt_x = attention(q, k, v)
        out = (txt_x + img_x).reshape(B, L, DIM)
        return linear(out, o_w, o_b)

    def _L0_ffn_ref(hidden_states, gate_weight, gate_up_weights, down_weights, shared_gate_up, shared_down):
        import jax, jax.numpy as jnp
        import numpy as np
        TOP_K = 2
        B, S, H = hidden_states.shape
        E, twoF, _ = gate_up_weights.shape
        F = twoF // 2
        T = B * S
        x = hidden_states.reshape(T, H)
        logits = x @ gate_weight.T
        scores = jax.nn.softmax(logits, axis=-1)
        topk_w, topk_idx = jax.lax.top_k(scores, TOP_K)
        combine = jnp.zeros((T, E), x.dtype).at[jnp.arange(T)[:, None], topk_idx].add(topk_w)
        gu = jnp.einsum('th,efh->tef', x, gate_up_weights)
        act = jax.nn.silu(gu[..., :F]) * gu[..., F:]
        y = jnp.einsum('tef,te,ehf->th', act, combine, down_weights)
        Fs = shared_gate_up.shape[0] // 2
        sgu = x @ shared_gate_up.T
        sact = jax.nn.silu(sgu[:, :Fs]) * sgu[:, Fs:]
        y = y + sact @ shared_down.T
        return y.reshape(B, S, H)
    x = x + _L0_attn_ref(_layernorm(x, axis=-1), L0_attn_w_attn, L0_attn_w_proj, L0_attn_norm_w)
    x = x + _L0_xattn_ref(_layernorm(x, axis=-1), ctx_2048, L0_xattn_q_w, L0_xattn_q_b, L0_xattn_k_w, L0_xattn_k_b, L0_xattn_v_w, L0_xattn_v_b, L0_xattn_k_img_w, L0_xattn_k_img_b, L0_xattn_v_img_w, L0_xattn_v_img_b, L0_xattn_o_w, L0_xattn_o_b, L0_xattn_norm_q_w, L0_xattn_norm_k_w, L0_xattn_norm_k_img_w)
    x = x + _L0_ffn_ref(_layernorm(x, axis=-1), L0_ffn_gate_weight, L0_ffn_gate_up_weights, L0_ffn_down_weights, L0_ffn_shared_gate_up, L0_ffn_shared_down)
    return x

_drawn_inputs = setup_inputs


def setup_inputs(seed=0):
    import zlib

    import numpy as np

    out = dict(_drawn_inputs(seed))
    spreads = {'L0_attn_norm_w': (1.0, 0.2),
     'L0_xattn_q_b': (0.0, 2.0),
     'L0_xattn_k_b': (0.0, 0.1),
     'L0_xattn_v_b': (0.0, 0.1),
     'L0_xattn_k_img_b': (0.0, 2.0),
     'L0_xattn_v_img_b': (0.0, 0.356),
     'L0_xattn_o_b': (0.0, 0.1),
     'L0_xattn_norm_q_w': (1.0, 0.6),
     'L0_xattn_norm_k_w': (1.0, 0.2),
     'L0_xattn_norm_k_img_w': (1.0, 0.6)}
    factors = {'L0_xattn_q_w': 4.535,
     'L0_xattn_k_img_w': 4.379,
     'L0_ffn_gate_weight': 8.0,
     'L0_ffn_gate_up_weights': 8.0,
     'L0_ffn_down_weights': 8.0,
     'L0_ffn_shared_gate_up': 4.04,
     'L0_ffn_shared_down': 4.003}
    for name, (base, spread) in spreads.items():
        noise = np.random.default_rng([zlib.crc32(name.encode()), seed]).standard_normal(out[name].shape)
        drawn = base * np.exp(spread * noise) if base else spread * noise
        out[name] = jnp.asarray(drawn.astype(out[name].dtype))
    for name, factor in factors.items():
        out[name] = (out[name] * factor).astype(out[name].dtype)
    return out
```

```python
from contextlib import ExitStack

import concourse.bass as bass
from concourse import mybir

ALU = mybir.AluOpType
ACT = mybir.ActivationFunctionType
AX = mybir.AxisListType
F32 = mybir.dt.float32
F32R = mybir.dt.float32r
BF16 = mybir.dt.bfloat16
U32 = mybir.dt.uint32

P = 128
B, S, D = 4, 256, 256
TT = S // P
KC = D // P
NH, HD, NKV = 16, 16, 4
GQ = NH // NKV
QKV = D + 2 * NKV * HD
E, F, FS = 8, 176, 352
FT = E * F + FS
NCH = -(-FT // P)
FLAST = FT - (NCH - 1) * P
NEC = E * F // P
GW = FT + E
LN_EPS, RMS_EPS = 1e-5, 1e-6
MASKED = -3.0e38
NP6, SW = 6, 96
PSLOTS = 6
VW = 32
Q_BIAS, K_BIAS, V_BIAS, O_BIAS, Q_NORM, K_NORM, A_NORM = range(7)


class Signal:

    def __init__(self, sem, per):
        self.sem, self.per = sem, per

    def __call__(self, it, k):
        return self.sem, it * self.per + k


class Ring:

    def __init__(self, banks, ready, uses, wrap=True):
        self.banks, self.ready_sem, self.total = banks, ready, len(uses)
        self.place, last = {}, [None] * len(banks)
        for i, (key, reader) in enumerate(uses):
            b = i % len(banks)
            self.place[key] = [i, b, last[b]]
            last[b] = reader
        for key, reader in uses[:len(banks)]:
            if self.place[key][2] is None and wrap:
                self.place[key][2] = last[self.place[key][1]] + (-1,)

    def bank(self, key):
        return self.banks[self.place[key][1]]

    def ready(self, it, key):
        return self.ready_sem, it * self.total + self.place[key][0] + 1

    def wait_free(self, pe, it, key):
        if self.place[key][2] is None:
            return
        signal, k, *before = self.place[key][2]
        if before:
            if isinstance(it, int) and it == 0:
                return
            k -= signal.per
        pe.wait_ge(*signal(it, k))


LAG = 2
FFN = [("ffn", n) for n in range(NCH + LAG)]
BODY = ["ctx", "ln0", FFN[0], "ln0_T", FFN[1], "qkv", "self_split", FFN[2], "ctx_kv", "self_T", FFN[3], "ctx_split", "self_max",
        FFN[4], "self_nm", "ctx_T", "self_attn", FFN[5], "self_o", FFN[6], "self_y", FFN[7], "self_proj", "ln1", FFN[8], "ln1_T",
        FFN[9], "xq", "x_split", FFN[10], FFN[11], "x_T", "x_max", FFN[12], "x_nm", FFN[13], "x_attn", "x_o", FFN[14], FFN[15], "x_y",
        "x_proj", "ln2", "ln2_T"]
ATTN = [st for st in BODY if isinstance(st, str)]
CHUNKS = [NCH - 1] + list(range(NEC, NCH - 1)) + list(range(NEC))


def build(nc, a):
    x_v = a["x"].rearrange("b (t p) d -> b p t d", p=P)
    out_v = a["out"].rearrange("b (t p) d -> b p t d", p=P)

    def by_row_chunk(name):
        return a[name].rearrange("(c p) n -> p c n", p=P)

    with ExitStack() as ctx:
        def sb(name, shape, dt=F32):
            return ctx.enter_context(nc.sbuf_tensor(name, shape, dt))

        def sem(name):
            return ctx.enter_context(nc.semaphore(name))

        def sig(name, per):
            return Signal(sem(name), per)

        wqkv = [sb("wqkv_" + s, [P, KC, QKV], F32R) for s in "hl"]
        wp = [sb("wp_" + s, [P, KC, D], F32R) for s in "hl"]
        wq = [sb("wq_" + s, [P, KC, D], F32R) for s in "hl"]
        wkv = [sb("wkv_" + s, [P, KC, 2 * D], F32R) for s in "hl"]
        wo = [sb("wo_" + s, [P, KC, D], F32R) for s in "hl"]
        wg = [sb("wg_" + s, [P, KC, GW], F32R) for s in "hl"]
        wu = [sb("wu_" + s, [P, KC, FT], F32R) for s in "hl"]
        wd = [sb("wd_" + s, [P, NCH, D], F32R) for s in "hl"]
        STAGE = 896
        stage = sb("stage", [P, 2, STAGE])
        rows = sb("rows", [P, 7, D])
        rope_c = sb("rope_c", [P, TT, HD])
        rope_s = sb("rope_s", [P, TT, HD])
        ident = sb("ident", [P, P])
        identb = sb("identb", [P, P], BF16)
        mask_q = sb("mask_q", [P, P], BF16)
        mask_k = sb("mask_k", [P, P], BF16)
        sel_exp = sb("sel_exp", [3 * E, NEC, P], BF16)
        iota_e = sb("iota_e", [P, E])
        neghalf = sb("neghalf", [P, TT])
        eps = sb("eps", [P, 2, TT])
        idle = sb("idle", [P, 1])
        x_in, x1, x2 = (sb(n, [P, TT, D]) for n in ("x_in", "x1", "x2"))
        xn = sb("xn", [P, TT, D])
        xT = [sb("xT_" + s, [P, KC, S], F32R) for s in "hl"]
        fT = [sb("fT_" + s, [P, KC, S], F32R) for s in "hl"]
        ctxT = sb("ctxT", [P, KC, S])
        cT = [sb("cT_" + s, [P, KC, S], F32R) for s in "hl"]
        bn, mv = sb("bn", [P, TT, 6]), sb("mv", [P, TT, 2])
        ve, rstd = sb("ve", [P, TT]), sb("rstd", [P, TT])
        rot, rot2 = (sb(n, [P, TT, (NH + NKV) * HD]) for n in ("rot", "rot2"))
        res = sb("res", [P, TT, D])
        kn = sb("kn", [P, TT, D])
        ssq, ms, rrms = sb("ssq", [P, 3, TT]), sb("ms", [P, 3, TT]), sb("rrms", [P, 3, TT])
        stack = sb("stack", [P, TT, NH, SW], BF16)
        stack_k = sb("stack_k", [P, TT, NKV, SW], BF16)
        QT = sb("QT", [P, NH, S], BF16)
        KT_s = sb("KT_s", [P, NKV, S], BF16)
        KT_x = sb("KT_x", [P, NH, S], BF16)
        V_s = sb("V_s", [P, TT, NKV, VW])
        V_x = sb("V_x", [P, TT, NH, VW])
        mx = sb("mx", [P, NH, 3])
        nmx, nmr = sb("nmx", [P, TT, NH]), sb("nmr", [P, TT, NH])
        nmp = sb("nmp", [P, TT, 3, NH], BF16)
        nmT = sb("nmT", [3 * NH, S], BF16)
        prob = sb("prob", [P, PSLOTS, 2 * S])
        oT = stack[:].rearrange("p t h c -> p (t h c)")[:, 0:8 * S].bitcast(F32).rearrange("p (g s) -> p g s", g=4)
        rden = sb("rden", [P, TT, NH])
        act = stage[:, 0, 0:2 * S].rearrange("p (n s) -> p n s", n=2)
        lgT = stage[:, 0, 2 * S:3 * S]
        cpT = stage[0:3 * E, 0, 2 * S:2 * S + P].bitcast(BF16)
        flat = stage[:].rearrange("p a n -> p (a n)")
        cb = flat[:, 3 * S:7 * S].rearrange("p (n s) -> p n s", n=2)
        act_p = [sb("act_" + s, [P, 2, S], F32R) for s in "hl"]
        gt = sb("gt", [P, 6, TT, E])
        gm = sb("gm", [P, 3, TT])
        top, topi, topf = sb("top", [P, TT, 8]), sb("topi", [P, TT, 8], U32), sb("topf", [P, TT, 8])
        cp = sb("cp", [P, TT, 3, E], BF16)

        bank = [ctx.enter_context(nc.psum_tensor(f"bank{i}", [P, 512], F32)) for i in range(8)]
        Y = bank[7]

        w_loaded = [sem("w_loaded0"), sem("w_loaded1")]
        const_loaded, dve_const, pool_const = sem("const_loaded"), sem("dve_const"), sem("pool_const")
        wh_ready, wl_ready = sem("wh_ready"), sem("wl_ready")
        x_loaded, ctx_loaded = sig("x_loaded", 16), sig("ctx_loaded", 16)
        ch_ready, cl_ready = sig("ch_ready", 1), sig("cl_ready", 1)
        ln_stats, ln_mv, ln_ve, ln_rstd = (sig(n, 3) for n in ("ln_stats", "ln_mv", "ln_ve", "ln_rstd"))
        xn_ready, xh_ready, xl_ready = (sig(n, 3) for n in ("xn_ready", "xh_ready", "xl_ready"))
        rope_parts, rot_ready, v_self, v_ctx = sig("rope_parts", TT), sig("rot_ready", TT), sig("v_self", TT), sig("v_ctx", TT)
        SPLITS = [("q", "k", "ck", "xq")[i] for i in range(4)]
        sp_h, sp_r, sp_m, sp_l = (sig(n, 4 * TT) for n in ("sp_h", "sp_r", "sp_m", "sp_l"))
        QT_ready, KTs_ready, KTx_ready = sig("QT_ready", 8), sig("KTs_ready", 1), sig("KTx_ready", 4)
        RMS = [st for st in ATTN if st in ("ctx_kv", "self_proj", "xq")]
        raw_ready, normed = sig("raw_ready", 2), sig("normed", 2)
        ssq_ready, ms_ready, rms_ready = (sig(n, 3) for n in ("ssq_ready", "ms_ready", "rms_ready"))
        head_max, nm_step, nmp_ready, nmT_ready, nm_placed = sig("head_max", 2 * NH), sig("nm_step", 8), sig("nmp_ready", 2), sig("nmT_ready", 2), sig("nm_placed", 96)
        exp_ready, oT_ready = sig("exp_ready", 2 * NH), sig("oT_ready", 8)
        rden_ready, y_ready, yh_ready, yl_ready = sig("rden_ready", 4), sig("y_ready", 4), sig("yh_ready", 2), sig("yl_ready", 2)
        res_ready, x1_ready, x2_ready = sig("res_ready", 2), sig("x1_ready", 1), sig("x2_ready", 1)
        tanh_ready, fa_ready, fb_ready = (sig(n, NCH) for n in ("tanh_ready", "fa_ready", "fb_ready"))
        fc_ready, cb_ready = sig("fc_ready", NEC), sig("cb_ready", (NEC + 1) // 2)
        ah_ready, al_ready, down_done = (sig(n, NCH) for n in ("ah_ready", "al_ready", "down_done"))
        lgT_ready, gate_step, gate_exp = sig("lgT_ready", 1), sig("gate_step", 14), sig("gate_exp", 1)
        cp_ready, cpT_ready, x3_ready, out_done = sig("cp_ready", 1), sig("cpT_ready", 1), sig("x3_ready", 1), sig("out_done", 16)

        g_readers = {"ln0_T": [(xl_ready, 1)], "ln1_T": [(xl_ready, 2)], "ln2_T": [(xl_ready, 3)],
                     "qkv": [(v_self, t + 1) for t in range(TT)], "ctx_kv": [(v_ctx, t + 1) for t in range(TT)],
                     "self_T": [(QT_ready, i + 1) for i in range(4)] + [(KTs_ready, 1)],
                     "ctx_T": [(KTx_ready, i + 1) for i in range(4)], "x_T": [(QT_ready, i + 5) for i in range(4)],
                     "self_nm": [(nmT_ready, 1)], "x_nm": [(nmT_ready, 2)],
                     "self_o": [(y_ready, 1), (y_ready, 2)], "x_o": [(y_ready, 3), (y_ready, 4)],
                     "self_y": [(yl_ready, 1)], "x_y": [(yl_ready, 2)],
                     "self_proj": [(res_ready, 1)], "xq": [(raw_ready, 2)], "x_proj": [(res_ready, 2)]}
        G = Ring([bank[0], bank[1]], sem("g_ready"), [((st, i), r) for st in ATTN for i, r in enumerate(g_readers.get(st, ()))])
        T = Ring([bank[2], bank[3]], sem("t_ready"),
                 [((st, h), r) for st in ATTN if st.endswith(("_max", "_attn")) for h in range(NH)
                  for r in [(head_max if st.endswith("_max") else exp_ready, (NH if st[0] == "x" else 0) + h + 1)]])
        O = Ring([bank[4]], sem("pv_ready"),
                 [((st, g), (oT_ready, 4 * (st[0] == "x") + g + 1)) for st in ATTN if st.endswith("_attn") for g in range(4)])
        f_uses = []
        for n, c in enumerate(CHUNKS):
            f_uses.append((("gu", n), (fb_ready, n + 1)))
            if n == 1:
                f_uses.append((("router", 1), (gate_step, 2)))
            if n == 2:
                f_uses.append((("router", 2), (cpT_ready, 1)))
            if c < NEC and c % 2 == 0:
                f_uses.append((("cb", c // 2), (cb_ready, c // 2 + 1)))
        FR = Ring([bank[5], bank[6]], sem("f_ready"), f_uses, wrap=False)

        pieces = [(by_row_chunk("w_attn"), wqkv[0][:], wqkv[1][:]),
                  (by_row_chunk("k_img_w"), wkv[0][:, :, 0:D], wkv[1][:, :, 0:D]),
                  (by_row_chunk("v_img_w"), wkv[0][:, :, D:], wkv[1][:, :, D:]),
                  (by_row_chunk("w_proj"), wp[0][:], wp[1][:]),
                  (by_row_chunk("q_w"), wq[0][:], wq[1][:]),
                  (by_row_chunk("o_w"), wo[0][:], wo[1][:])]
        NSMALL = len(pieces)
        for name, w, n in (("wg", wg, GW), ("wu", wu, FT)):
            for c in range(KC):
                for s0, s1 in ((0, n // 2), (n // 2, n)):
                    pieces.append((a[name][c * P:(c + 1) * P, s0:s1].unsqueeze(1), w[0][:, c:c + 1, s0:s1], w[1][:, c:c + 1, s0:s1]))
        for c0 in range(0, NCH - 1, 3):
            c1 = min(c0 + 3, NCH - 1)
            pieces.append((a["wd"][c0 * P:c1 * P, :].rearrange("(c p) n -> p c n", p=P), wd[0][:, c0:c1], wd[1][:, c0:c1]))
        pieces.append((a["wd"][(NCH - 1) * P:FT, :].unsqueeze(1), wd[0][0:FLAST, NCH - 1:NCH], wd[1][0:FLAST, NCH - 1:NCH]))
        NPIECE = len(pieces)
        W_AFTER = {"ctx": range(1, 3), "ctx_kv": range(3, NSMALL)}
        late = ["ctx_split", "self_max", "self_o", "self_proj", "ln1", "x_split", "x_T", "x_max", "x_o"]
        per = -(-(NPIECE - NSMALL) // len(late))
        for i, st in enumerate(late):
            W_AFTER[st] = range(min(NSMALL + i * per, NPIECE), min(NSMALL + (i + 1) * per, NPIECE))

        def staged(n):
            rows_, c, w = pieces[n][1].shape
            assert c * w <= STAGE
            return stage[0:rows_, n % 2, 0:c * w].rearrange("p (c n) -> p c n", c=c)

        def heads(ap):
            return ap.rearrange("p (h c) -> p h c", c=HD)

        QPOS, KPOS = (slice(1, 6, 2), slice(0, 3, 2), 4), (slice(2, 5), slice(0, 2), 5)
        CUT = {"q": (lambda t: heads(rot[:, t, 0:NH * HD]), stack, NH, QPOS),
               "k": (lambda t: heads(rot[:, t, NH * HD:]), stack_k, NKV, KPOS),
               "ck": (lambda t: heads(kn[:, t]), stack, NH, KPOS),
               "xq": (lambda t: heads(res[:, t]), stack, NH, QPOS)}

        def blocks(which, t):
            return CUT[which][1][:, t].rearrange("p h (r c) -> p h r c", c=HD)

        def two(ap):
            return ap.rearrange("p (c n) -> p c n", c=2)

        def run(e, it, steps, ffn_steps, attn=True, ffn=True, after=None):
            for st in BODY:
                if isinstance(st, tuple):
                    if ffn and ffn_steps:
                        ffn_steps(it - 1, st[1])
                elif attn:
                    if st in steps:
                        steps[st](it)
                    if after:
                        after(st)

        def program(e, steps, ffn_steps, after=None):
            run(e, 0, steps, ffn_steps, ffn=False, after=after)
            with e.Fori(1, B) as it:
                run(e, it, steps, ffn_steps)
            run(e, B, steps, ffn_steps, attn=False)

        block = ctx.enter_context(nc.Block())

        @block.sync
        def _(sp):
            def load_piece(n):
                if n >= 2:
                    sp.wait_ge(wl_ready, n - 1)
                sp.dma_start(staged(n), pieces[n][0]).then_inc(w_loaded[n % 2], 16)

            sp.dma_start(x_in[:], x_v[0]).then_inc(x_loaded.sem, 16)
            load_piece(0)
            for dst, name in ((ident, "ident"), (rope_c, "rope_c"), (rope_s, "rope_s"), (identb, "identb")):
                sp.dma_start(dst[:], a[name]).then_inc(const_loaded, 16)
            sp.dma_start(ctxT[:], a["ctxT"][0]).then_inc(ctx_loaded.sem, 16)
            load_piece(1)
            sp.dma_start(rows[:].rearrange("p r d -> p (r d)"), a["rows"].rearrange("r d -> (r d)").partition_broadcast(P)).then_inc(const_loaded, 16)
            for dst, name in ((mask_q, "mask_q"), (mask_k, "mask_k"), (sel_exp, "sel_exp"), (iota_e, "iota_e")):
                sp.dma_start(dst[:], a[name]).then_inc(const_loaded, 16)
            for n in range(2, NPIECE):
                load_piece(n)

            def store(it):
                sp.wait_ge(*x3_ready(it, 1))
                sp.dma_start(out_v[it], x2[:]).then_inc(out_done.sem, 16)

            with sp.Fori(1, B) as it:
                sp.wait_ge(*x1_ready(it, 0))
                sp.dma_start(x_in[:], x_v[it]).then_inc(x_loaded.sem, 16)
                sp.wait_ge(*cl_ready(it, 0))
                sp.wait_ge(*ch_ready(it, 0))
                sp.dma_start(ctxT[:], a["ctxT"][it]).then_inc(ctx_loaded.sem, 16)
                store(it - 1)
            store(B - 1)
            sp.wait_ge(*out_done(B, 0))

        NCONST = 9

        @block.scalar
        def _(e):
            A = nc.scalar

            def weight(n):
                e.wait_ge(w_loaded[n % 2], 16 * (n // 2 + 1))
                A.copy(pieces[n][1], staged(n)).then_inc(wh_ready, 1)

            def context_high(it):
                e.wait_ge(*ctx_loaded(it, 16))
                A.copy(cT[0][:], ctxT[:]).then_inc(ch_ready.sem, 1)

            def ln(k):
                def step(it):
                    e.wait_ge(*G.ready(it, (f"ln{k}_T", 0)))
                    dst = fT[0] if k == 2 else xT[0]
                    A.copy(dst[:], two(G.bank((f"ln{k}_T", 0))[:])).then_inc(xh_ready.sem, 1)
                return step

            def cut(which, it, source_ready):
                src, _, nh, (hpos, mpos, _) = CUT[which]
                k = SPLITS.index(which) * TT
                e.wait_ge(*source_ready)
                for t in range(TT):
                    A.copy(blocks(which, t)[:, :, hpos], src(t).unsqueeze(2).to_broadcast([P, nh, 3, HD])).then_inc(sp_h.sem, 1)
                for t in range(TT):
                    e.wait_ge(*sp_r(it, k + t + 1))
                    A.copy(blocks(which, t)[:, :, mpos], src(t).unsqueeze(2).to_broadcast([P, nh, 2, HD])).then_inc(sp_m.sem, 1)

            def self_split(it):
                cut("q", it, rot_ready(it, TT))
                cut("k", it, rot_ready(it, TT))

            def ctx_split(it):
                e.wait_ge(*G.ready(it, ("self_T", 3)))
                cut("ck", it, normed(it, 1))

            def x_split(it):
                cut("xq", it, normed(it, 2))

            def sumsq(st, src, ready):
                r = RMS.index(st)

                def step(it):
                    e.wait_ge(*ready(it))
                    for t in range(TT):
                        ins = A.activation(rot2[:, t, 0:D // 2].bitcast(BF16), src(t), ACT.Square, scale=D ** -0.5, accum_out=ssq[:, r, t:t + 1])
                    ins.then_inc(ssq_ready.sem, 1)
                return step

            def exps(kind, width):
                st = kind + "_attn"

                def step(it):
                    for h in range(NH):
                        n = h + (NH if kind == "x" else 0)
                        e.wait_ge(*T.ready(it, (st, h)))
                        groups = max((n - PSLOTS) // 4 + 1, 0)
                        e.wait_ge(O.ready_sem, it * O.total + groups)
                        A.activation(prob[:, n % PSLOTS, 0:width], T.bank((st, h))[:, 0:width], ACT.Exp, scale=HD ** -0.5)\
                            .then_inc(exp_ready.sem, 1)
                return step

            def place_maxima(k):
                def step(it):
                    e.wait_ge(*nmT_ready(it, k + 1))
                    for r in range(3):
                        e.dma_start(QT[SW + r:SW + r + 1], nmT[r * NH:(r + 1) * NH]).then_inc(nm_placed.sem, 16)
                return step

            def y_high(kind):
                def step(it):
                    key = (kind + "_y", 0)
                    e.wait_ge(*G.ready(it, key))
                    A.copy(xT[0][:], two(G.bank(key)[:])).then_inc(yh_ready.sem, 1)
                return step

            pb = ("self_proj", 0)
            steps = {"ctx": context_high, "ln0_T": ln(0), "ln1_T": ln(1), "ln2_T": ln(2), "self_split": self_split,
                     "ctx_split": ctx_split, "x_split": x_split,
                     "ctx_kv": sumsq("ctx_kv", lambda t: kn[:, t], lambda it: raw_ready(it, 1)),
                     "xq": sumsq("xq", lambda t: res[:, t], lambda it: raw_ready(it, 2)),
                     "self_proj": sumsq("self_proj", lambda t: G.bank(pb)[:, t * D:(t + 1) * D], lambda it: G.ready(it, pb)),
                     "self_nm": place_maxima(0), "x_nm": place_maxima(1), "self_attn": exps("self", S + P), "x_attn": exps("x", 2 * S), "self_y": y_high("self"), "x_y": y_high("x")}

            def ffn(it, n):
                if n < NCH:
                    r = P if CHUNKS[n] < NCH - 1 else FLAST
                    e.wait_ge(*FR.ready(it, ("gu", n)))
                    if n >= 2:
                        e.wait_ge(*al_ready(it, n - 1))
                    A.activation(act[0:r, n % 2], FR.bank(("gu", n))[0:r, 0:S], ACT.Tanh, scale=0.5).then_inc(tanh_ready.sem, 1)
                if n == 1:
                    e.wait_ge(*gate_step(it, 2))
                    A.activation(gt[:, 1], gt[:, 0], ACT.Exp).then_inc(gate_exp.sem, 1)
                if n < NCH and CHUNKS[n] < NEC and CHUNKS[n] % 2 == 0:
                    j = CHUNKS[n] // 2
                    e.wait_ge(*FR.ready(it, ("cb", j)))
                    if j >= 2:
                        e.wait_ge(*fc_ready(it, 2 * (j - 1)))
                    w = 2 * S if CHUNKS[n] + 1 < NEC else S
                    A.copy(cb[:, j % 2, 0:w], FR.bank(("cb", j))[:, 0:w]).then_inc(cb_ready.sem, 1)
                if 1 <= n <= NCH:
                    m = n - 1
                    c = CHUNKS[m]
                    r = P if c < NCH - 1 else FLAST
                    e.wait_ge(*(fc_ready(it, c + 1) if c < NEC else fb_ready(it, m + 1)))
                    if m >= 2:
                        e.wait_ge(*down_done(it, m - 1))
                    A.copy(act_p[0][0:r, m % 2], act[0:r, m % 2]).then_inc(ah_ready.sem, 1)

            weight(0)
            program(e, steps, ffn, lambda st: [weight(n) for n in W_AFTER.get(st, ())])

        @block.gpsimd
        def _(e):
            L = nc.gpsimd

            def weight(n):
                e.wait_ge(wh_ready, n + 1)
                L.tensor_tensor(pieces[n][2], staged(n), pieces[n][1], ALU.subtract).then_inc(wl_ready, 1)

            def context_low(it):
                e.wait_ge(*ch_ready(it, 1))
                L.tensor_tensor(cT[1][:], ctxT[:], cT[0][:], ALU.subtract).then_inc(cl_ready.sem, 1)

            def ln(k):
                def step(it):
                    e.wait_ge(*ln_mv(it, k + 1))
                    L.tensor_tensor(ve[:], mv[:, :, 1], eps[:, 0], ALU.add).then_inc(ln_ve.sem, 1)
                    e.wait_ge(*ln_ve(it, k + 1))
                    L.tensor_tensor(rstd[:], ve[:], neghalf[:], ALU.pow).then_inc(ln_rstd.sem, 1)
                return step

            def cut(which, it):
                src, _, nh, (hpos, mpos, lpos) = CUT[which]
                k = SPLITS.index(which) * TT
                for t in range(TT):
                    e.wait_ge(*sp_h(it, k + t + 1))
                    L.tensor_tensor(src(t), src(t), blocks(which, t)[:, :, hpos][:, :, 0], ALU.subtract).then_inc(sp_r.sem, 1)
                for t in range(TT):
                    e.wait_ge(*sp_m(it, k + t + 1))
                    L.tensor_tensor(blocks(which, t)[:, :, lpos], src(t), blocks(which, t)[:, :, mpos][:, :, 0], ALU.subtract)\
                        .then_inc(sp_l.sem, 1)

            def rms(st):
                r = RMS.index(st)

                def step(it):
                    e.wait_ge(*ssq_ready(it, r + 1))
                    L.tensor_tensor(ms[:, r], ssq[:, r], eps[:, 1], ALU.add).then_inc(ms_ready.sem, 1)
                    e.wait_ge(*ms_ready(it, r + 1))
                    L.tensor_tensor(rrms[:, r], ms[:, r], neghalf[:], ALU.pow).then_inc(rms_ready.sem, 1)
                return step

            steps = {"ctx": context_low, "ln0": ln(0), "ln1": ln(1), "ln2": ln(2),
                     "self_split": lambda it: (cut("q", it), cut("k", it)), "ctx_split": lambda it: cut("ck", it),
                     "x_split": lambda it: cut("xq", it), "ctx_kv": rms("ctx_kv"), "self_proj": rms("self_proj"), "xq": rms("xq")}

            def ffn(it, n):
                if 1 <= n <= NCH:
                    m = n - 1
                    r = P if CHUNKS[m] < NCH - 1 else FLAST
                    e.wait_ge(*ah_ready(it, m + 1))
                    L.tensor_tensor(act_p[1][0:r, m % 2], act[0:r, m % 2], act_p[0][0:r, m % 2], ALU.subtract).then_inc(al_ready.sem, 1)

            L.memset(eps[:, 0], LN_EPS)
            L.memset(eps[:, 1], RMS_EPS)
            L.memset(neghalf[:], -0.5).then_inc(pool_const, 1)
            e.wait_ge(pool_const, 1)
            weight(0)
            program(e, steps, ffn, lambda st: [weight(n) for n in W_AFTER.get(st, ())])

        @block.vector
        def _(e):
            V = nc.vector

            def carry(signal, count):
                e.wait_ge(signal, count)
                V.memset(idle[:], 0.0)

            def ln(k):
                src = (x_in, x1, x2)[k]

                def step(it):
                    if k == 0:
                        e.wait_ge(*x_loaded(it, 16))
                    else:
                        e.wait_ge(*(x1_ready, x2_ready)[k - 1](it, 1))
                    for t in range(TT):
                        ins = V.bn_stats(bn[:, t], src[:, t])
                    ins.then_inc(ln_stats.sem, 1)
                    carry(*ln_stats(it, k + 1))
                    for t in range(TT):
                        ins = V.bn_aggr(mv[:, t], bn[:, t])
                    ins.then_inc(ln_mv.sem, 1)
                    e.wait_ge(*ln_rstd(it, k + 1))
                    for t in range(TT):
                        ins = V.tensor_scalar(xn[:, t], src[:, t], mv[:, t, 0:1], rstd[:, t:t + 1], ALU.subtract, ALU.mult)
                    ins.then_inc(xn_ready.sem, 1)
                return step

            def ln_low(k):
                def step(it):
                    key = (f"ln{k}_T", 0)
                    e.wait_ge(*xh_ready(it, k + 1))
                    hl = fT if k == 2 else xT
                    V.tensor_tensor(hl[1][:], two(G.bank(key)[:]), hl[0][:], ALU.subtract).then_inc(xl_ready.sem, 1)
                return step

            def qkv(it):
                pair = lambda ap, n: ap.rearrange("p (h c j) -> p h c j", c=HD // 2, j=2)
                n = NH + NKV
                for t in range(TT):
                    key = ("qkv", t)
                    e.wait_ge(*G.ready(it, key))
                    ps = G.bank(key)
                    qk = pair(ps[:, 0:n * HD], n)
                    cs = rope_c[:, t].rearrange("p (c j) -> p c j", j=2)
                    sn = rope_s[:, t].rearrange("p (c j) -> p c j", j=2)
                    V.tensor_tensor(heads(rot[:, t]), heads(ps[:, 0:n * HD]), rope_c[:, t].unsqueeze(1).to_broadcast([P, n, HD]), ALU.mult)
                    for j in range(2):
                        ins = V.tensor_tensor(pair(rot2[:, t], n)[:, :, :, j], qk[:, :, :, 1 - j],
                                              sn[:, :, j].unsqueeze(1).to_broadcast([P, n, HD // 2]), ALU.mult)
                    ins.then_inc(rope_parts.sem, 1)
                    V.tensor_copy(V_s[:, t, :, 0:HD], heads(ps[:, n * HD:QKV])).then_inc(v_self.sem, 1)
                    e.wait_ge(*rope_parts(it, t + 1))
                    V.tensor_tensor(rot[:, t], rot[:, t], rot2[:, t], ALU.add).then_inc(rot_ready.sem, 1)

            def ctx_kv(it):
                for t in range(TT):
                    key = ("ctx_kv", t)
                    e.wait_ge(*G.ready(it, key))
                    ps = G.bank(key)
                    ins = V.tensor_tensor(kn[:, t], ps[:, 0:D], rows[:, K_BIAS], ALU.add)
                    if t == TT - 1:
                        ins.then_inc(raw_ready.sem, 1)
                    V.tensor_tensor(V_x[:, t, :, 0:HD], heads(ps[:, D:]), heads(rows[:, V_BIAS]), ALU.add).then_inc(v_ctx.sem, 1)

            def norm(st, buf, row):
                r = RMS.index(st)

                def step(it):
                    e.wait_ge(*rms_ready(it, r + 1))
                    for t in range(TT):
                        ins = V.scalar_tensor_tensor(buf[:, t], buf[:, t], rrms[:, r, t:t + 1], rows[:, row], ALU.mult, ALU.mult)
                    ins.then_inc(normed.sem, 1)
                return step

            def evacuate(st, count, dst, ready):
                def step(it):
                    for i in range(count):
                        e.wait_ge(*G.ready(it, (st, i)))
                        out, signal = dst(i)
                        V.tensor_copy(out, G.bank((st, i))[0:SW, :].bitcast(BF16).rearrange("p (h s) -> p h s", s=S)).then_inc(signal.sem, 1)
                return step

            def row_max(kind):
                st = kind + "_max"

                def step(it):
                    for h in range(NH):
                        e.wait_ge(*T.ready(it, (st, h)))
                        ps = T.bank((st, h))
                        if kind == "self":
                            ins = V.tensor_reduce(mx[:, h], ps[:, 0:3 * P].rearrange("p (b k) -> p b k", k=P), AX.X, ALU.max)
                        else:
                            ins = V.tensor_reduce(mx[:, h, 0:TT], two(ps[:]), AX.X, ALU.max)
                        ins.then_inc(head_max.sem, 1)
                    k = 0 if kind == "self" else 1
                    e.wait_ge(*head_max(it, (k + 1) * NH))
                    if kind == "self":
                        V.tensor_copy(nmx[:, 0], mx[:, :, 0])
                        V.tensor_tensor(nmx[:, 1], mx[:, :, 1], mx[:, :, 2], ALU.max).then_inc(nm_step.sem, 1)
                    else:
                        V.tensor_copy(nmx[:], mx[:, :, 0:TT].rearrange("p h t -> p t h")).then_inc(nm_step.sem, 1)
                    e.wait_ge(*nm_step(it, 4 * k + 1))
                    V.tensor_scalar(nmp[:, :, 0], nmx[:], -1.0, None, ALU.mult).then_inc(nm_step.sem, 1)
                    e.wait_ge(*nm_step(it, 4 * k + 2))
                    V.scalar_tensor_tensor(nmr[:], nmx[:], -1.0, nmp[:, :, 0], ALU.mult, ALU.subtract).then_inc(nm_step.sem, 1)
                    e.wait_ge(*nm_step(it, 4 * k + 3))
                    V.tensor_copy(nmp[:, :, 1], nmr[:]).then_inc(nm_step.sem, 1)
                    e.wait_ge(*nm_step(it, 4 * k + 4))
                    V.tensor_tensor(nmp[:, :, 2], nmr[:], nmp[:, :, 1], ALU.subtract).then_inc(nmp_ready.sem, 1)
                return step

            def nm_out(kind):
                def step(it):
                    key = (kind + "_nm", 0)
                    e.wait_ge(*G.ready(it, key))
                    V.tensor_copy(nmT[:], G.bank(key)[0:3 * NH, 0:S]).then_inc(nmT_ready.sem, 1)
                return step

            def attn(kind):
                st = kind + "_attn"

                def step(it):
                    for g in range(4):
                        e.wait_ge(*O.ready(it, (st, g)))
                        V.tensor_copy(oT[:, g], O.bank((st, g))[:, 0:S]).then_inc(oT_ready.sem, 1)
                return step

            def out_tokens(kind):
                k = 0 if kind == "self" else 1

                def step(it):
                    for t in range(TT):
                        key = (kind + "_o", t)
                        e.wait_ge(*G.ready(it, key))
                        ps = G.bank(key)[:].rearrange("p (h c) -> p h c", c=VW)
                        V.reciprocal(rden[:, t], ps[:, :, HD]).then_inc(rden_ready.sem, 1)
                        e.wait_ge(*rden_ready(it, k * TT + t + 1))
                        V.tensor_tensor(heads(xn[:, t]), ps[:, :, 0:HD], rden[:, t].unsqueeze(2).to_broadcast([P, NH, HD]), ALU.mult)\
                            .then_inc(y_ready.sem, 1)
                return step

            def y_low(kind):
                k = 0 if kind == "self" else 1

                def step(it):
                    key = (kind + "_y", 0)
                    e.wait_ge(*yh_ready(it, k + 1))
                    V.tensor_tensor(xT[1][:], two(G.bank(key)[:]), xT[0][:], ALU.subtract).then_inc(yl_ready.sem, 1)
                return step

            def self_proj(it):
                key = ("self_proj", 0)
                r = RMS.index("self_proj")
                e.wait_ge(*rms_ready(it, r + 1))
                for t in range(TT):
                    ins = V.scalar_tensor_tensor(res[:, t], G.bank(key)[:, t * D:(t + 1) * D], rrms[:, r, t:t + 1], rows[:, A_NORM],
                                                 ALU.mult, ALU.mult)
                ins.then_inc(res_ready.sem, 1)
                e.wait_ge(*res_ready(it, 1))
                V.tensor_tensor(x1[:], res[:], x_in[:], ALU.add).then_inc(x1_ready.sem, 1)

            def xq(it):
                key = ("xq", 0)
                e.wait_ge(*G.ready(it, key))
                V.tensor_tensor(res[:], two(G.bank(key)[:]), rows[:, Q_BIAS].unsqueeze(1).to_broadcast([P, TT, D]), ALU.add)\
                    .then_inc(raw_ready.sem, 1)

            def x_proj(it):
                key = ("x_proj", 0)
                e.wait_ge(*G.ready(it, key))
                V.tensor_tensor(res[:], two(G.bank(key)[:]), rows[:, O_BIAS].unsqueeze(1).to_broadcast([P, TT, D]), ALU.add)\
                    .then_inc(res_ready.sem, 1)
                e.wait_ge(*res_ready(it, 2))
                e.wait_ge(*out_done(it, 0)) if not isinstance(it, int) else None
                V.tensor_tensor(x2[:], res[:], x1[:], ALU.add).then_inc(x2_ready.sem, 1)

            steps = {"ln0": ln(0), "ln1": ln(1), "ln2": ln(2), "ln0_T": ln_low(0), "ln1_T": ln_low(1), "ln2_T": ln_low(2),
                     "self_nm": nm_out("self"), "x_nm": nm_out("x"), "self_y": y_low("self"), "x_y": y_low("x"),
                     "qkv": qkv, "ctx_kv": ctx_kv, "ctx_split": norm("ctx_kv", kn, K_NORM), "x_split": norm("xq", res, Q_NORM),
                     "self_T": evacuate("self_T", 5, lambda i: (QT[0:SW, 4 * i:4 * i + 4], QT_ready) if i < 4 else (KT_s[0:SW], KTs_ready), None),
                     "ctx_T": evacuate("ctx_T", 4, lambda i: (KT_x[0:SW, 4 * i:4 * i + 4], KTx_ready), None),
                     "x_T": evacuate("x_T", 4, lambda i: (QT[0:SW, 4 * i:4 * i + 4], QT_ready), None),
                     "self_max": row_max("self"), "x_max": row_max("x"), "self_attn": attn("self"), "x_attn": attn("x"),
                     "self_o": out_tokens("self"), "x_o": out_tokens("x"), "self_proj": self_proj, "xq": xq, "x_proj": x_proj}

            def router(it):
                lg = FR.bank(("router", 1))[:, 0:TT * E].rearrange("p (t e) -> p t e", e=E)
                wide = lambda ap: ap.unsqueeze(2).to_broadcast([P, TT, E])
                k = [0]

                def after(ins):
                    ins.then_inc(gate_step.sem, 1)
                    k[0] += 1
                    carry(*gate_step(it, k[0]))

                e.wait_ge(*FR.ready(it, ("router", 1)))
                after(V.tensor_reduce(gm[:, 0], lg, AX.X, ALU.max))
                after(V.tensor_tensor(gt[:, 0], lg, wide(gm[:, 0]), ALU.subtract))
                e.wait_ge(*gate_exp(it, 1))
                after(V.tensor_reduce(gm[:, 1], gt[:, 1], AX.X, ALU.add))
                after(V.reciprocal(gm[:, 2], gm[:, 1]))
                after(V.tensor_tensor(gt[:, 2], gt[:, 1], wide(gm[:, 2]), ALU.mult))
                for t in range(TT):
                    ins = V.max(top[:, t], gt[:, 2, t])
                after(ins)
                for t in range(TT):
                    ins = V.max_index(topi[:, t], top[:, t], gt[:, 2, t])
                after(ins)
                after(V.tensor_copy(topf[:], topi[:]))
                for j in range(2):
                    ins = V.tensor_tensor(gt[:, 3 + j], iota_e[:].unsqueeze(1).to_broadcast([P, TT, E]),
                                          topf[:, :, j:j + 1].to_broadcast([P, TT, E]), ALU.is_equal)
                after(ins)
                after(V.tensor_tensor(gt[:, 3], gt[:, 3], gt[:, 4], ALU.add))
                after(V.tensor_tensor(gt[:, 5], gt[:, 3], gt[:, 2], ALU.mult))
                after(V.tensor_copy(cp[:, :, 0], gt[:, 5]))
                after(V.tensor_tensor(gt[:, 4], gt[:, 5], cp[:, :, 0], ALU.subtract))
                after(V.tensor_copy(cp[:, :, 1], gt[:, 4]))
                V.tensor_tensor(cp[:, :, 2], gt[:, 4], cp[:, :, 1], ALU.subtract).then_inc(cp_ready.sem, 1)

            def ffn(it, n):
                if n < NCH:
                    c = CHUNKS[n]
                    r = P if c < NCH - 1 else FLAST
                    ps = FR.bank(("gu", n))
                    slot = act[0:r, n % 2]
                    if n == 0:
                        e.wait_ge(*FR.ready(it, ("gu", 0)))
                        V.tensor_copy(lgT[FLAST:FLAST + E, :], ps[FLAST:FLAST + E, 0:S]).then_inc(lgT_ready.sem, 1)
                    e.wait_ge(*tanh_ready(it, n + 1))
                    V.scalar_tensor_tensor(slot, slot, 1.0, ps[0:r, 0:S], ALU.add, ALU.mult).then_inc(fa_ready.sem, 1)
                    e.wait_ge(*fa_ready(it, n + 1))
                    V.scalar_tensor_tensor(slot, slot, 0.5, ps[0:r, S:2 * S], ALU.mult, ALU.mult).then_inc(fb_ready.sem, 1)
                    if c < NEC:
                        e.wait_ge(*cb_ready(it, c // 2 + 1))
                        e.wait_ge(*fb_ready(it, n + 1))
                        V.tensor_tensor(slot, slot, cb[:, c // 2 % 2, c % 2 * S:(c % 2 + 1) * S], ALU.mult).then_inc(fc_ready.sem, 1)
                if n == 1:
                    router(it)
                if n == 2:
                    e.wait_ge(*FR.ready(it, ("router", 2)))
                    V.tensor_copy(cpT, FR.bank(("router", 2))[0:3 * E, 0:P].bitcast(BF16)).then_inc(cpT_ready.sem, 1)
                if n == NCH + LAG - 1:
                    e.wait_ge(*down_done(it, NCH))
                    V.tensor_tensor(x2[:], two(Y[:]), x2[:], ALU.add).then_inc(x3_ready.sem, 1)

            V.memset(QT[SW:P], 0.0)
            V.memset(KT_s[SW:P], 1.0)
            V.memset(KT_x[SW:P], 1.0)
            V.memset(V_s[:], 0.0)
            V.memset(V_x[:], 0.0).then_inc(dve_const, 1)
            e.wait_ge(dve_const, 1)
            V.memset(V_s[:, :, :, HD:HD + 1], 1.0)
            V.memset(V_x[:, :, :, HD:HD + 1], 1.0).then_inc(dve_const, 1)
            e.wait_ge(const_loaded, 16 * NCONST)
            program(e, steps, ffn)

        @block.tensor
        def _(e):
            def product(out, lhs, lcols, rhs, rcols, chunks, first=True, rows_=P):
                todo = [(c, i, j) for c in chunks for i, j in ((0, 0), (0, 1), (1, 0))]
                for n, (c, i, j) in enumerate(todo):
                    ins = e.matmul(out, lhs[i][0:rows_, c, lcols], rhs[j][0:rows_, c, rcols], start=first and n == 0, stop=n == len(todo) - 1,
                                   skip_group_check=True)
                return ins

            def tile(t):
                return slice(t * P, (t + 1) * P)

            def weights(it, n):
                if isinstance(it, int) and it == 0:
                    e.wait_ge(wl_ready, n)

            def ln(k):
                def step(it):
                    key = (f"ln{k}_T", 0)
                    e.wait_ge(*xn_ready(it, k + 1))
                    if k == 0 and isinstance(it, int) and it == 0:
                        e.wait_ge(const_loaded, 16 * NCONST)
                    G.wait_free(e, it, key)
                    for c in range(KC):
                        for t in range(TT):
                            ins = e.transpose(two(G.bank(key)[:])[:, c, tile(t)], xn[:, t, c * P:(c + 1) * P], ident[:])
                    ins.then_inc(G.ready_sem, 1)
                return step

            def qkv(it):
                weights(it, 1)
                e.wait_ge(*xh_ready(it, 1))
                e.wait_ge(*xl_ready(it, 1))
                for t in range(TT):
                    key = ("qkv", t)
                    G.wait_free(e, it, key)
                    product(G.bank(key)[:, 0:QKV], xT, tile(t), wqkv, slice(0, QKV), range(KC)).then_inc(G.ready_sem, 1)

            def ctx_kv(it):
                weights(it, 3)
                e.wait_ge(*ch_ready(it, 1))
                e.wait_ge(*cl_ready(it, 1))
                for t in range(TT):
                    key = ("ctx_kv", t)
                    G.wait_free(e, it, key)
                    product(G.bank(key)[:], cT, tile(t), wkv, slice(0, 2 * D), range(KC)).then_inc(G.ready_sem, 1)

            def unstack(st, cuts):
                def step(it):
                    i = 0
                    for which in cuts:
                        _, stk, nh, _ = CUT[which]
                        e.wait_ge(*sp_l(it, (SPLITS.index(which) + 1) * TT))
                        for h0 in range(0, nh, 4):
                            key = (st, i)
                            G.wait_free(e, it, key)
                            ps = G.bank(key)[0:SW, :].bitcast(BF16).rearrange("p (h s) -> p h s", s=S)
                            for h in range(4):
                                for t in range(TT):
                                    ins = e.transpose(ps[:, h, tile(t)], stk[:, t, h0 + h, :], identb[:])
                            ins.then_inc(G.ready_sem, 1)
                            i += 1
                return step

            def self_max(it):
                e.wait_ge(*QT_ready(it, 4))
                e.wait_ge(*KTs_ready(it, 1))
                for h in range(NH):
                    key = ("self_max", h)
                    ps = T.bank(key)
                    T.wait_free(e, it, key)
                    e.matmul(ps[:, 0:3 * P].rearrange("p (b k) -> p b k", k=P)[:, 0:3:2], identb[:], mask_q[:].unsqueeze(1).to_broadcast([P, 2, P]),
                             start=True, stop=False, skip_group_check=True)
                    e.matmul(ps[:, 0:P], QT[0:SW, h, 0:P], KT_s[0:SW, h // GQ, 0:P], start=False, stop=False, skip_group_check=True)
                    e.matmul(ps[:, P:3 * P], QT[0:SW, h, P:S], KT_s[0:SW, h // GQ, :], start=False, stop=True, skip_group_check=True)\
                        .then_inc(T.ready_sem, 1)

            def x_max(it):
                e.wait_ge(*QT_ready(it, 8))
                e.wait_ge(*KTx_ready(it, 4))
                for h in range(NH):
                    key = ("x_max", h)
                    T.wait_free(e, it, key)
                    for t in range(TT):
                        ins = e.matmul(T.bank(key)[:, t * S:(t + 1) * S], QT[0:SW, h, tile(t)], KT_x[0:SW, h, :], start=True, stop=True,
                                       skip_group_check=True)
                    ins.then_inc(T.ready_sem, 1)

            def attn(kind):
                st = kind + "_attn"
                k = 0 if kind == "self" else 1

                def values(it, g):
                    O.wait_free(e, it, (st, g))
                    out = O.bank((st, g))
                    for kt in range(TT):
                        for j in range(4):
                            h = 4 * g + j
                            if kt == 0:
                                e.wait_ge(*exp_ready(it, k * NH + h + 1))
                            v = V_s[:, kt, h // GQ, :] if kind == "self" else V_x[:, kt, h, :]
                            p = prob[:, (k * NH + h) % PSLOTS, :]
                            if kind == "self" and kt == 1:
                                o, p = out[VW * j:VW * (j + 1), P:S], p[:, S:S + P]
                            else:
                                o, p = out[VW * j:VW * (j + 1), 0:S], p[:, kt * S:(kt + 1) * S]
                            ins = e.matmul(o, v, p, start=kt == 0, stop=kt == TT - 1, skip_group_check=True, tile_position=(0, VW * j))
                    ins.then_inc(O.ready_sem, 1)

                def maxima(it):
                    key = (kind + "_nm", 0)
                    e.wait_ge(*nmp_ready(it, k + 1))
                    G.wait_free(e, it, key)
                    ps = G.bank(key)[0:3 * NH, 0:S]
                    for t in range(TT):
                        ins = e.matmul(ps[:, tile(t)], nmp[:, t].rearrange("p r h -> p (r h)"), identb[:], start=True, stop=True,
                                       skip_group_check=True)
                    ins.then_inc(G.ready_sem, 1)

                def step(it):
                    e.wait_ge(*(v_self, v_ctx)[k](it, TT))
                    e.wait_ge(*nm_placed(it, 48 * (k + 1)))
                    for h in range(NH):
                        key = (st, h)
                        ps = T.bank(key)
                        T.wait_free(e, it, key)
                        if kind == "self":
                            kT = KT_s[:, h // GQ]
                            e.matmul(ps[:, 0:3 * P].rearrange("p (b k) -> p b k", k=P)[:, 0:3:2], identb[:], mask_k[:].unsqueeze(1).to_broadcast([P, 2, P]),
                                     start=True, stop=False, skip_group_check=True)
                            e.matmul(ps[:, 0:S], kT[:, 0:P], QT[:, h, :], start=False, stop=False, skip_group_check=True)
                            ins = e.matmul(ps[:, S:S + P], kT[:, P:S], QT[:, h, P:S], start=False, stop=True, skip_group_check=True)
                        else:
                            kT = KT_x[:, h]
                            e.matmul(ps[:, 0:S], kT[:, 0:P], QT[:, h, :], start=True, stop=True, skip_group_check=True)
                            ins = e.matmul(ps[:, S:2 * S], kT[:, P:S], QT[:, h, :], start=True, stop=True, skip_group_check=True)
                        ins.then_inc(T.ready_sem, 1)
                        if h % 4 == 1 and h > 4:
                            values(it, h // 4 - 1)
                    values(it, 3)
                return maxima, step

            def to_tokens(kind):
                k = 0 if kind == "self" else 1

                def step(it):
                    e.wait_ge(*oT_ready(it, 4 * (k + 1)))
                    for t in range(TT):
                        key = (kind + "_o", t)
                        G.wait_free(e, it, key)
                        for g in range(4):
                            ins = e.transpose(G.bank(key)[:, g * P:(g + 1) * P], oT[:, g, tile(t)], ident[:])
                        ins.then_inc(G.ready_sem, 1)
                return step

            def y_transposed(kind):
                k = 0 if kind == "self" else 1

                def step(it):
                    key = (kind + "_y", 0)
                    G.wait_free(e, it, key)
                    e.wait_ge(*y_ready(it, (k + 1) * TT))
                    for c in range(KC):
                        for t in range(TT):
                            ins = e.transpose(two(G.bank(key)[:])[:, c, tile(t)], xn[:, t, c * P:(c + 1) * P], ident[:])
                    ins.then_inc(G.ready_sem, 1)
                return step

            def project(st, lhs, rhs, n, waits):
                def step(it):
                    weights(it, n)
                    for w, k in waits:
                        e.wait_ge(*w(it, k))
                    G.wait_free(e, it, (st, 0))
                    for t in range(TT):
                        ins = product(two(G.bank((st, 0))[:])[:, t], lhs, tile(t), rhs, slice(0, D), range(KC))
                    ins.then_inc(G.ready_sem, 1)
                return step

            (self_nm, self_attn), (x_nm, x_attn) = attn("self"), attn("x")
            steps = {"ln0_T": ln(0), "ln1_T": ln(1), "ln2_T": ln(2), "qkv": qkv, "ctx_kv": ctx_kv, "self_T": unstack("self_T", ("q", "k")), "ctx_T": unstack("ctx_T", ("ck",)), "x_T": unstack("x_T", ("xq",)),
                     "self_max": self_max, "x_max": x_max, "self_nm": self_nm, "x_nm": x_nm,
                     "self_attn": self_attn, "x_attn": x_attn, "self_o": to_tokens("self"), "x_o": to_tokens("x"),
                     "self_y": y_transposed("self"), "x_y": y_transposed("x"),
                     "self_proj": project("self_proj", xT, wp, 4, [(yh_ready, 1), (yl_ready, 1)]),
                     "xq": project("xq", xT, wq, 5, [(xh_ready, 2), (xl_ready, 2)]),
                     "x_proj": project("x_proj", xT, wo, 6, [(yh_ready, 2), (yl_ready, 2)])}

            def ffn(it, n):
                if n == 0:
                    e.wait_ge(wl_ready, NPIECE)
                    e.wait_ge(*xh_ready(it, 3))
                    e.wait_ge(*xl_ready(it, 3))
                if n < NCH:
                    c = CHUNKS[n]
                    key = ("gu", n)
                    last = c == NCH - 1
                    FR.wait_free(e, it, key)
                    gc, uc = slice(c * P, GW if last else (c + 1) * P), slice(c * P, FT if last else (c + 1) * P)
                    ps = FR.bank(key)
                    product(ps[0:FLAST + E if last else P, 0:S], wg, gc, fT, slice(0, S), range(KC))
                    product(ps[0:FLAST if last else P, S:2 * S], wu, uc, fT, slice(0, S), range(KC)).then_inc(FR.ready_sem, 1)
                if n == 1:
                    e.wait_ge(*lgT_ready(it, 1))
                    FR.wait_free(e, it, ("router", 1))
                    for t in range(TT):
                        ins = e.matmul(FR.bank(("router", 1))[:, t * E:(t + 1) * E], lgT[FLAST:FLAST + E, tile(t)],
                                       ident[FLAST:FLAST + E, FLAST:FLAST + E], start=True, stop=True, skip_group_check=True)
                    ins.then_inc(FR.ready_sem, 1)
                if n == 2:
                    e.wait_ge(*cp_ready(it, 1))
                    FR.wait_free(e, it, ("router", 2))
                    for t in range(TT):
                        ins = e.transpose(FR.bank(("router", 2))[0:3 * E, 0:P].bitcast(BF16)[:, tile(t)], cp[:, t].rearrange("p r e -> p (r e)"), identb[:])
                    ins.then_inc(FR.ready_sem, 1)
                if n < NCH and CHUNKS[n] < NEC and CHUNKS[n] % 2 == 0:
                    j = CHUNKS[n] // 2
                    FR.wait_free(e, it, ("cb", j))
                    e.wait_ge(*cpT_ready(it, 1))
                    for i in range(2 * j, min(2 * j + 2, NEC)):
                        ins = e.matmul(FR.bank(("cb", j))[:, i % 2 * S:(i % 2 + 1) * S], sel_exp[:, i, :], cpT, start=True, stop=True,
                                       skip_group_check=True)
                    ins.then_inc(FR.ready_sem, 1)
                if n >= LAG:
                    m = n - LAG
                    c = CHUNKS[m]
                    r = P if c < NCH - 1 else FLAST
                    e.wait_ge(*ah_ready(it, m + 1))
                    e.wait_ge(*al_ready(it, m + 1))
                    for t in range(TT):
                        for i, (ai, wi) in enumerate(((0, 0), (0, 1), (1, 0))):
                            ins = e.matmul(two(Y[:])[:, t], act_p[ai][0:r, m % 2, tile(t)], wd[wi][0:r, c, :],
                                           start=m == 0 and t == 0 and i == 0, stop=m == NCH - 1 and i == 2, skip_group_check=True)
                    ins.then_inc(down_done.sem, 1)

            e.wait_ge(dve_const, 2)
            program(e, steps, ffn)


_OUT = ((B, S, D), "float32")


def _constants(np):
    p = np.arange(P)
    pos = np.arange(S, dtype=np.float32)
    inv = (1.0 / np.float32(10000.0) ** (np.arange(0, HD, 2, dtype=np.float32) / np.float32(HD))).astype(np.float32)
    angle = (pos[:, None] * inv[None, :]).astype(np.float32)
    cos, sin = np.cos(angle), np.sin(angle)
    by_tile = lambda t: np.ascontiguousarray(t.reshape(TT, P, HD).transpose(1, 0, 2).astype(np.float32))
    sel_exp = np.zeros((3, E, NEC * P), np.float32)
    for e in range(E):
        sel_exp[:, e, e * F:(e + 1) * F] = 1.0
    return {"rope_c": by_tile(np.repeat(cos, 2, axis=1)), "rope_s": by_tile(np.stack([-sin, sin], axis=-1).reshape(S, HD)),
            "ident": np.eye(P, dtype=np.float32), "identb": np.eye(P, dtype=np.float32),
            "mask_q": np.where(p[None, :] <= p[:, None], 0.0, MASKED).astype(np.float32),
            "mask_k": np.where(p[:, None] <= p[None, :], 0.0, MASKED).astype(np.float32),
            "sel_exp": sel_exp.reshape(3 * E, NEC, P),
            "iota_e": np.tile(np.arange(E, dtype=np.float32), (P, 1))}


_BF16 = ("identb", "mask_q", "mask_k", "sel_exp")


def kernel(**inputs):
    import ml_dtypes as _ml_dtypes
    import numpy as _np
    import concourse.bacc as _bacc
    from concourse.bass_utils import run_bass_kernel_spmd as _run

    g = {n: _np.asarray(v) for n, v in inputs.items()}
    gu, sgu = g["L0_ffn_gate_up_weights"], g["L0_ffn_shared_gate_up"]
    lay = {
        "x": g["x"],
        "ctxT": g["ctx_2048"].reshape(B, S, KC, P).transpose(0, 3, 2, 1),
        "w_attn": g["L0_attn_w_attn"], "w_proj": g["L0_attn_w_proj"],
        **{n: g["L0_xattn_" + n].T for n in ("q_w", "k_img_w", "v_img_w", "o_w")},
        "wg": _np.concatenate([gu[:, :F].reshape(E * F, D), sgu[:FS], g["L0_ffn_gate_weight"]]).T,
        "wu": _np.concatenate([gu[:, F:].reshape(E * F, D), sgu[FS:]]).T,
        "wd": _np.concatenate([g["L0_ffn_down_weights"].transpose(0, 2, 1).reshape(E * F, D), g["L0_ffn_shared_down"].T]),
        "rows": _np.stack([g["L0_xattn_" + n] for n in ("q_b", "k_img_b", "v_img_b", "o_b", "norm_q_w", "norm_k_img_w")]
                          + [g["L0_attn_norm_w"]]),
        **_constants(_np)}
    nc = _bacc.Bacc("TRN2", target_bir_lowering=False, num_devices=1)
    arrays, aps = {}, {}
    for name, v in lay.items():
        v = _np.array(v, dtype=_ml_dtypes.bfloat16) if name in _BF16 else _np.ascontiguousarray(v)
        arrays["in_" + name] = v
        aps[name] = nc.dram_tensor("in_" + name, v.shape, mybir.dt.from_np(v.dtype), kind="ExternalInput").ap()
    aps["out"] = nc.dram_tensor("out_0", _OUT[0], F32, kind="ExternalOutput").ap()
    build(nc, aps)
    r = _run(nc, [arrays], core_ids=[0])
    return r.results[0]["out_0"]
```

```python
from contextlib import ExitStack

import concourse.bass as bass
from concourse import mybir

ALU = mybir.AluOpType
ACT = mybir.ActivationFunctionType
AX = mybir.AxisListType
F32 = mybir.dt.float32
F32R = mybir.dt.float32r
BF16 = mybir.dt.bfloat16
U32 = mybir.dt.uint32

P = 128
B, S, D = 4, 256, 256
TT = S // P
KC = D // P
NH, HD, NKV = 16, 16, 4
GQ = NH // NKV
QKV = D + 2 * NKV * HD
E, F, FS = 8, 176, 352
FT = E * F + FS
NCH = -(-FT // P)
FLAST = FT - (NCH - 1) * P
NEC = E * F // P
GW = FT + E
LN_EPS, RMS_EPS = 1e-5, 1e-6
MASKED = -3.0e38
NP6, SW = 6, 96
PSLOTS = 6
VW = 32
Q_BIAS, K_BIAS, V_BIAS, O_BIAS, Q_NORM, K_NORM, A_NORM = range(7)


class Signal:

    def __init__(self, sem, per):
        self.sem, self.per = sem, per

    def __call__(self, it, k):
        return self.sem, it * self.per + k


class Ring:

    def __init__(self, banks, ready, uses, wrap=True):
        self.banks, self.ready_sem, self.total = banks, ready, len(uses)
        self.place, last = {}, [None] * len(banks)
        for i, (key, reader) in enumerate(uses):
            b = i % len(banks)
            self.place[key] = [i, b, last[b]]
            last[b] = reader
        for key, reader in uses[:len(banks)]:
            if self.place[key][2] is None and wrap:
                self.place[key][2] = last[self.place[key][1]] + (-1,)

    def bank(self, key):
        return self.banks[self.place[key][1]]

    def ready(self, it, key):
        return self.ready_sem, it * self.total + self.place[key][0] + 1

    def wait_free(self, pe, it, key):
        if self.place[key][2] is None:
            return
        signal, k, *before = self.place[key][2]
        if before:
            if isinstance(it, int) and it == 0:
                return
            k -= signal.per
        pe.wait_ge(*signal(it, k))


LAG = 2
PLAN = {
    "tensor": """
        self_T x_proj- self_max0 ln2_T- self_max1 F self_max2 F self_max3 F self_nm ctx_kv
        self_attn0 self_attn1 self_attn2 self_attn3 F self_o F self_y self_proj F F ln1_T ctx_T xq F ln0_T+ F x_T
        x_max0 qkv+ x_max1 F x_max2 x_max3 F x_nm F F x_attn0 x_attn1 F x_attn2 F x_attn3 F x_o x_y""",
    "vector": """
        self_T x_proj- ln2s- self_max0 self_max1 ln2n- self_max2 self_max3 ln2_T- self_max4 self_max5 self_max6 self_max7
        F self_max8 self_max9 self_max10 self_max11 F self_max12 self_max13 self_max14 self_max15 r self_nm F r ctx_kv
        r r self_attn0 r r r self_attn1 r r r self_attn2 r r r r r self_attn3 F self_o F self_y ctx_split self_proj
        ln1s F F ln1n ln1_T ctx_T ln0s+ xq F ln0n+ x_split ln0_T+ F x_T
        x_max0 x_max1 x_max2 x_max3 qkv+ x_max4 x_max5 x_max6 x_max7 F x_max8 x_max9 x_max10 x_max11
        x_max12 x_max13 x_max14 x_max15 F x_nm F F x_attn0 x_attn1 F x_attn2 F x_attn3 F x_o self_split+ x_y stored-""",
    "scalar": """
        ctx_load+ ln2s- ln2_T- F F self_nm F ctx_kv ctx+ self_attn0 self_attn1 self_attn2 self_attn3 F self_y F self_proj
        ln1s F ctx_split F ln1_T x_load+ ln0s+ xq F x_split ln0_T+ F F F x_nm F F x_attn0 x_attn1 F x_attn2 F x_attn3 F
        self_split+ x_y"""}
PLAN = {engine: plan.split() for engine, plan in PLAN.items()}
PLAN["gpsimd"] = PLAN["scalar"]
NR = 15
assert all(plan.count("F") == NCH + LAG for plan in PLAN.values()) and PLAN["vector"].count("r") == NR
HEAD = ["ln0s", "ln0n", "ctx", "ln0_T", "qkv", "self_split"]
ATTN = [st for st in PLAN["tensor"] if st[-1] not in "F+-"]
CHUNKS = [NCH - 1] + list(range(NEC, NCH - 1)) + list(range(NEC))


def build(nc, a):
    x_v = a["x"].rearrange("b (t p) d -> b p t d", p=P)
    out_v = a["out"].rearrange("b (t p) d -> b p t d", p=P)

    def by_row_chunk(name):
        return a[name].rearrange("(c p) n -> p c n", p=P)

    with ExitStack() as ctx:
        def sb(name, shape, dt=F32):
            return ctx.enter_context(nc.sbuf_tensor(name, shape, dt))

        def sem(name):
            return ctx.enter_context(nc.semaphore(name))

        def sig(name, per):
            return Signal(sem(name), per)

        wqkv = [sb("wqkv_" + s, [P, KC, QKV], F32R) for s in "hl"]
        wp = [sb("wp_" + s, [P, KC, D], F32R) for s in "hl"]
        wq = [sb("wq_" + s, [P, KC, D], F32R) for s in "hl"]
        wkv = [sb("wkv_" + s, [P, KC, 2 * D], F32R) for s in "hl"]
        wo = [sb("wo_" + s, [P, KC, D], F32R) for s in "hl"]
        wg = [sb("wg_" + s, [P, KC, GW], F32R) for s in "hl"]
        wu = [sb("wu_" + s, [P, KC, FT], F32R) for s in "hl"]
        wd = [sb("wd_" + s, [P, NCH, D], F32R) for s in "hl"]
        STAGE = 896
        stage = sb("stage", [P, 2, STAGE])
        rows = sb("rows", [P, 7, D])
        rope_c = sb("rope_c", [P, TT, HD])
        rope_s = sb("rope_s", [P, TT, HD])
        ident = sb("ident", [P, P])
        identb = sb("identb", [P, P], BF16)
        mask_q = sb("mask_q", [P, P], BF16)
        mask_k = sb("mask_k", [P, P], BF16)
        sel_exp = sb("sel_exp", [3 * E, NEC, P], BF16)
        iota_e = sb("iota_e", [P, E])
        neghalf = sb("neghalf", [P, TT])
        eps = sb("eps", [P, 2, TT])
        idle = sb("idle", [P, 1])
        x_in, x1, x2 = (sb(n, [P, TT, D]) for n in ("x_in", "x1", "x2"))
        xn = sb("xn", [P, TT, D])
        xT = [sb("xT_" + s, [P, KC, S], F32R) for s in "hl"]
        fT = [sb("fT_" + s, [P, KC, S], F32R) for s in "hl"]
        ctxT = sb("ctxT", [P, KC, S])
        cT = [sb("cT_" + s, [P, KC, S], F32R) for s in "hl"]
        bn, mv = sb("bn", [P, TT, 6]), sb("mv", [P, TT, 2])
        ve, rstd = sb("ve", [P, TT]), sb("rstd", [P, TT])
        rot, rot2 = (sb(n, [P, TT, (NH + NKV) * HD]) for n in ("rot", "rot2"))
        res = sb("res", [P, TT, D])
        kn = sb("kn", [P, TT, D])
        ssq, ms, rrms = sb("ssq", [P, 3, TT]), sb("ms", [P, 3, TT]), sb("rrms", [P, 3, TT])
        stack = sb("stack", [P, TT, NH, SW], BF16)
        stack_k = sb("stack_k", [P, TT, NKV, SW], BF16)
        QT = sb("QT", [P, NH, S], BF16)
        KT_s = sb("KT_s", [P, NKV, S], BF16)
        KT_x = sb("KT_x", [P, NH, S], BF16)
        V_s = sb("V_s", [P, TT, NKV, VW])
        V_x = sb("V_x", [P, TT, NH, VW])
        mx = sb("mx", [P, NH, 3])
        nmx, nmr = sb("nmx", [P, TT, NH]), sb("nmr", [P, TT, NH])
        nmp = sb("nmp", [P, TT, 3, NH], BF16)
        nmT = sb("nmT", [3 * NH, S], BF16)
        prob = sb("prob", [P, PSLOTS, 2 * S])
        oT = stack[:].rearrange("p t h c -> p (t h c)")[:, 0:8 * S].bitcast(F32).rearrange("p (g s) -> p g s", g=4)
        rden = sb("rden", [P, TT, NH])
        act = stage[:, 0, 0:2 * S].rearrange("p (n s) -> p n s", n=2)
        lgT = stage[:, 0, 2 * S:3 * S]
        cpT = stage[0:3 * E, 0, 2 * S:2 * S + P].bitcast(BF16)
        flat = stage[:].rearrange("p a n -> p (a n)")
        cb = flat[:, 3 * S:7 * S].rearrange("p (n s) -> p n s", n=2)
        act_p = [sb("act_" + s, [P, 2, S], F32R) for s in "hl"]
        gt = sb("gt", [P, 6, TT, E])
        gm = sb("gm", [P, 3, TT])
        top, topi, topf = sb("top", [P, TT, 8]), sb("topi", [P, TT, 8], U32), sb("topf", [P, TT, 8])
        cp = sb("cp", [P, TT, 3, E], BF16)

        bank = [ctx.enter_context(nc.psum_tensor(f"bank{i}", [P, 512], F32)) for i in range(8)]
        Y = bank[7]

        w_loaded = [sem("w_loaded0"), sem("w_loaded1")]
        const_loaded, dve_const, pool_const = sem("const_loaded"), sem("dve_const"), sem("pool_const")
        wh_ready, wl_ready = sem("wh_ready"), sem("wl_ready")
        x_loaded, ctx_loaded = sig("x_loaded", 16), sig("ctx_loaded", 16)
        ch_ready, cl_ready = sig("ch_ready", 1), sig("cl_ready", 1)
        ln_stats, ln_mv, ln_ve, ln_rstd, xn_ready, xh_ready, xl_ready = (
            [sig(f"ln{k}_{n}", 1) for k in range(3)] for n in ("stats", "mv", "ve", "rstd", "xn_ready", "high_ready", "low_ready"))
        rope_parts, rot_ready, v_self, v_ctx = sig("rope_parts", TT), sig("rot_ready", TT), sig("v_self", TT), sig("v_ctx", TT)
        high_ready, rest_ready, middle_ready, low_ready = ({w: sig(f"{w}_{n}_ready", TT) for w in ("q", "k", "ck", "xq")}
                                                           for n in ("high", "rest", "middle", "low"))
        QT_ready, KTs_ready, KTx_ready = sig("QT_ready", 8), sig("KTs_ready", 1), sig("KTx_ready", 4)
        RMS = ["ctx_kv", "self_proj", "xq"]
        raw_ready, normed = sig("raw_ready", 2), sig("normed", 2)
        ssq_ready, ms_ready, rms_ready = (sig(n, 3) for n in ("ssq_ready", "ms_ready", "rms_ready"))
        head_max, nm_step, nmp_ready, nmT_ready, nm_placed = sig("head_max", 2 * NH), sig("nm_step", 8), sig("nmp_ready", 2), sig("nmT_ready", 2), sig("nm_placed", 96)
        exp_ready, oT_ready = sig("exp_ready", 2 * NH), sig("oT_ready", 8)
        rden_ready, y_ready, yh_ready, yl_ready = sig("rden_ready", 4), sig("y_ready", 4), sig("yh_ready", 2), sig("yl_ready", 2)
        res_ready, x1_ready, x2_ready = sig("res_ready", 2), sig("x1_ready", 1), sig("x2_ready", 1)
        tanh_ready, fa_ready, fb_ready = (sig(n, NCH) for n in ("tanh_ready", "fa_ready", "fb_ready"))
        fc_ready, cb_ready = sig("fc_ready", NEC), sig("cb_ready", (NEC + 1) // 2)
        ah_ready, al_ready, down_done = (sig(n, NCH) for n in ("ah_ready", "al_ready", "down_done"))
        lgT_ready, gate_step, gate_exp = sig("lgT_ready", 1), sig("gate_step", 14), sig("gate_exp", 1)
        cp_ready, cpT_ready, x3_ready, out_done = sig("cp_ready", 1), sig("cpT_ready", 1), sig("x3_ready", 1), sig("out_done", 16)

        g_readers = {"ln1_T": [(xl_ready[1], 1)], "ctx_kv": [(v_ctx, t + 1) for t in range(TT)],
                     "self_T": [(KTs_ready, 1)] + [(QT_ready, i + 1) for i in range(4)],
                     "ctx_T": [(KTx_ready, i + 1) for i in range(4)], "x_T": [(QT_ready, i + 5) for i in range(4)],
                     "self_nm": [(nmT_ready, 1)], "x_nm": [(nmT_ready, 2)],
                     "self_o": [(y_ready, 1), (y_ready, 2)], "x_o": [(y_ready, 3), (y_ready, 4)],
                     "self_y": [(yl_ready, 1)], "x_y": [(yl_ready, 2)],
                     "self_proj": [(res_ready, 1)], "xq": [(raw_ready, 2)]}
        for kind, signal in (("_max", head_max), ("_attn", exp_ready)):
            for k, name in enumerate(("self", "x")):
                for g in range(4):
                    g_readers[f"{name}{kind}{g}"] = [(signal, k * NH + 4 * g + j + 1) for j in range(4)]
        G = T = Ring(bank[0:4], sem("g_ready"), [((st, i), r) for st in ATTN for i, r in enumerate(g_readers.get(st, ()))])
        O = Ring([bank[4]], sem("pv_ready"),
                 [((st, g), (oT_ready, 4 * k + g + 1)) for k, st in enumerate(("self_attn", "x_attn")) for g in range(4)])
        H = Ring([bank[4]], sem("head_ready"), [(("ln0_T", 0), (xl_ready[0], 1)), (("qkv", 0), (v_self, 1)), (("qkv", 1), (v_self, 2))],
                 wrap=False)
        R = Ring([bank[4]], sem("tail_ready"), [(("x_proj", 0), (res_ready, 2)), (("ln2_T", 0), (xl_ready[2], 1))], wrap=False)
        f_uses = []
        for n, c in enumerate(CHUNKS):
            f_uses.append((("gu", n), (fb_ready, n + 1)))
            if n == 1:
                f_uses.append((("router", 1), (gate_step, 2)))
            if n == 3:
                f_uses.append((("router", 2), (cpT_ready, 1)))
            if c < NEC and c % 2 == 0:
                f_uses.append((("cb", c // 2), (cb_ready, c // 2 + 1)))
        FR = Ring([bank[5], bank[6]], sem("f_ready"), f_uses, wrap=False)

        pieces = [(by_row_chunk("w_attn"), wqkv[0][:], wqkv[1][:]),
                  (by_row_chunk("k_img_w"), wkv[0][:, :, 0:D], wkv[1][:, :, 0:D]),
                  (by_row_chunk("v_img_w"), wkv[0][:, :, D:], wkv[1][:, :, D:]),
                  (by_row_chunk("w_proj"), wp[0][:], wp[1][:]),
                  (by_row_chunk("q_w"), wq[0][:], wq[1][:]),
                  (by_row_chunk("o_w"), wo[0][:], wo[1][:])]
        NSMALL = len(pieces)
        for name, w, n in (("wg", wg, GW), ("wu", wu, FT)):
            for c in range(KC):
                for s0, s1 in ((0, n // 2), (n // 2, n)):
                    pieces.append((a[name][c * P:(c + 1) * P, s0:s1].unsqueeze(1), w[0][:, c:c + 1, s0:s1], w[1][:, c:c + 1, s0:s1]))
        for c0 in range(0, NCH - 1, 3):
            c1 = min(c0 + 3, NCH - 1)
            pieces.append((a["wd"][c0 * P:c1 * P, :].rearrange("(c p) n -> p c n", p=P), wd[0][:, c0:c1], wd[1][:, c0:c1]))
        pieces.append((a["wd"][(NCH - 1) * P:FT, :].unsqueeze(1), wd[0][0:FLAST, NCH - 1:NCH], wd[1][0:FLAST, NCH - 1:NCH]))
        NPIECE = len(pieces)
        W_AFTER = {"ln0_T": range(1, 3), "self_split": range(3, NSMALL)}
        late = ["ctx_kv", "self_attn3", "self_y", "self_proj", "ctx_split", "x_split", "x_nm", "x_attn3", "x_y"]
        per = -(-(NPIECE - NSMALL) // len(late))
        for i, st in enumerate(late):
            W_AFTER[st] = range(min(NSMALL + i * per, NPIECE), min(NSMALL + (i + 1) * per, NPIECE))

        def staged(n):
            rows_, c, w = pieces[n][1].shape
            assert c * w <= STAGE
            return stage[0:rows_, n % 2, 0:c * w].rearrange("p (c n) -> p c n", c=c)

        def heads(ap):
            return ap.rearrange("p (h c) -> p h c", c=HD)

        QPOS, KPOS = (slice(1, 6, 2), slice(0, 3, 2), 4), (slice(2, 5), slice(0, 2), 5)
        CUT = {"q": (lambda t: heads(rot[:, t, 0:NH * HD]), stack, NH, QPOS),
               "k": (lambda t: heads(rot[:, t, NH * HD:]), stack_k, NKV, KPOS),
               "ck": (lambda t: heads(kn[:, t]), stack, NH, KPOS),
               "xq": (lambda t: heads(res[:, t]), stack, NH, QPOS)}

        def blocks(which, t):
            return CUT[which][1][:, t].rearrange("p h (r c) -> p h r c", c=HD)

        def cut_rest(e, engine, which, it):
            src, _, nh, (hpos, mpos, lpos) = CUT[which]
            for t in range(TT):
                e.wait_ge(*high_ready[which](it, t + 1))
                engine.tensor_tensor(src(t), src(t), blocks(which, t)[:, :, hpos][:, :, 0], ALU.subtract).then_inc(rest_ready[which].sem, 1)
            for t in range(TT):
                e.wait_ge(*middle_ready[which](it, t + 1))
                engine.tensor_tensor(blocks(which, t)[:, :, lpos], src(t), blocks(which, t)[:, :, mpos][:, :, 0], ALU.subtract)\
                    .then_inc(low_ready[which].sem, 1)

        def two(ap):
            return ap.rearrange("p (c n) -> p c n", c=2)

        def first(it):
            return isinstance(it, int) and it == 0

        def run(plan, it, steps, ffn_steps, attn=True, ffn=True, head=True, after=None):
            for i, st in enumerate(plan):
                name = st.rstrip("0123456789+-")
                if name == "F":
                    if ffn and ffn_steps:
                        ffn_steps(it - 1, plan[:i].count("F"))
                elif name == "r":
                    if ffn:
                        steps["router"](it - 1, plan[:i].count("r"))
                elif st[-1] == "-":
                    if ffn and name in steps:
                        steps[name](it - 1)
                elif st[-1] == "+":
                    if attn and head and name in steps:
                        steps[name](it + 1)
                elif attn:
                    if st in steps:
                        steps[st](it)
                    elif name in steps:
                        steps[name](it, int(st[len(name):]))
                    if after:
                        after(st)

        def program(e, plan, steps, ffn_steps, after=None):
            for st in HEAD:
                if st in steps:
                    steps[st](0)
                if after:
                    after(st)
            run(plan, 0, steps, ffn_steps, ffn=False, after=after)
            with e.Fori(1, B - 1) as it:
                run(plan, it, steps, ffn_steps)
            run(plan, B - 1, steps, ffn_steps, head=False)
            run(plan, B, steps, ffn_steps, attn=False)

        block = ctx.enter_context(nc.Block())

        @block.sync
        def _(sp):
            def load_piece(n):
                if n >= 2:
                    sp.wait_ge(wl_ready, n - 1)
                sp.dma_start(staged(n), pieces[n][0]).then_inc(w_loaded[n % 2], 16)

            sp.dma_start(x_in[:], x_v[0]).then_inc(x_loaded.sem, 16)
            load_piece(0)
            for dst, name in ((ident, "ident"), (rope_c, "rope_c"), (rope_s, "rope_s"), (identb, "identb")):
                sp.dma_start(dst[:], a[name]).then_inc(const_loaded, 16)
            sp.dma_start(ctxT[:], a["ctxT"][0]).then_inc(ctx_loaded.sem, 16)
            load_piece(1)
            sp.dma_start(rows[:].rearrange("p r d -> p (r d)"), a["rows"].rearrange("r d -> (r d)").partition_broadcast(P)).then_inc(const_loaded, 16)
            for dst, name in ((mask_q, "mask_q"), (mask_k, "mask_k"), (sel_exp, "sel_exp"), (iota_e, "iota_e")):
                sp.dma_start(dst[:], a[name]).then_inc(const_loaded, 16)
            for n in range(2, NPIECE):
                load_piece(n)

            def store(it):
                sp.wait_ge(*x3_ready(it, 1))
                sp.dma_start(out_v[it], x2[:]).then_inc(out_done.sem, 16)

            with sp.Fori(0, B) as it:
                store(it)
            sp.wait_ge(*out_done(B, 0))

        NCONST = 9

        @block.scalar
        def _(e):
            A = nc.scalar

            def weight(n):
                e.wait_ge(w_loaded[n % 2], 16 * (n // 2 + 1))
                A.copy(pieces[n][1], staged(n)).then_inc(wh_ready, 1)

            def context_high(it):
                e.wait_ge(*ctx_loaded(it, 16))
                A.copy(cT[0][:], ctxT[:]).then_inc(ch_ready.sem, 1)

            def x_load(it):
                e.wait_ge(*x1_ready(it - 1, 1))
                e.dma_start(x_in[:], x_v[it]).then_inc(x_loaded.sem, 16)

            def ctx_load(it):
                e.wait_ge(*cl_ready(it - 1, 1))
                e.wait_ge(*ch_ready(it - 1, 1))
                e.dma_start(ctxT[:], a["ctxT"][it]).then_inc(ctx_loaded.sem, 16)

            def ln(k):
                ring = (H, G, R)[k]

                def step(it):
                    e.wait_ge(*ring.ready(it, (f"ln{k}_T", 0)))
                    dst = fT[0] if k == 2 else xT[0]
                    A.copy(dst[:], two(ring.bank((f"ln{k}_T", 0))[:])).then_inc(xh_ready[k].sem, 1)
                return step

            def cut(which, it, source_ready):
                src, _, nh, (hpos, mpos, _) = CUT[which]
                e.wait_ge(*source_ready)
                for t in range(TT):
                    A.copy(blocks(which, t)[:, :, hpos], src(t).unsqueeze(2).to_broadcast([P, nh, 3, HD])).then_inc(high_ready[which].sem, 1)
                for t in range(TT):
                    e.wait_ge(*rest_ready[which](it, t + 1))
                    A.copy(blocks(which, t)[:, :, mpos], src(t).unsqueeze(2).to_broadcast([P, nh, 2, HD])).then_inc(middle_ready[which].sem, 1)

            def self_split(it):
                if not first(it):
                    e.wait_ge(*G.ready(it - 1, ("x_o", 1)))
                cut("q", it, rot_ready(it, TT))
                cut("k", it, rot_ready(it, TT))

            def ctx_split(it):
                e.wait_ge(*G.ready(it, ("self_o", 1)))
                cut("ck", it, normed(it, 1))

            def x_split(it):
                cut("xq", it, normed(it, 2))

            def sumsq(st, src, ready):
                r = RMS.index(st)

                def step(it):
                    e.wait_ge(*ready(it))
                    for t in range(TT):
                        ins = A.activation(rot2[:, t, 0:D // 2].bitcast(BF16), src(t), ACT.Square, scale=D ** -0.5, accum_out=ssq[:, r, t:t + 1])
                    ins.then_inc(ssq_ready.sem, 1)
                return step

            def exps(kind, width):
                st = kind + "_attn"

                def step(it, g):
                    for j in range(4):
                        key = (f"{st}{g}", j)
                        n = 4 * g + j + (NH if kind == "x" else 0)
                        e.wait_ge(*T.ready(it, key))
                        groups = max((n - PSLOTS) // 4 + 1, 0)
                        e.wait_ge(O.ready_sem, it * O.total + groups)
                        A.activation(prob[:, n % PSLOTS, 0:width], T.bank(key)[:, 0:width], ACT.Exp, scale=HD ** -0.5)\
                            .then_inc(exp_ready.sem, 1)
                return step

            def place_maxima(k):
                def step(it):
                    e.wait_ge(*nmT_ready(it, k + 1))
                    for r in range(3):
                        e.dma_start(QT[SW + r:SW + r + 1], nmT[r * NH:(r + 1) * NH]).then_inc(nm_placed.sem, 16)
                return step

            def y_high(kind):
                def step(it):
                    key = (kind + "_y", 0)
                    e.wait_ge(*G.ready(it, key))
                    A.copy(xT[0][:], two(G.bank(key)[:])).then_inc(yh_ready.sem, 1)
                return step

            pb = ("self_proj", 0)
            steps = {"x_load": x_load, "ctx_load": ctx_load, "ctx": context_high, "ln0_T": ln(0), "ln1_T": ln(1), "ln2_T": ln(2), "self_split": self_split,
                     "ctx_split": ctx_split, "x_split": x_split,
                     "ctx_kv": sumsq("ctx_kv", lambda t: kn[:, t], lambda it: raw_ready(it, 1)),
                     "xq": sumsq("xq", lambda t: res[:, t], lambda it: raw_ready(it, 2)),
                     "self_proj": sumsq("self_proj", lambda t: G.bank(pb)[:, t * D:(t + 1) * D], lambda it: G.ready(it, pb)),
                     "self_nm": place_maxima(0), "x_nm": place_maxima(1), "self_attn": exps("self", S + P), "x_attn": exps("x", 2 * S), "self_y": y_high("self"), "x_y": y_high("x")}

            def ffn(it, n):
                if n < NCH:
                    r = P if CHUNKS[n] < NCH - 1 else FLAST
                    e.wait_ge(*FR.ready(it, ("gu", n)))
                    if n >= 2:
                        e.wait_ge(*al_ready(it, n - 1))
                    A.activation(act[0:r, n % 2], FR.bank(("gu", n))[0:r, 0:S], ACT.Tanh, scale=0.5).then_inc(tanh_ready.sem, 1)
                if n == 2:
                    e.wait_ge(*gate_step(it, 2))
                    A.activation(gt[:, 1], gt[:, 0], ACT.Exp).then_inc(gate_exp.sem, 1)
                if n < NCH and CHUNKS[n] < NEC and CHUNKS[n] % 2 == 0:
                    j = CHUNKS[n] // 2
                    e.wait_ge(*FR.ready(it, ("cb", j)))
                    if j >= 2:
                        e.wait_ge(*fc_ready(it, 2 * (j - 1)))
                    w = 2 * S if CHUNKS[n] + 1 < NEC else S
                    A.copy(cb[:, j % 2, 0:w], FR.bank(("cb", j))[:, 0:w]).then_inc(cb_ready.sem, 1)
                if 1 <= n <= NCH:
                    m = n - 1
                    c = CHUNKS[m]
                    r = P if c < NCH - 1 else FLAST
                    e.wait_ge(*(fc_ready(it, c + 1) if c < NEC else fb_ready(it, m + 1)))
                    if m >= 2:
                        e.wait_ge(*down_done(it, m - 1))
                    A.copy(act_p[0][0:r, m % 2], act[0:r, m % 2]).then_inc(ah_ready.sem, 1)

            weight(0)
            program(e, PLAN["scalar"], steps, ffn, lambda st: [weight(n) for n in W_AFTER.get(st, ())])

        @block.gpsimd
        def _(e):
            L = nc.gpsimd

            def weight(n):
                e.wait_ge(wh_ready, n + 1)
                L.tensor_tensor(pieces[n][2], staged(n), pieces[n][1], ALU.subtract).then_inc(wl_ready, 1)

            def context_low(it):
                e.wait_ge(*ch_ready(it, 1))
                L.tensor_tensor(cT[1][:], ctxT[:], cT[0][:], ALU.subtract).then_inc(cl_ready.sem, 1)

            def ln(k):
                def step(it):
                    e.wait_ge(*ln_mv[k](it, 1))
                    L.tensor_tensor(ve[:], mv[:, :, 1], eps[:, 0], ALU.add).then_inc(ln_ve[k].sem, 1)
                    e.wait_ge(*ln_ve[k](it, 1))
                    L.tensor_tensor(rstd[:], ve[:], neghalf[:], ALU.pow).then_inc(ln_rstd[k].sem, 1)
                return step

            def rms(st):
                r = RMS.index(st)

                def step(it):
                    e.wait_ge(*ssq_ready(it, r + 1))
                    L.tensor_tensor(ms[:, r], ssq[:, r], eps[:, 1], ALU.add).then_inc(ms_ready.sem, 1)
                    e.wait_ge(*ms_ready(it, r + 1))
                    L.tensor_tensor(rrms[:, r], ms[:, r], neghalf[:], ALU.pow).then_inc(rms_ready.sem, 1)
                return step

            steps = {"ctx": context_low, "ln0s": ln(0), "ln1s": ln(1), "ln2s": ln(2),
                     "self_split": lambda it: cut_rest(e, L, "k", it), "ctx_split": lambda it: cut_rest(e, L, "ck", it), "ctx_kv": rms("ctx_kv"), "self_proj": rms("self_proj"), "xq": rms("xq")}

            def ffn(it, n):
                if 1 <= n <= NCH:
                    m = n - 1
                    r = P if CHUNKS[m] < NCH - 1 else FLAST
                    e.wait_ge(*ah_ready(it, m + 1))
                    L.tensor_tensor(act_p[1][0:r, m % 2], act[0:r, m % 2], act_p[0][0:r, m % 2], ALU.subtract).then_inc(al_ready.sem, 1)

            L.memset(eps[:, 0], LN_EPS)
            L.memset(eps[:, 1], RMS_EPS)
            L.memset(neghalf[:], -0.5).then_inc(pool_const, 1)
            e.wait_ge(pool_const, 1)
            weight(0)
            program(e, PLAN["gpsimd"], steps, ffn, lambda st: [weight(n) for n in W_AFTER.get(st, ())])

        @block.vector
        def _(e):
            V = nc.vector

            def carry(signal, count):
                e.wait_ge(signal, count)
                V.memset(idle[:], 0.0)

            def ln_stats_of(k):
                src = (x_in, x1, x2)[k]

                def step(it):
                    if k == 0:
                        e.wait_ge(*x_loaded(it, 16))
                    else:
                        e.wait_ge(*(x1_ready, x2_ready)[k - 1](it, 1))
                    for t in range(TT):
                        ins = V.bn_stats(bn[:, t], src[:, t])
                    ins.then_inc(ln_stats[k].sem, 1)
                    carry(*ln_stats[k](it, 1))
                    for t in range(TT):
                        ins = V.bn_aggr(mv[:, t], bn[:, t])
                    ins.then_inc(ln_mv[k].sem, 1)
                return step

            def ln(k):
                src = (x_in, x1, x2)[k]

                def step(it):
                    e.wait_ge(*ln_rstd[k](it, 1))
                    for t in range(TT):
                        ins = V.tensor_scalar(xn[:, t], src[:, t], mv[:, t, 0:1], rstd[:, t:t + 1], ALU.subtract, ALU.mult)
                    ins.then_inc(xn_ready[k].sem, 1)
                return step

            def ln_low(k):
                ring = (H, G, R)[k]

                def step(it):
                    key = (f"ln{k}_T", 0)
                    e.wait_ge(*xh_ready[k](it, 1))
                    hl = fT if k == 2 else xT
                    V.tensor_tensor(hl[1][:], two(ring.bank(key)[:]), hl[0][:], ALU.subtract).then_inc(xl_ready[k].sem, 1)
                return step

            def qkv(it):
                pair = lambda ap, n: ap.rearrange("p (h c j) -> p h c j", c=HD // 2, j=2)
                n = NH + NKV
                for t in range(TT):
                    key = ("qkv", t)
                    e.wait_ge(*H.ready(it, key))
                    ps = H.bank(key)
                    qk = pair(ps[:, 0:n * HD], n)
                    cs = rope_c[:, t].rearrange("p (c j) -> p c j", j=2)
                    sn = rope_s[:, t].rearrange("p (c j) -> p c j", j=2)
                    V.tensor_tensor(heads(rot[:, t]), heads(ps[:, 0:n * HD]), rope_c[:, t].unsqueeze(1).to_broadcast([P, n, HD]), ALU.mult)
                    for j in range(2):
                        ins = V.tensor_tensor(pair(rot2[:, t], n)[:, :, :, j], qk[:, :, :, 1 - j],
                                              sn[:, :, j].unsqueeze(1).to_broadcast([P, n, HD // 2]), ALU.mult)
                    ins.then_inc(rope_parts.sem, 1)
                    V.tensor_copy(V_s[:, t, :, 0:HD], heads(ps[:, n * HD:QKV])).then_inc(v_self.sem, 1)
                    e.wait_ge(*rope_parts(it, t + 1))
                    V.tensor_tensor(rot[:, t], rot[:, t], rot2[:, t], ALU.add).then_inc(rot_ready.sem, 1)

            def ctx_kv(it):
                for t in range(TT):
                    key = ("ctx_kv", t)
                    e.wait_ge(*G.ready(it, key))
                    ps = G.bank(key)
                    ins = V.tensor_tensor(kn[:, t], ps[:, 0:D], rows[:, K_BIAS], ALU.add)
                    if t == TT - 1:
                        ins.then_inc(raw_ready.sem, 1)
                    V.tensor_tensor(V_x[:, t, :, 0:HD], heads(ps[:, D:]), heads(rows[:, V_BIAS]), ALU.add).then_inc(v_ctx.sem, 1)

            def norm(st, buf, row):
                r = RMS.index(st)

                def step(it):
                    e.wait_ge(*rms_ready(it, r + 1))
                    for t in range(TT):
                        ins = V.scalar_tensor_tensor(buf[:, t], buf[:, t], rrms[:, r, t:t + 1], rows[:, row], ALU.mult, ALU.mult)
                    ins.then_inc(normed.sem, 1)
                return step

            def evacuate(st, count, dst, ready):
                def step(it):
                    for i in range(count):
                        e.wait_ge(*G.ready(it, (st, i)))
                        out, signal = dst(i)
                        V.tensor_copy(out, G.bank((st, i))[0:SW, :].bitcast(BF16).rearrange("p (h s) -> p h s", s=S)).then_inc(signal.sem, 1)
                return step

            def row_max(kind):
                st = kind + "_max"

                def step(it, h):
                    key = (f"{st}{h // 4}", h % 4)
                    e.wait_ge(*T.ready(it, key))
                    ps = T.bank(key)
                    if kind == "self":
                        ins = V.tensor_reduce(mx[:, h], ps[:, 0:3 * P].rearrange("p (b k) -> p b k", k=P), AX.X, ALU.max)
                    else:
                        ins = V.tensor_reduce(mx[:, h, 0:TT], two(ps[:]), AX.X, ALU.max)
                    ins.then_inc(head_max.sem, 1)
                    if h < NH - 1:
                        return
                    k = 0 if kind == "self" else 1
                    e.wait_ge(*head_max(it, (k + 1) * NH))
                    if kind == "self":
                        V.tensor_copy(nmx[:, 0], mx[:, :, 0])
                        V.tensor_tensor(nmx[:, 1], mx[:, :, 1], mx[:, :, 2], ALU.max).then_inc(nm_step.sem, 1)
                    else:
                        V.tensor_copy(nmx[:], mx[:, :, 0:TT].rearrange("p h t -> p t h")).then_inc(nm_step.sem, 1)
                    e.wait_ge(*nm_step(it, 4 * k + 1))
                    V.tensor_scalar(nmp[:, :, 0], nmx[:], -1.0, None, ALU.mult).then_inc(nm_step.sem, 1)
                    e.wait_ge(*nm_step(it, 4 * k + 2))
                    V.scalar_tensor_tensor(nmr[:], nmx[:], -1.0, nmp[:, :, 0], ALU.mult, ALU.subtract).then_inc(nm_step.sem, 1)
                    e.wait_ge(*nm_step(it, 4 * k + 3))
                    V.tensor_copy(nmp[:, :, 1], nmr[:]).then_inc(nm_step.sem, 1)
                    e.wait_ge(*nm_step(it, 4 * k + 4))
                    V.tensor_tensor(nmp[:, :, 2], nmr[:], nmp[:, :, 1], ALU.subtract).then_inc(nmp_ready.sem, 1)
                return step

            def nm_out(kind):
                def step(it):
                    key = (kind + "_nm", 0)
                    e.wait_ge(*G.ready(it, key))
                    V.tensor_copy(nmT[:], G.bank(key)[0:3 * NH, 0:S]).then_inc(nmT_ready.sem, 1)
                return step

            def attn(kind):
                st = kind + "_attn"

                def step(it, after):
                    for g in ((), (0,), (1,), (2, 3))[after]:
                        e.wait_ge(*O.ready(it, (st, g)))
                        V.tensor_copy(oT[:, g], O.bank((st, g))[:, 0:S]).then_inc(oT_ready.sem, 1)
                return step

            def out_tokens(kind):
                k = 0 if kind == "self" else 1

                def step(it):
                    for t in range(TT):
                        key = (kind + "_o", t)
                        e.wait_ge(*G.ready(it, key))
                        ps = G.bank(key)[:].rearrange("p (h c) -> p h c", c=VW)
                        V.reciprocal(rden[:, t], ps[:, :, HD]).then_inc(rden_ready.sem, 1)
                        e.wait_ge(*rden_ready(it, k * TT + t + 1))
                        V.tensor_tensor(heads(xn[:, t]), ps[:, :, 0:HD], rden[:, t].unsqueeze(2).to_broadcast([P, NH, HD]), ALU.mult)\
                            .then_inc(y_ready.sem, 1)
                return step

            def y_low(kind):
                k = 0 if kind == "self" else 1

                def step(it):
                    key = (kind + "_y", 0)
                    e.wait_ge(*yh_ready(it, k + 1))
                    V.tensor_tensor(xT[1][:], two(G.bank(key)[:]), xT[0][:], ALU.subtract).then_inc(yl_ready.sem, 1)
                return step

            def self_proj(it):
                key = ("self_proj", 0)
                r = RMS.index("self_proj")
                e.wait_ge(*rms_ready(it, r + 1))
                for t in range(TT):
                    ins = V.scalar_tensor_tensor(res[:, t], G.bank(key)[:, t * D:(t + 1) * D], rrms[:, r, t:t + 1], rows[:, A_NORM],
                                                 ALU.mult, ALU.mult)
                ins.then_inc(res_ready.sem, 1)
                e.wait_ge(*res_ready(it, 1))
                V.tensor_tensor(x1[:], res[:], x_in[:], ALU.add).then_inc(x1_ready.sem, 1)

            def xq(it):
                key = ("xq", 0)
                e.wait_ge(*G.ready(it, key))
                V.tensor_tensor(res[:], two(G.bank(key)[:]), rows[:, Q_BIAS].unsqueeze(1).to_broadcast([P, TT, D]), ALU.add)\
                    .then_inc(raw_ready.sem, 1)

            def stored(it):
                carry(*out_done(it, 16))

            def x_proj(it):
                key = ("x_proj", 0)
                e.wait_ge(*R.ready(it, key))
                V.tensor_tensor(res[:], two(R.bank(key)[:]), rows[:, O_BIAS].unsqueeze(1).to_broadcast([P, TT, D]), ALU.add)\
                    .then_inc(res_ready.sem, 1)
                e.wait_ge(*res_ready(it, 2))
                V.tensor_tensor(x2[:], res[:], x1[:], ALU.add).then_inc(x2_ready.sem, 1)

            steps = {"ln0s": ln_stats_of(0), "ln1s": ln_stats_of(1), "ln2s": ln_stats_of(2), "ln0n": ln(0), "ln1n": ln(1), "ln2n": ln(2),
                     "ln0_T": ln_low(0), "ln1_T": ln_low(1), "ln2_T": ln_low(2),
                     "self_nm": nm_out("self"), "x_nm": nm_out("x"), "self_y": y_low("self"), "x_y": y_low("x"),
                     "qkv": qkv, "ctx_kv": ctx_kv, "ctx_split": norm("ctx_kv", kn, K_NORM), "self_split": lambda it: cut_rest(e, V, "q", it),
                     "x_split": lambda it: (norm("xq", res, Q_NORM)(it), cut_rest(e, V, "xq", it)),
                     "self_T": evacuate("self_T", 5, lambda i: (QT[0:SW, 4 * i - 4:4 * i], QT_ready) if i else (KT_s[0:SW], KTs_ready), None),
                     "ctx_T": evacuate("ctx_T", 4, lambda i: (KT_x[0:SW, 4 * i:4 * i + 4], KTx_ready), None),
                     "x_T": evacuate("x_T", 4, lambda i: (QT[0:SW, 4 * i:4 * i + 4], QT_ready), None),
                     "self_max": row_max("self"), "x_max": row_max("x"), "self_attn": attn("self"), "x_attn": attn("x"),
                     "self_o": out_tokens("self"), "x_o": out_tokens("x"), "self_proj": self_proj, "xq": xq, "x_proj": x_proj, "stored": stored}

            def router(it, k):
                lg = FR.bank(("router", 1))[:, 0:TT * E].rearrange("p (t e) -> p t e", e=E)
                wide = lambda ap: ap.unsqueeze(2).to_broadcast([P, TT, E])
                if k == 0:
                    e.wait_ge(*FR.ready(it, ("router", 1)))
                elif k in (5, 6):
                    carry(*gate_step(it, k))
                else:
                    e.wait_ge(*gate_step(it, k))
                if k == 0:
                    ins = V.tensor_reduce(gm[:, 0], lg, AX.X, ALU.max)
                elif k == 1:
                    ins = V.tensor_tensor(gt[:, 0], lg, wide(gm[:, 0]), ALU.subtract)
                elif k == 2:
                    e.wait_ge(*gate_exp(it, 1))
                    ins = V.tensor_reduce(gm[:, 1], gt[:, 1], AX.X, ALU.add)
                elif k == 3:
                    ins = V.reciprocal(gm[:, 2], gm[:, 1])
                elif k == 4:
                    ins = V.tensor_tensor(gt[:, 2], gt[:, 1], wide(gm[:, 2]), ALU.mult)
                elif k == 5:
                    for t in range(TT):
                        ins = V.max(top[:, t], gt[:, 2, t])
                elif k == 6:
                    for t in range(TT):
                        ins = V.max_index(topi[:, t], top[:, t], gt[:, 2, t])
                elif k == 7:
                    ins = V.tensor_copy(topf[:], topi[:])
                elif k == 8:
                    for j in range(2):
                        ins = V.tensor_tensor(gt[:, 3 + j], iota_e[:].unsqueeze(1).to_broadcast([P, TT, E]),
                                              topf[:, :, j:j + 1].to_broadcast([P, TT, E]), ALU.is_equal)
                elif k == 9:
                    ins = V.tensor_tensor(gt[:, 3], gt[:, 3], gt[:, 4], ALU.add)
                elif k == 10:
                    ins = V.tensor_tensor(gt[:, 5], gt[:, 3], gt[:, 2], ALU.mult)
                elif k == 11:
                    ins = V.tensor_copy(cp[:, :, 0], gt[:, 5])
                elif k == 12:
                    ins = V.tensor_tensor(gt[:, 4], gt[:, 5], cp[:, :, 0], ALU.subtract)
                elif k == 13:
                    ins = V.tensor_copy(cp[:, :, 1], gt[:, 4])
                else:
                    ins = V.tensor_tensor(cp[:, :, 2], gt[:, 4], cp[:, :, 1], ALU.subtract)
                ins.then_inc(gate_step.sem if k < NR - 1 else cp_ready.sem, 1)

            steps["router"] = router

            def ffn(it, n):
                if n < NCH:
                    c = CHUNKS[n]
                    r = P if c < NCH - 1 else FLAST
                    ps = FR.bank(("gu", n))
                    slot = act[0:r, n % 2]
                    if n == 0:
                        e.wait_ge(*FR.ready(it, ("gu", 0)))
                        V.tensor_copy(lgT[FLAST:FLAST + E, :], ps[FLAST:FLAST + E, 0:S]).then_inc(lgT_ready.sem, 1)
                    e.wait_ge(*tanh_ready(it, n + 1))
                    V.scalar_tensor_tensor(slot, slot, 1.0, ps[0:r, 0:S], ALU.add, ALU.mult).then_inc(fa_ready.sem, 1)
                    e.wait_ge(*fa_ready(it, n + 1))
                    V.scalar_tensor_tensor(slot, slot, 0.5, ps[0:r, S:2 * S], ALU.mult, ALU.mult).then_inc(fb_ready.sem, 1)
                    if n == 3:
                        e.wait_ge(*FR.ready(it, ("router", 2)))
                        V.tensor_copy(cpT, FR.bank(("router", 2))[0:3 * E, 0:P].bitcast(BF16)).then_inc(cpT_ready.sem, 1)
                    if c < NEC:
                        e.wait_ge(*cb_ready(it, c // 2 + 1))
                        e.wait_ge(*fb_ready(it, n + 1))
                        V.tensor_tensor(slot, slot, cb[:, c // 2 % 2, c % 2 * S:(c % 2 + 1) * S], ALU.mult).then_inc(fc_ready.sem, 1)
                if n == NCH + LAG - 1:
                    e.wait_ge(*down_done(it, NCH))
                    V.tensor_tensor(x2[:], two(Y[:]), x2[:], ALU.add).then_inc(x3_ready.sem, 1)

            V.memset(QT[SW:P], 0.0)
            V.memset(KT_s[SW:P], 1.0)
            V.memset(KT_x[SW:P], 1.0)
            V.memset(V_s[:], 0.0)
            V.memset(V_x[:], 0.0).then_inc(dve_const, 1)
            e.wait_ge(dve_const, 1)
            V.memset(V_s[:, :, :, HD:HD + 1], 1.0)
            V.memset(V_x[:, :, :, HD:HD + 1], 1.0).then_inc(dve_const, 1)
            e.wait_ge(const_loaded, 16 * NCONST)
            program(e, PLAN["vector"], steps, ffn)

        @block.tensor
        def _(e):
            def product(out, lhs, lcols, rhs, rcols, chunks, first=True, rows_=P):
                todo = [(c, i, j) for c in chunks for i, j in ((0, 0), (0, 1), (1, 0))]
                for n, (c, i, j) in enumerate(todo):
                    ins = e.matmul(out, lhs[i][0:rows_, c, lcols], rhs[j][0:rows_, c, rcols], start=first and n == 0, stop=n == len(todo) - 1,
                                   skip_group_check=True)
                return ins

            def tile(t):
                return slice(t * P, (t + 1) * P)

            def weights(it, n):
                if isinstance(it, int) and it == 0:
                    e.wait_ge(wl_ready, n)

            def values_bank_free(it):
                if not first(it):
                    e.wait_ge(*oT_ready(it - 1, 4))

            def ln(k):
                ring = (H, G, R)[k]

                def step(it):
                    key = (f"ln{k}_T", 0)
                    e.wait_ge(*xn_ready[k](it, 1))
                    if k == 0:
                        values_bank_free(it)
                    if k == 0 and isinstance(it, int) and it == 0:
                        e.wait_ge(const_loaded, 16 * NCONST)
                    ring.wait_free(e, it, key)
                    for c in range(KC):
                        for t in range(TT):
                            ins = e.transpose(two(ring.bank(key)[:])[:, c, tile(t)], xn[:, t, c * P:(c + 1) * P], ident[:])
                    ins.then_inc(ring.ready_sem, 1)
                return step

            def qkv(it):
                weights(it, 1)
                e.wait_ge(*xh_ready[0](it, 1))
                e.wait_ge(*xl_ready[0](it, 1))
                for t in range(TT):
                    key = ("qkv", t)
                    H.wait_free(e, it, key)
                    product(H.bank(key)[:, 0:QKV], xT, tile(t), wqkv, slice(0, QKV), range(KC)).then_inc(H.ready_sem, 1)

            def ctx_kv(it):
                weights(it, 3)
                e.wait_ge(*ch_ready(it, 1))
                e.wait_ge(*cl_ready(it, 1))
                for t in range(TT):
                    key = ("ctx_kv", t)
                    G.wait_free(e, it, key)
                    product(G.bank(key)[:], cT, tile(t), wkv, slice(0, 2 * D), range(KC)).then_inc(G.ready_sem, 1)

            def unstack(st, cuts):
                def step(it):
                    i = 0
                    for which in cuts:
                        _, stk, nh, _ = CUT[which]
                        e.wait_ge(*low_ready[which](it, TT))
                        for h0 in range(0, nh, 4):
                            key = (st, i)
                            G.wait_free(e, it, key)
                            ps = G.bank(key)[0:SW, :].bitcast(BF16).rearrange("p (h s) -> p h s", s=S)
                            for h in range(4):
                                for t in range(TT):
                                    ins = e.transpose(ps[:, h, tile(t)], stk[:, t, h0 + h, :], identb[:])
                            ins.then_inc(G.ready_sem, 1)
                            i += 1
                return step

            def self_max(it, g):
                e.wait_ge(*QT_ready(it, g + 1))
                if g == 0:
                    e.wait_ge(*KTs_ready(it, 1))
                for h in range(4 * g, 4 * g + 4):
                    key = (f"self_max{g}", h % 4)
                    ps = T.bank(key)
                    T.wait_free(e, it, key)
                    e.matmul(ps[:, 0:3 * P].rearrange("p (b k) -> p b k", k=P)[:, 0:3:2], identb[:], mask_q[:].unsqueeze(1).to_broadcast([P, 2, P]),
                             start=True, stop=False, skip_group_check=True)
                    e.matmul(ps[:, 0:P], QT[0:SW, h, 0:P], KT_s[0:SW, h // GQ, 0:P], start=False, stop=False, skip_group_check=True)
                    e.matmul(ps[:, P:3 * P], QT[0:SW, h, P:S], KT_s[0:SW, h // GQ, :], start=False, stop=True, skip_group_check=True)\
                        .then_inc(T.ready_sem, 1)

            def x_max(it, g):
                e.wait_ge(*QT_ready(it, 4 + g + 1))
                e.wait_ge(*KTx_ready(it, g + 1))
                for h in range(4 * g, 4 * g + 4):
                    key = (f"x_max{g}", h % 4)
                    T.wait_free(e, it, key)
                    for t in range(TT):
                        ins = e.matmul(T.bank(key)[:, t * S:(t + 1) * S], QT[0:SW, h, tile(t)], KT_x[0:SW, h, :], start=True, stop=True,
                                       skip_group_check=True)
                    ins.then_inc(T.ready_sem, 1)

            def attn(kind):
                st = kind + "_attn"
                k = 0 if kind == "self" else 1

                def values(it, g):
                    if kind == "self" and g == 0 and not first(it):
                        e.wait_ge(*xl_ready[2](it - 1, 1))
                    if kind == "x" and g == 0 and not (isinstance(it, int) and it == B - 1):
                        e.wait_ge(*v_self(it + 1, TT))
                    O.wait_free(e, it, (st, g))
                    out = O.bank((st, g))
                    for kt in range(TT):
                        for j in range(4):
                            h = 4 * g + j
                            if kt == 0:
                                e.wait_ge(*exp_ready(it, k * NH + h + 1))
                            v = V_s[:, kt, h // GQ, :] if kind == "self" else V_x[:, kt, h, :]
                            p = prob[:, (k * NH + h) % PSLOTS, :]
                            if kind == "self" and kt == 1:
                                o, p = out[VW * j:VW * (j + 1), P:S], p[:, S:S + P]
                            else:
                                o, p = out[VW * j:VW * (j + 1), 0:S], p[:, kt * S:(kt + 1) * S]
                            ins = e.matmul(o, v, p, start=kt == 0, stop=kt == TT - 1, skip_group_check=True, tile_position=(0, VW * j))
                    ins.then_inc(O.ready_sem, 1)

                def maxima(it):
                    key = (kind + "_nm", 0)
                    e.wait_ge(*nmp_ready(it, k + 1))
                    G.wait_free(e, it, key)
                    ps = G.bank(key)[0:3 * NH, 0:S]
                    for t in range(TT):
                        ins = e.matmul(ps[:, tile(t)], nmp[:, t].rearrange("p r h -> p (r h)"), identb[:], start=True, stop=True,
                                       skip_group_check=True)
                    ins.then_inc(G.ready_sem, 1)

                def step(it, group):
                    if group == 0:
                        e.wait_ge(*(v_self, v_ctx)[k](it, TT))
                        e.wait_ge(*nm_placed(it, 48 * (k + 1)))
                    for h in range(4 * group, 4 * group + 4):
                        key = (f"{st}{group}", h % 4)
                        ps = T.bank(key)
                        T.wait_free(e, it, key)
                        if kind == "self":
                            kT = KT_s[:, h // GQ]
                            e.matmul(ps[:, 0:3 * P].rearrange("p (b k) -> p b k", k=P)[:, 0:3:2], identb[:], mask_k[:].unsqueeze(1).to_broadcast([P, 2, P]),
                                     start=True, stop=False, skip_group_check=True)
                            e.matmul(ps[:, 0:S], kT[:, 0:P], QT[:, h, :], start=False, stop=False, skip_group_check=True)
                            ins = e.matmul(ps[:, S:S + P], kT[:, P:S], QT[:, h, P:S], start=False, stop=True, skip_group_check=True)
                        else:
                            kT = KT_x[:, h]
                            e.matmul(ps[:, 0:S], kT[:, 0:P], QT[:, h, :], start=True, stop=True, skip_group_check=True)
                            ins = e.matmul(ps[:, S:2 * S], kT[:, P:S], QT[:, h, :], start=True, stop=True, skip_group_check=True)
                        ins.then_inc(T.ready_sem, 1)
                        if h % 4 == 1 and h > 4:
                            values(it, h // 4 - 1)
                    if group == 3:
                        values(it, 3)
                return maxima, step

            def to_tokens(kind):
                k = 0 if kind == "self" else 1

                def step(it):
                    e.wait_ge(*oT_ready(it, 4 * (k + 1)))
                    for t in range(TT):
                        key = (kind + "_o", t)
                        G.wait_free(e, it, key)
                        for g in range(4):
                            ins = e.transpose(G.bank(key)[:, g * P:(g + 1) * P], oT[:, g, tile(t)], ident[:])
                        ins.then_inc(G.ready_sem, 1)
                return step

            def y_transposed(kind):
                k = 0 if kind == "self" else 1

                def step(it):
                    key = (kind + "_y", 0)
                    G.wait_free(e, it, key)
                    e.wait_ge(*y_ready(it, (k + 1) * TT))
                    for c in range(KC):
                        for t in range(TT):
                            ins = e.transpose(two(G.bank(key)[:])[:, c, tile(t)], xn[:, t, c * P:(c + 1) * P], ident[:])
                    ins.then_inc(G.ready_sem, 1)
                return step

            def project(st, lhs, rhs, n, waits):
                ring = R if st == "x_proj" else G

                def step(it):
                    if st == "x_proj":
                        e.wait_ge(wl_ready, n)
                        e.wait_ge(*oT_ready(it, 8))
                    weights(it, n)
                    for w, k in waits:
                        e.wait_ge(*w(it, k))
                    ring.wait_free(e, it, (st, 0))
                    for t in range(TT):
                        ins = product(two(ring.bank((st, 0))[:])[:, t], lhs, tile(t), rhs, slice(0, D), range(KC))
                    ins.then_inc(ring.ready_sem, 1)
                return step

            (self_nm, self_attn), (x_nm, x_attn) = attn("self"), attn("x")
            steps = {"ln0_T": ln(0), "ln1_T": ln(1), "ln2_T": ln(2), "qkv": qkv, "ctx_kv": ctx_kv, "self_T": unstack("self_T", ("k", "q")), "ctx_T": unstack("ctx_T", ("ck",)), "x_T": unstack("x_T", ("xq",)),
                     "self_max": self_max, "x_max": x_max, "self_nm": self_nm, "x_nm": x_nm,
                     "self_attn": self_attn, "x_attn": x_attn, "self_o": to_tokens("self"), "x_o": to_tokens("x"),
                     "self_y": y_transposed("self"), "x_y": y_transposed("x"),
                     "self_proj": project("self_proj", xT, wp, 4, [(yh_ready, 1), (yl_ready, 1)]),
                     "xq": project("xq", xT, wq, 5, [(xh_ready[1], 1), (xl_ready[1], 1)]),
                     "x_proj": project("x_proj", xT, wo, 6, [(yh_ready, 2), (yl_ready, 2)])}

            def ffn(it, n):
                if n == 0:
                    e.wait_ge(wl_ready, NPIECE)
                    e.wait_ge(*xh_ready[2](it, 1))
                    e.wait_ge(*xl_ready[2](it, 1))
                if n < NCH:
                    c = CHUNKS[n]
                    key = ("gu", n)
                    last = c == NCH - 1
                    FR.wait_free(e, it, key)
                    gc, uc = slice(c * P, GW if last else (c + 1) * P), slice(c * P, FT if last else (c + 1) * P)
                    ps = FR.bank(key)
                    product(ps[0:FLAST + E if last else P, 0:S], wg, gc, fT, slice(0, S), range(KC))
                    product(ps[0:FLAST if last else P, S:2 * S], wu, uc, fT, slice(0, S), range(KC)).then_inc(FR.ready_sem, 1)
                if n == 1:
                    e.wait_ge(*lgT_ready(it, 1))
                    FR.wait_free(e, it, ("router", 1))
                    for t in range(TT):
                        ins = e.matmul(FR.bank(("router", 1))[:, t * E:(t + 1) * E], lgT[FLAST:FLAST + E, tile(t)],
                                       ident[FLAST:FLAST + E, FLAST:FLAST + E], start=True, stop=True, skip_group_check=True)
                    ins.then_inc(FR.ready_sem, 1)
                if n == 3:
                    e.wait_ge(*cp_ready(it, 1))
                    FR.wait_free(e, it, ("router", 2))
                    for t in range(TT):
                        ins = e.transpose(FR.bank(("router", 2))[0:3 * E, 0:P].bitcast(BF16)[:, tile(t)], cp[:, t].rearrange("p r e -> p (r e)"), identb[:])
                    ins.then_inc(FR.ready_sem, 1)
                if n < NCH and CHUNKS[n] < NEC and CHUNKS[n] % 2 == 0:
                    j = CHUNKS[n] // 2
                    FR.wait_free(e, it, ("cb", j))
                    e.wait_ge(*cpT_ready(it, 1))
                    for i in range(2 * j, min(2 * j + 2, NEC)):
                        ins = e.matmul(FR.bank(("cb", j))[:, i % 2 * S:(i % 2 + 1) * S], sel_exp[:, i, :], cpT, start=True, stop=True,
                                       skip_group_check=True)
                    ins.then_inc(FR.ready_sem, 1)
                if n >= LAG:
                    m = n - LAG
                    c = CHUNKS[m]
                    r = P if c < NCH - 1 else FLAST
                    e.wait_ge(*ah_ready(it, m + 1))
                    e.wait_ge(*al_ready(it, m + 1))
                    for t in range(TT):
                        for i, (ai, wi) in enumerate(((0, 0), (0, 1), (1, 0))):
                            ins = e.matmul(two(Y[:])[:, t], act_p[ai][0:r, m % 2, tile(t)], wd[wi][0:r, c, :],
                                           start=m == 0 and t == 0 and i == 0, stop=m == NCH - 1 and i == 2, skip_group_check=True)
                    ins.then_inc(down_done.sem, 1)

            e.wait_ge(dve_const, 2)
            program(e, PLAN["tensor"], steps, ffn)


_OUT = ((B, S, D), "float32")


def _constants(np):
    p = np.arange(P)
    pos = np.arange(S, dtype=np.float32)
    inv = (1.0 / np.float32(10000.0) ** (np.arange(0, HD, 2, dtype=np.float32) / np.float32(HD))).astype(np.float32)
    angle = (pos[:, None] * inv[None, :]).astype(np.float32)
    cos, sin = np.cos(angle), np.sin(angle)
    by_tile = lambda t: np.ascontiguousarray(t.reshape(TT, P, HD).transpose(1, 0, 2).astype(np.float32))
    sel_exp = np.zeros((3, E, NEC * P), np.float32)
    for e in range(E):
        sel_exp[:, e, e * F:(e + 1) * F] = 1.0
    return {"rope_c": by_tile(np.repeat(cos, 2, axis=1)), "rope_s": by_tile(np.stack([-sin, sin], axis=-1).reshape(S, HD)),
            "ident": np.eye(P, dtype=np.float32), "identb": np.eye(P, dtype=np.float32),
            "mask_q": np.where(p[None, :] <= p[:, None], 0.0, MASKED).astype(np.float32),
            "mask_k": np.where(p[:, None] <= p[None, :], 0.0, MASKED).astype(np.float32),
            "sel_exp": sel_exp.reshape(3 * E, NEC, P),
            "iota_e": np.tile(np.arange(E, dtype=np.float32), (P, 1))}


_BF16 = ("identb", "mask_q", "mask_k", "sel_exp")


def kernel(**inputs):
    import ml_dtypes as _ml_dtypes
    import numpy as _np
    import concourse.bacc as _bacc
    from concourse.bass_utils import run_bass_kernel_spmd as _run

    g = {n: _np.asarray(v) for n, v in inputs.items()}
    gu, sgu = g["L0_ffn_gate_up_weights"], g["L0_ffn_shared_gate_up"]
    lay = {
        "x": g["x"],
        "ctxT": g["ctx_2048"].reshape(B, S, KC, P).transpose(0, 3, 2, 1),
        "w_attn": g["L0_attn_w_attn"], "w_proj": g["L0_attn_w_proj"],
        **{n: g["L0_xattn_" + n].T for n in ("q_w", "k_img_w", "v_img_w", "o_w")},
        "wg": _np.concatenate([gu[:, :F].reshape(E * F, D), sgu[:FS], g["L0_ffn_gate_weight"]]).T,
        "wu": _np.concatenate([gu[:, F:].reshape(E * F, D), sgu[FS:]]).T,
        "wd": _np.concatenate([g["L0_ffn_down_weights"].transpose(0, 2, 1).reshape(E * F, D), g["L0_ffn_shared_down"].T]),
        "rows": _np.stack([g["L0_xattn_" + n] for n in ("q_b", "k_img_b", "v_img_b", "o_b", "norm_q_w", "norm_k_img_w")]
                          + [g["L0_attn_norm_w"]]),
        **_constants(_np)}
    nc = _bacc.Bacc("TRN2", target_bir_lowering=False, num_devices=1)
    arrays, aps = {}, {}
    for name, v in lay.items():
        v = _np.array(v, dtype=_ml_dtypes.bfloat16) if name in _BF16 else _np.ascontiguousarray(v)
        arrays["in_" + name] = v
        aps[name] = nc.dram_tensor("in_" + name, v.shape, mybir.dt.from_np(v.dtype), kind="ExternalInput").ap()
    aps["out"] = nc.dram_tensor("out_0", _OUT[0], F32, kind="ExternalOutput").ap()
    build(nc, aps)
    r = _run(nc, [arrays], core_ids=[0])
    return r.results[0]["out_0"]
```

```python
from contextlib import ExitStack

import concourse.bass as bass
import numpy as np
from concourse import mybir

ALU = mybir.AluOpType
ACT = mybir.ActivationFunctionType
AX = mybir.AxisListType
F32 = mybir.dt.float32
F32R = mybir.dt.float32r
BF16 = mybir.dt.bfloat16
U32 = mybir.dt.uint32

P = 128
B, S, D = 4, 256, 256
TT = S // P
KC = D // P
NH, HD, NKV = 16, 16, 4
GQ = NH // NKV
QKV = D + 2 * NKV * HD
E, F, FS = 8, 176, 352
FT = E * F + FS
NCH = -(-FT // P)
FLAST = FT - (NCH - 1) * P
NEC = E * F // P
GW = FT + E
LN_EPS, RMS_EPS = 1e-5, 1e-6
MASKED = -3.0e38
SW = 6 * HD
PSLOTS = 6
VW = 32
Q_BIAS, K_BIAS, V_BIAS, O_BIAS, Q_NORM, K_NORM, A_NORM = range(7)


class Signal:

    def __init__(self, sem, per):
        self.sem, self.per = sem, per

    def __call__(self, it, k):
        return self.sem, it * self.per + k


class Ring:

    def __init__(self, banks, ready, uses, wrap=True):
        self.banks, self.ready_sem, self.total = banks, ready, len(uses)
        self.place, last = {}, [None] * len(banks)
        for i, (key, reader) in enumerate(uses):
            b = i % len(banks)
            self.place[key] = [i, b, last[b]]
            last[b] = reader
        for key, reader in uses[:len(banks)]:
            if self.place[key][2] is None and wrap:
                self.place[key][2] = last[self.place[key][1]] + (-1,)

    def bank(self, key):
        return self.banks[self.place[key][1]]

    def ready(self, it, key):
        return self.ready_sem, it * self.total + self.place[key][0] + 1

    def wait_free(self, pe, it, key):
        if self.place[key][2] is None:
            return
        signal, k, *before = self.place[key][2]
        if before:
            if isinstance(it, int) and it == 0:
                return
            k -= signal.per
        pe.wait_ge(*signal(it, k))


LAG = 2
PLAN = {
    "tensor": """
        self_T self_max0 x_o- ctx_kv x_y- self_max1 x_proj- self_max2 self_max3 ln2_T- self_nm ctx_T F F
        self_attn0 self_attn1 self_attn2 self_attn3 self_o F self_y self_proj F F F ln1_T F xq F ln0_T+ F x_T
        x_max0 qkv+ x_max1 F x_max2 x_max3 F x_nm F F x_attn0 F x_attn1 F x_attn2 F x_attn3""",
    "vector": """
        self_T self_max0 self_max1 x_o- self_max2 self_max3 ctx_kv self_max4 x_y- self_max5 ctx_split self_max6 self_max7
        x_proj- ln2s- self_max8 self_max9 self_max10 self_max11 self_max12 ln2n- self_max13 self_max14 self_max15 ln2_T-
        self_nm ctx_T F F r r r r self_attn0 r r r self_attn1 r r r self_attn2 r r r r r self_attn3 self_o F self_y
        F self_proj ln1s F ln1n F ln1_T ln0s+ F xq F ln0n+ x_split ln0_T+ F x_T
        x_max0 x_max1 x_max2 x_max3 qkv+ x_max4 x_max5 x_max6 x_max7 F x_max8 x_max9 x_max10 x_max11
        x_max12 x_max13 x_max14 x_max15 F x_nm F F x_attn0 F x_attn1 F x_attn2 F x_attn3 stored-""",
    "scalar": """
        self_T ctx_load+ ctx_kv x_y- ctx_split ln2s- ln2_T- self_nm ctx_T F F ctx+ self_attn0 self_attn1 self_attn2 self_attn3
        F self_y self_proj F ln1s F F ln1_T x_load+ ln0s+ F xq F x_split ln0_T+ F x_T qkv+ F self_split+ F x_nm F F
        x_attn0 F x_attn1 F x_attn2 F x_attn3"""}
PLAN = {engine: plan.split() for engine, plan in PLAN.items()}
PLAN["gpsimd"] = PLAN["scalar"]
NR = 15
assert all(plan.count("F") == NCH + LAG for plan in PLAN.values()) and PLAN["vector"].count("r") == NR
HEAD = ["ln0s", "ln0n", "ln0_T", "qkv", "self_split", "ctx"]
ATTN = [st for st in PLAN["tensor"] if st[-1] not in "F+-"]
CHUNKS = [NCH - 1] + list(range(NEC, NCH - 1)) + list(range(NEC))


def build(nc, a):
    x_v = a["x"].rearrange("b (t p) d -> b p t d", p=P)
    out_v = a["out"].rearrange("b (t p) d -> b p t d", p=P)

    def by_row_chunk(name):
        return a[name].rearrange("(c p) n -> p c n", p=P)

    with ExitStack() as ctx:
        def sb(name, shape, dt=F32):
            return ctx.enter_context(nc.sbuf_tensor(name, shape, dt))

        def sem(name):
            return ctx.enter_context(nc.semaphore(name))

        def sig(name, per):
            return Signal(sem(name), per)

        wqkv = [sb("wqkv_" + s, [P, KC, QKV], F32R) for s in "hl"]
        wp = [sb("wp_" + s, [P, KC, D], F32R) for s in "hl"]
        wq = [sb("wq_" + s, [P, KC, D], F32R) for s in "hl"]
        wkv = [sb("wkv_" + s, [P, KC, 2 * D], F32R) for s in "hl"]
        wo = [sb("wo_" + s, [P, KC, D], F32R) for s in "hl"]
        wg = [sb("wg_" + s, [P, KC, GW], F32R) for s in "hl"]
        wu = [sb("wu_" + s, [P, KC, FT], F32R) for s in "hl"]
        wd = [sb("wd_" + s, [P, NCH, D], F32R) for s in "hl"]
        STAGE = 896
        stage = sb("stage", [P, 2, STAGE])
        rows = sb("rows", [P, 7, D])
        rope_c = sb("rope_c", [P, TT, HD])
        rope_s = sb("rope_s", [P, TT, HD])
        ident = sb("ident", [P, P])
        identb = sb("identb", [P, P], BF16)
        mask_q = sb("mask_q", [P, P], BF16)
        mask_k = sb("mask_k", [P, P], BF16)
        sel_exp = sb("sel_exp", [3 * E, NEC, P], BF16)
        iota_e = sb("iota_e", [P, E])
        neghalf = sb("neghalf", [P, TT])
        eps = sb("eps", [P, 2, TT])
        idle = sb("idle", [P, 1])
        x_in, x1, x2 = (sb(n, [P, TT, D]) for n in ("x_in", "x1", "x2"))
        xn = sb("xn", [P, TT, D])
        xT = [sb("xT_" + s, [P, KC, S], F32R) for s in "hl"]
        fT = [sb("fT_" + s, [P, KC, S], F32R) for s in "hl"]
        ctxT = sb("ctxT", [P, KC, S])
        cT = [sb("cT_" + s, [P, KC, S], F32R) for s in "hl"]
        bn, mv = sb("bn", [P, TT, 6]), sb("mv", [P, TT, 2])
        ve, rstd = sb("ve", [P, TT]), sb("rstd", [P, TT])
        rot, rot2 = (sb(n, [P, TT, (NH + NKV) * HD]) for n in ("rot", "rot2"))
        kn_res = sb("kn_res", [P, 2 * TT, D])
        kn, res, oT = kn_res[:, 0:TT], kn_res[:, TT:], kn_res[:].rearrange("p a n -> p (a n)").rearrange("p (g s) -> p g s", g=4)
        ssq, ms, rrms = sb("ssq", [P, 3, TT]), sb("ms", [P, 3, TT]), sb("rrms", [P, 3, TT])
        stack = sb("stack", [P, TT, NH, SW], BF16)
        stack_k = sb("stack_k", [P, TT, NKV, SW], BF16)
        QT = sb("QT", [P, NH, S], BF16)
        KT_s = sb("KT_s", [P, NKV, S], BF16)
        KT_x = sb("KT_x", [P, NH, S], BF16)
        V_s = sb("V_s", [P, TT, NKV, VW])
        V_x = sb("V_x", [P, TT, NH, VW])
        mx = sb("mx", [P, NH, 3])
        nmx, nmr = sb("nmx", [P, TT, NH]), sb("nmr", [P, TT, NH])
        nmp = sb("nmp", [P, TT, 3, NH], BF16)
        nmT = sb("nmT", [3 * NH, S], BF16)
        prob = sb("prob", [P, PSLOTS, 2 * S])
        rden = sb("rden", [P, TT, NH])
        act = stage[:, 0, 0:2 * S].rearrange("p (n s) -> p n s", n=2)
        lgT = stage[:, 0, 2 * S:3 * S]
        cpT = stage[0:3 * E, 0, 2 * S:2 * S + P].bitcast(BF16)
        flat = stage[:].rearrange("p a n -> p (a n)")
        cb = flat[:, 3 * S:7 * S].rearrange("p (n s) -> p n s", n=2)
        act_p = [sb("act_" + s, [P, 2, S], F32R) for s in "hl"]
        gt = sb("gt", [P, 6, TT, E])
        gm = sb("gm", [P, 3, TT])
        top, topi, topf = sb("top", [P, TT, 8]), sb("topi", [P, TT, 8], U32), sb("topf", [P, TT, 8])
        cp = sb("cp", [P, TT, 3, E], BF16)

        bank = [ctx.enter_context(nc.psum_tensor(f"bank{i}", [P, 512], F32)) for i in range(8)]
        Y = bank[7]

        w_loaded = [sem("w_loaded0"), sem("w_loaded1")]
        ident_loaded, const_loaded = sem("ident_loaded"), sem("const_loaded")
        dve_const, pool_const = sem("dve_const"), sem("pool_const")
        wh_ready, wl_ready = sem("wh_ready"), sem("wl_ready")
        x_loaded, ctx_loaded = sig("x_loaded", 16), sig("ctx_loaded", 16)
        ch_ready, cl_ready = sig("ch_ready", 1), sig("cl_ready", 1)
        ln_stats, ln_mv, ln_ve, ln_rstd, xn_ready, xh_ready, xl_ready = (
            [sig(f"ln{k}_{n}", 1) for k in range(3)] for n in ("stats", "mv", "ve", "rstd", "xn_ready", "high_ready", "low_ready"))
        rope_parts, rot_ready, v_self, v_ctx = sig("rope_parts", TT), sig("rot_ready", TT), sig("v_self", TT), sig("v_ctx", TT)
        high_ready, rest_ready, middle_ready, low_ready = ({w: sig(f"{w}_{n}_ready", TT) for w in ("q", "k", "ck", "xq")}
                                                           for n in ("high", "rest", "middle", "low"))
        KTs_ready = sig("KTs_ready", 1)
        QT_ready = sig("QT_even_ready", 4), sig("QT_odd_ready", 4)
        KTx_ready = sig("KTx_even_ready", 2), sig("KTx_odd_ready", 2)
        RMS = ["ctx_kv", "self_proj", "xq"]
        raw_ready, normed = sig("raw_ready", 2), sig("normed", 2)
        ssq_ready, ms_ready, rms_ready = (sig(n, 3) for n in ("ssq_ready", "ms_ready", "rms_ready"))
        head_max, nm_step, nmp_ready = sig("head_max", 2 * NH), sig("nm_step", 8), sig("nmp_ready", 2)
        nmT_ready, nm_placed = sig("nmT_ready", 2), sig("nm_placed", 32)
        exp_ready, oT_ready = sig("exp_ready", 2 * NH), sig("oT_ready", 8)
        rden_ready, y_ready, yh_ready, yl_ready = sig("rden_ready", 4), sig("y_ready", 4), sig("yh_ready", 2), sig("yl_ready", 2)
        res_ready, x1_ready, x2_ready = sig("res_ready", 2), sig("x1_ready", 1), sig("x2_ready", 1)
        tanh_ready, fa_ready, fb_ready = (sig(n, NCH) for n in ("tanh_ready", "fa_ready", "fb_ready"))
        fc_ready, cb_ready = sig("fc_ready", NEC), sig("cb_ready", (NEC + 1) // 2)
        ah_ready, al_ready, down_done = (sig(n, NCH) for n in ("ah_ready", "al_ready", "down_done"))
        lgT_ready, gate_step, gate_exp = sig("lgT_ready", 1), sig("gate_step", NR - 1), sig("gate_exp", 1)
        cp_ready, cpT_ready, x3_ready, out_done = sig("cp_ready", 1), sig("cpT_ready", 1), sig("x3_ready", 1), sig("out_done", 16)

        g_readers = {"ln1_T": [(xl_ready[1], 1)], "ctx_kv": [(v_ctx, t + 1) for t in range(TT)],
                     "self_T": [(KTs_ready, 1)] + [(QT_ready[i % 2], i // 2 + 1) for i in range(4)],
                     "ctx_T": [(KTx_ready[i % 2], i // 2 + 1) for i in range(4)], "x_T": [(QT_ready[i % 2], i // 2 + 3) for i in range(4)],
                     "self_nm": [(nmT_ready, 1)], "x_nm": [(nmT_ready, 2)],
                     "self_o": [(y_ready, 1), (y_ready, 2)], "self_y": [(yl_ready, 1)],
                     "self_proj": [(res_ready, 1)], "xq": [(raw_ready, 2)]}
        for kind, signal in (("_max", head_max), ("_attn", exp_ready)):
            for k, name in enumerate(("self", "x")):
                for g in range(4):
                    g_readers[f"{name}{kind}{g}"] = [(signal, k * NH + 4 * g + j + 1) for j in range(4)]
        G = Ring(bank[0:4], sem("g_ready"), [((st, i), r) for st in ATTN for i, r in enumerate(g_readers.get(st, ()))])
        O = Ring([bank[4]], sem("pv_ready"),
                 [((st, g), (oT_ready, 4 * k + g + 1)) for k, st in enumerate(("self_attn", "x_attn")) for g in range(4)])
        H = Ring([bank[4]], sem("head_ready"), [(("ln0_T", 0), (xl_ready[0], 1)), (("qkv", 0), (v_self, 1)),
                                                 (("qkv", 1), (v_self, 2))], wrap=False)
        R = Ring([bank[4]], sem("tail_ready"), [(("x_o", 0), (y_ready, 3)), (("x_o", 1), (y_ready, 4)), (("x_y", 0), (yl_ready, 2)),
                                                 (("x_proj", 0), (res_ready, 2)), (("ln2_T", 0), (xl_ready[2], 1))], wrap=False)
        f_uses = []
        for n, c in enumerate(CHUNKS):
            if n == 3:
                f_uses.append((("router", 2), (cpT_ready, 1)))
            f_uses.append((("gu", n), (fb_ready, n + 1)))
            if n == 1:
                f_uses.append((("router", 1), (gate_step, 2)))
            if c < NEC and c % 2 == 0:
                f_uses.append((("cb", c // 2), (cb_ready, c // 2 + 1)))
        FR = Ring([bank[5], bank[6]], sem("f_ready"), f_uses, wrap=False)

        pieces = [(by_row_chunk("w_attn"), wqkv[0][:], wqkv[1][:]),
                  (by_row_chunk("k_img_w"), wkv[0][:, :, 0:D], wkv[1][:, :, 0:D]),
                  (by_row_chunk("v_img_w"), wkv[0][:, :, D:], wkv[1][:, :, D:]),
                  (by_row_chunk("w_proj"), wp[0][:], wp[1][:]),
                  (by_row_chunk("q_w"), wq[0][:], wq[1][:]),
                  (by_row_chunk("o_w"), wo[0][:], wo[1][:])]
        NSMALL = len(pieces)
        for name, w, n in (("wg", wg, GW), ("wu", wu, FT)):
            for c in range(KC):
                for s0, s1 in ((0, n // 2), (n // 2, n)):
                    pieces.append((a[name][c * P:(c + 1) * P, s0:s1].unsqueeze(1), w[0][:, c:c + 1, s0:s1], w[1][:, c:c + 1, s0:s1]))
        for c0 in range(0, NCH - 1, 3):
            c1 = min(c0 + 3, NCH - 1)
            pieces.append((a["wd"][c0 * P:c1 * P, :].rearrange("(c p) n -> p c n", p=P), wd[0][:, c0:c1], wd[1][:, c0:c1]))
        pieces.append((a["wd"][(NCH - 1) * P:FT, :].unsqueeze(1), wd[0][0:FLAST, NCH - 1:NCH], wd[1][0:FLAST, NCH - 1:NCH]))
        NPIECE = len(pieces)
        W_AFTER, late = {"self_split": range(1, 3)}, 3
        for st, n in (("ctx_split", 2), ("ctx_T", 1), ("self_attn0", 1), ("self_attn1", 1), ("self_attn2", 1), ("self_attn3", 1),
                      ("x_T", 4), ("x_nm", 2), ("x_attn0", 1), ("x_attn1", 1), ("x_attn2", 1), ("x_attn3", 1)):
            W_AFTER[st] = range(late, late + n)
            late += n
        assert late == NPIECE

        def staged(n):
            rows_, c, w = pieces[n][1].shape
            assert c * w <= STAGE
            return stage[0:rows_, n % 2, 0:c * w].rearrange("p (c n) -> p c n", c=c)

        def heads(ap):
            return ap.rearrange("p (h c) -> p h c", c=HD)

        QPOS, KPOS = (slice(1, 6, 2), slice(0, 3, 2), 4), (slice(2, 5), slice(0, 2), 5)
        CUT = {"q": (lambda t: heads(rot[:, t, 0:NH * HD]), stack, NH, QPOS),
               "k": (lambda t: heads(rot[:, t, NH * HD:]), stack_k, NKV, KPOS),
               "ck": (lambda t: heads(kn[:, t]), stack, NH, KPOS),
               "xq": (lambda t: heads(res[:, t]), stack, NH, QPOS)}

        def blocks(which, t):
            return CUT[which][1][:, t].rearrange("p h (r c) -> p h r c", c=HD)

        def move(st, copy, e, odd):
            def step(it):
                pieces_ = [(QT, g, QT_ready[g % 2]) for g in range(4)]
                if st == "self_T":
                    pieces_ = [(KT_s, 0, KTs_ready)] + pieces_
                if st == "ctx_T":
                    pieces_ = [(KT_x, g, KTx_ready[g % 2]) for g in range(4)]
                for i, (dst, g, signal) in enumerate(pieces_):
                    if g % 2 == odd:
                        e.wait_ge(*G.ready(it, (st, i)))
                        copy(dst[0:SW, 4 * g:4 * g + 4], G.bank((st, i))[0:SW, :].bitcast(BF16).rearrange("p (h s) -> p h s", s=S))\
                            .then_inc(signal.sem, 1)
            return step

        def cut_rest(e, engine, which, it):
            src, _, nh, (hpos, mpos, lpos) = CUT[which]
            for t in range(TT):
                e.wait_ge(*high_ready[which](it, t + 1))
                engine.tensor_tensor(src(t), src(t), blocks(which, t)[:, :, hpos][:, :, 0], ALU.subtract).then_inc(rest_ready[which].sem, 1)
            for t in range(TT):
                e.wait_ge(*middle_ready[which](it, t + 1))
                engine.tensor_tensor(blocks(which, t)[:, :, lpos], src(t), blocks(which, t)[:, :, mpos][:, :, 0], ALU.subtract)\
                    .then_inc(low_ready[which].sem, 1)

        def two(ap):
            return ap.rearrange("p (c n) -> p c n", c=2)

        def first(it):
            return isinstance(it, int) and it == 0

        def run(plan, it, steps, ffn_steps, attn=True, ffn=True, head=True, after=None):
            for i, st in enumerate(plan):
                name = st.rstrip("0123456789+-")
                if name == "F":
                    if ffn and ffn_steps:
                        ffn_steps(it - 1, plan[:i].count("F"))
                elif name == "r":
                    if ffn:
                        steps["router"](it - 1, plan[:i].count("r"))
                elif st[-1] == "-":
                    if ffn and name in steps:
                        steps[name](it - 1)
                elif st[-1] == "+":
                    if attn and head and name in steps:
                        steps[name](it + 1)
                elif attn:
                    if st in steps:
                        steps[st](it)
                    elif name in steps:
                        steps[name](it, int(st[len(name):]))
                    if after:
                        after(st)

        def program(e, plan, steps, ffn_steps, after=None, between=None):
            for st in HEAD:
                if st in steps:
                    steps[st](0)
                if after:
                    after(st)
            if between:
                between()
            run(plan, 0, steps, ffn_steps, ffn=False, after=after)
            with e.Fori(1, B - 1) as it:
                run(plan, it, steps, ffn_steps)
            run(plan, B - 1, steps, ffn_steps, head=False)
            run(plan, B, steps, ffn_steps, attn=False)

        block = ctx.enter_context(nc.Block())

        @block.sync
        def _(sp):
            def load_piece(n):
                if n >= 2:
                    sp.wait_ge(wl_ready, n - 1)
                sp.dma_start(staged(n), pieces[n][0]).then_inc(w_loaded[n % 2], 16)

            sp.dma_start(x_in[:], x_v[0]).then_inc(x_loaded.sem, 16)
            sp.dma_start(ident[:], a["ident"]).then_inc(ident_loaded, 16)
            load_piece(0)
            for dst, name in ((rope_c, "rope_c"), (rope_s, "rope_s"), (identb, "identb")):
                sp.dma_start(dst[:], a[name]).then_inc(const_loaded, 16)
            sp.dma_start(ctxT[:], a["ctxT"][0]).then_inc(ctx_loaded.sem, 16)
            load_piece(1)
            sp.dma_start(rows[:].rearrange("p r d -> p (r d)"), a["rows"].rearrange("r d -> (r d)").partition_broadcast(P)).then_inc(const_loaded, 16)
            for dst, name in ((mask_q, "mask_q"), (mask_k, "mask_k"), (sel_exp, "sel_exp"), (iota_e, "iota_e")):
                sp.dma_start(dst[:], a[name]).then_inc(const_loaded, 16)

            def place_maxima(it, k):
                sp.wait_ge(*nmT_ready(it, k + 1))
                sp.dma_start(QT[SW:SW + 3], nmT[:]).then_inc(nm_placed.sem, 16)

            def store(it):
                sp.wait_ge(*x3_ready(it, 1))
                sp.dma_start(out_v[it], x2[:]).then_inc(out_done.sem, 16)

            maxima_before = {W_AFTER["ctx_T"][0] + 2: 0, W_AFTER["x_nm"][0] + 2: 1}
            for n in range(2, NPIECE):
                if n in maxima_before:
                    place_maxima(0, maxima_before[n])
                load_piece(n)
            with sp.Fori(1, B) as it:
                place_maxima(it, 0)
                place_maxima(it, 1)
                store(it - 1)
            store(B - 1)
            sp.wait_ge(*out_done(B, 0))

        NCONST = 8

        @block.scalar
        def _(e):
            A = nc.scalar

            def weight(n):
                e.wait_ge(w_loaded[n % 2], 16 * (n // 2 + 1))
                A.copy(pieces[n][1], staged(n)).then_inc(wh_ready, 1)

            def context_high(it):
                e.wait_ge(*ctx_loaded(it, 16))
                A.copy(cT[0][:], ctxT[:]).then_inc(ch_ready.sem, 1)

            def x_load(it):
                e.wait_ge(*x1_ready(it - 1, 1))
                e.dma_start(x_in[:], x_v[it]).then_inc(x_loaded.sem, 16)

            def ctx_load(it):
                e.wait_ge(*cl_ready(it - 1, 1))
                e.wait_ge(*ch_ready(it - 1, 1))
                e.dma_start(ctxT[:], a["ctxT"][it]).then_inc(ctx_loaded.sem, 16)

            def ln(k):
                ring = (H, G, R)[k]

                def step(it):
                    e.wait_ge(*ring.ready(it, (f"ln{k}_T", 0)))
                    dst = fT[0] if k == 2 else xT[0]
                    A.copy(dst[:], two(ring.bank((f"ln{k}_T", 0))[:])).then_inc(xh_ready[k].sem, 1)
                return step

            def cut(which, it, source_ready):
                src, _, nh, (hpos, mpos, _) = CUT[which]
                for t in range(TT):
                    e.wait_ge(*source_ready(t))
                    A.copy(blocks(which, t)[:, :, hpos], src(t).unsqueeze(2).to_broadcast([P, nh, 3, HD])).then_inc(high_ready[which].sem, 1)
                for t in range(TT):
                    e.wait_ge(*rest_ready[which](it, t + 1))
                    A.copy(blocks(which, t)[:, :, mpos], src(t).unsqueeze(2).to_broadcast([P, nh, 2, HD])).then_inc(middle_ready[which].sem, 1)

            def self_split(it):
                if not first(it):
                    e.wait_ge(*G.ready(it - 1, ("x_T", 3)))
                cut("q", it, lambda t: rot_ready(it, t + 1))
                cut("k", it, lambda t: rot_ready(it, t + 1))

            def ctx_split(it):
                e.wait_ge(*G.ready(it, ("self_T", 4)))
                cut("ck", it, lambda t: normed(it, 1))

            def x_split(it):
                cut("xq", it, lambda t: normed(it, 2))

            def sumsq(st, src, ready):
                r = RMS.index(st)

                def step(it):
                    e.wait_ge(*ready(it))
                    for t in range(TT):
                        ins = A.activation(rot2[:, t, 0:D // 2].bitcast(BF16), src(t), ACT.Square, scale=D ** -0.5, accum_out=ssq[:, r, t:t + 1])
                    ins.then_inc(ssq_ready.sem, 1)
                return step

            def exps(kind, width):
                st = kind + "_attn"

                def step(it, g):
                    for j in range(4):
                        key = (f"{st}{g}", j)
                        n = 4 * g + j + (NH if kind == "x" else 0)
                        e.wait_ge(*G.ready(it, key))
                        groups = max((n - PSLOTS) // 4 + 1, 0)
                        if groups or not first(it):
                            e.wait_ge(O.ready_sem, it * O.total + groups)
                        A.activation(prob[:, n % PSLOTS, 0:width], G.bank(key)[:, 0:width], ACT.Exp, scale=HD ** -0.5)\
                            .then_inc(exp_ready.sem, 1)
                return step

            def y_high(kind):
                ring = R if kind == "x" else G

                def step(it):
                    key = (kind + "_y", 0)
                    e.wait_ge(*ring.ready(it, key))
                    A.copy(xT[0][:], two(ring.bank(key)[:])).then_inc(yh_ready.sem, 1)
                return step

            pb = ("self_proj", 0)
            steps = {**{st: move(st, A.copy, e, 1) for st in ("self_T", "ctx_T", "x_T")},
                     "x_load": x_load, "ctx_load": ctx_load, "ctx": context_high,
                     "ln0_T": ln(0), "ln1_T": ln(1), "ln2_T": ln(2), "self_split": self_split, "ctx_split": ctx_split, "x_split": x_split,
                     "ctx_kv": sumsq("ctx_kv", lambda t: kn[:, t], lambda it: raw_ready(it, 1)),
                     "xq": sumsq("xq", lambda t: res[:, t], lambda it: raw_ready(it, 2)),
                     "self_proj": sumsq("self_proj", lambda t: G.bank(pb)[:, t * D:(t + 1) * D], lambda it: G.ready(it, pb)),
                     "self_attn": exps("self", S + P), "x_attn": exps("x", 2 * S), "self_y": y_high("self"), "x_y": y_high("x")}

            def ffn(it, n):
                if n < NCH:
                    r = P if CHUNKS[n] < NCH - 1 else FLAST
                    e.wait_ge(*FR.ready(it, ("gu", n)))
                    if n >= 2:
                        e.wait_ge(*al_ready(it, n - 1))
                    A.activation(act[0:r, n % 2], FR.bank(("gu", n))[0:r, 0:S], ACT.Tanh, scale=0.5).then_inc(tanh_ready.sem, 1)
                if n < NCH and CHUNKS[n] < NEC and CHUNKS[n] % 2 == 0:
                    j = CHUNKS[n] // 2
                    e.wait_ge(*FR.ready(it, ("cb", j)))
                    if j >= 2:
                        e.wait_ge(*fc_ready(it, 2 * (j - 1)))
                    w = 2 * S if CHUNKS[n] + 1 < NEC else S
                    A.copy(cb[:, j % 2, 0:w], FR.bank(("cb", j))[:, 0:w]).then_inc(cb_ready.sem, 1)
                if 1 <= n <= NCH:
                    m = n - 1
                    c = CHUNKS[m]
                    r = P if c < NCH - 1 else FLAST
                    e.wait_ge(*(fc_ready(it, c + 1) if c < NEC else fb_ready(it, m + 1)))
                    if m >= 2:
                        e.wait_ge(*down_done(it, m - 1))
                    A.copy(act_p[0][0:r, m % 2], act[0:r, m % 2]).then_inc(ah_ready.sem, 1)
                if n == 1:
                    e.wait_ge(*gate_step(it, 2))
                    A.activation(gt[:, 1], gt[:, 0], ACT.Exp).then_inc(gate_exp.sem, 1)

            weight(0)
            program(e, PLAN["scalar"], steps, ffn, lambda st: [weight(n) for n in W_AFTER.get(st, ())])

        @block.gpsimd
        def _(e):
            L = nc.gpsimd

            def weight(n):
                e.wait_ge(wh_ready, n + 1)
                L.tensor_tensor(pieces[n][2], staged(n), pieces[n][1], ALU.subtract).then_inc(wl_ready, 1)

            def rotated(it):
                for t in range(TT):
                    e.wait_ge(*rope_parts(it, t + 1))
                    L.tensor_tensor(rot[:, t], rot[:, t], rot2[:, t], ALU.add).then_inc(rot_ready.sem, 1)

            def context_low(it):
                e.wait_ge(*ch_ready(it, 1))
                L.tensor_tensor(cT[1][:], ctxT[:], cT[0][:], ALU.subtract).then_inc(cl_ready.sem, 1)

            def ln(k):
                def step(it):
                    e.wait_ge(*ln_mv[k](it, 1))
                    L.tensor_tensor(ve[:], mv[:, :, 1], eps[:, 0], ALU.add).then_inc(ln_ve[k].sem, 1)
                    e.wait_ge(*ln_ve[k](it, 1))
                    L.tensor_tensor(rstd[:], ve[:], neghalf[:], ALU.pow).then_inc(ln_rstd[k].sem, 1)
                return step

            def rms(st):
                r = RMS.index(st)

                def step(it):
                    e.wait_ge(*ssq_ready(it, r + 1))
                    L.tensor_tensor(ms[:, r], ssq[:, r], eps[:, 1], ALU.add).then_inc(ms_ready.sem, 1)
                    e.wait_ge(*ms_ready(it, r + 1))
                    L.tensor_tensor(rrms[:, r], ms[:, r], neghalf[:], ALU.pow).then_inc(rms_ready.sem, 1)
                return step

            steps = {"ctx": context_low, "qkv": rotated, "ln0s": ln(0), "ln1s": ln(1), "ln2s": ln(2),
                     "self_split": lambda it: (cut_rest(e, L, "q", it), cut_rest(e, L, "k", it)),
                     "ctx_split": lambda it: cut_rest(e, L, "ck", it),
                     "ctx_kv": rms("ctx_kv"), "self_proj": rms("self_proj"), "xq": rms("xq")}

            def ffn(it, n):
                if 1 <= n <= NCH:
                    m = n - 1
                    r = P if CHUNKS[m] < NCH - 1 else FLAST
                    e.wait_ge(*ah_ready(it, m + 1))
                    L.tensor_tensor(act_p[1][0:r, m % 2], act[0:r, m % 2], act_p[0][0:r, m % 2], ALU.subtract).then_inc(al_ready.sem, 1)
                if n < NCH and CHUNKS[n] < NEC:
                    c = CHUNKS[n]
                    e.wait_ge(*cb_ready(it, c // 2 + 1))
                    e.wait_ge(*fb_ready(it, n + 1))
                    L.tensor_tensor(act[:, n % 2], act[:, n % 2], cb[:, c // 2 % 2, c % 2 * S:(c % 2 + 1) * S], ALU.mult).then_inc(fc_ready.sem, 1)

            L.memset(eps[:, 0], LN_EPS)
            L.memset(eps[:, 1], RMS_EPS)
            L.memset(neghalf[:], -0.5).then_inc(pool_const, 1)
            e.wait_ge(pool_const, 1)
            weight(0)
            program(e, PLAN["gpsimd"], steps, ffn, lambda st: [weight(n) for n in W_AFTER.get(st, ())])

        @block.vector
        def _(e):
            V = nc.vector

            def carry(signal, count):
                e.wait_ge(signal, count)
                V.memset(idle[:], 0.0)

            def ln_stats_of(k):
                src = (x_in, x1, x2)[k]

                def step(it):
                    if k == 0:
                        e.wait_ge(*x_loaded(it, 16))
                    else:
                        e.wait_ge(*(x1_ready, x2_ready)[k - 1](it, 1))
                    for t in range(TT):
                        ins = V.bn_stats(bn[:, t], src[:, t])
                    ins.then_inc(ln_stats[k].sem, 1)
                    carry(*ln_stats[k](it, 1))
                    for t in range(TT):
                        ins = V.bn_aggr(mv[:, t], bn[:, t])
                    ins.then_inc(ln_mv[k].sem, 1)
                return step

            def ln(k):
                src = (x_in, x1, x2)[k]

                def step(it):
                    e.wait_ge(*ln_rstd[k](it, 1))
                    for t in range(TT):
                        ins = V.tensor_scalar(xn[:, t], src[:, t], mv[:, t, 0:1], rstd[:, t:t + 1], ALU.subtract, ALU.mult)
                    ins.then_inc(xn_ready[k].sem, 1)
                return step

            def ln_low(k):
                ring = (H, G, R)[k]

                def step(it):
                    key = (f"ln{k}_T", 0)
                    e.wait_ge(*xh_ready[k](it, 1))
                    hl = fT if k == 2 else xT
                    V.tensor_tensor(hl[1][:], two(ring.bank(key)[:]), hl[0][:], ALU.subtract).then_inc(xl_ready[k].sem, 1)
                return step

            def qkv(it):
                pair = lambda ap, n: ap.rearrange("p (h c j) -> p h c j", c=HD // 2, j=2)
                n = NH + NKV
                if first(it):
                    e.wait_ge(const_loaded, 16 * NCONST)
                for t in range(TT):
                    key = ("qkv", t)
                    e.wait_ge(*H.ready(it, key))
                    ps = H.bank(key)
                    qk = pair(ps[:, 0:n * HD], n)
                    cs = rope_c[:, t].rearrange("p (c j) -> p c j", j=2)
                    sn = rope_s[:, t].rearrange("p (c j) -> p c j", j=2)
                    V.tensor_tensor(heads(rot[:, t]), heads(ps[:, 0:n * HD]), rope_c[:, t].unsqueeze(1).to_broadcast([P, n, HD]), ALU.mult)
                    for j in range(2):
                        ins = V.tensor_tensor(pair(rot2[:, t], n)[:, :, :, j], qk[:, :, :, 1 - j],
                                              sn[:, :, j].unsqueeze(1).to_broadcast([P, n, HD // 2]), ALU.mult)
                    ins.then_inc(rope_parts.sem, 1)
                    V.tensor_copy(V_s[:, t, :, 0:HD], heads(ps[:, n * HD:QKV])).then_inc(v_self.sem, 1)

            def ctx_kv(it):
                for t in range(TT):
                    key = ("ctx_kv", t)
                    e.wait_ge(*G.ready(it, key))
                    ps = G.bank(key)
                    ins = V.tensor_tensor(kn[:, t], ps[:, 0:D], rows[:, K_BIAS], ALU.add)
                    if t == TT - 1:
                        ins.then_inc(raw_ready.sem, 1)
                    V.tensor_tensor(V_x[:, t, :, 0:HD], heads(ps[:, D:]), heads(rows[:, V_BIAS]), ALU.add).then_inc(v_ctx.sem, 1)

            def norm(st, buf, row):
                r = RMS.index(st)

                def step(it):
                    e.wait_ge(*rms_ready(it, r + 1))
                    for t in range(TT):
                        ins = V.scalar_tensor_tensor(buf[:, t], buf[:, t], rrms[:, r, t:t + 1], rows[:, row], ALU.mult, ALU.mult)
                    ins.then_inc(normed.sem, 1)
                return step

            def row_max(kind):
                st = kind + "_max"

                def step(it, h):
                    key = (f"{st}{h // 4}", h % 4)
                    e.wait_ge(*G.ready(it, key))
                    ps = G.bank(key)
                    if kind == "self":
                        ins = V.tensor_reduce(mx[:, h], ps[:, 0:3 * P].rearrange("p (b k) -> p b k", k=P), AX.X, ALU.max)
                    else:
                        ins = V.tensor_reduce(mx[:, h, 0:TT], two(ps[:]), AX.X, ALU.max)
                    ins.then_inc(head_max.sem, 1)
                    if h < NH - 1:
                        return
                    k = 0 if kind == "self" else 1
                    e.wait_ge(*head_max(it, (k + 1) * NH))
                    if kind == "self":
                        V.tensor_copy(nmx[:, 0], mx[:, :, 0])
                        V.tensor_tensor(nmx[:, 1], mx[:, :, 1], mx[:, :, 2], ALU.max).then_inc(nm_step.sem, 1)
                    else:
                        V.tensor_copy(nmx[:], mx[:, :, 0:TT].rearrange("p h t -> p t h")).then_inc(nm_step.sem, 1)
                    e.wait_ge(*nm_step(it, 4 * k + 1))
                    V.tensor_scalar(nmp[:, :, 0], nmx[:], -1.0, None, ALU.mult).then_inc(nm_step.sem, 1)
                    e.wait_ge(*nm_step(it, 4 * k + 2))
                    V.scalar_tensor_tensor(nmr[:], nmx[:], -1.0, nmp[:, :, 0], ALU.mult, ALU.subtract).then_inc(nm_step.sem, 1)
                    e.wait_ge(*nm_step(it, 4 * k + 3))
                    V.tensor_copy(nmp[:, :, 1], nmr[:]).then_inc(nm_step.sem, 1)
                    e.wait_ge(*nm_step(it, 4 * k + 4))
                    V.tensor_tensor(nmp[:, :, 2], nmr[:], nmp[:, :, 1], ALU.subtract).then_inc(nmp_ready.sem, 1)
                return step

            def nm_out(kind):
                def step(it):
                    key = (kind + "_nm", 0)
                    e.wait_ge(*G.ready(it, key))
                    V.tensor_copy(nmT[:], G.bank(key)[0:3 * NH, 0:S]).then_inc(nmT_ready.sem, 1)
                return step

            def attn(kind):
                st = kind + "_attn"

                def step(it, after):
                    for g in ((), (0,), (1,), (2, 3))[after]:
                        e.wait_ge(*O.ready(it, (st, g)))
                        V.tensor_copy(oT[:, g], O.bank((st, g))[:, 0:S]).then_inc(oT_ready.sem, 1)
                return step

            def out_tokens(kind):
                ring = R if kind == "x" else G

                k = 0 if kind == "self" else 1

                def step(it):
                    for t in range(TT):
                        key = (kind + "_o", t)
                        e.wait_ge(*ring.ready(it, key))
                        ps = ring.bank(key)[:].rearrange("p (h c) -> p h c", c=VW)
                        V.reciprocal(rden[:, t], ps[:, :, HD]).then_inc(rden_ready.sem, 1)
                        e.wait_ge(*rden_ready(it, k * TT + t + 1))
                        V.tensor_tensor(heads(xn[:, t]), ps[:, :, 0:HD], rden[:, t].unsqueeze(2).to_broadcast([P, NH, HD]), ALU.mult)\
                            .then_inc(y_ready.sem, 1)
                return step

            def y_low(kind):
                ring = R if kind == "x" else G

                k = 0 if kind == "self" else 1

                def step(it):
                    key = (kind + "_y", 0)
                    e.wait_ge(*yh_ready(it, k + 1))
                    V.tensor_tensor(xT[1][:], two(ring.bank(key)[:]), xT[0][:], ALU.subtract).then_inc(yl_ready.sem, 1)
                return step

            def self_proj(it):
                key = ("self_proj", 0)
                r = RMS.index("self_proj")
                e.wait_ge(*rms_ready(it, r + 1))
                for t in range(TT):
                    ins = V.scalar_tensor_tensor(res[:, t], G.bank(key)[:, t * D:(t + 1) * D], rrms[:, r, t:t + 1], rows[:, A_NORM],
                                                 ALU.mult, ALU.mult)
                ins.then_inc(res_ready.sem, 1)
                e.wait_ge(*res_ready(it, 1))
                V.tensor_tensor(x1[:], res[:], x_in[:], ALU.add).then_inc(x1_ready.sem, 1)

            def xq(it):
                key = ("xq", 0)
                e.wait_ge(*G.ready(it, key))
                V.tensor_tensor(res[:], two(G.bank(key)[:]), rows[:, Q_BIAS].unsqueeze(1).to_broadcast([P, TT, D]), ALU.add)\
                    .then_inc(raw_ready.sem, 1)

            def stored(it):
                carry(*out_done(it, 16))

            def x_proj(it):
                key = ("x_proj", 0)
                e.wait_ge(*R.ready(it, key))
                V.tensor_tensor(res[:], two(R.bank(key)[:]), rows[:, O_BIAS].unsqueeze(1).to_broadcast([P, TT, D]), ALU.add)\
                    .then_inc(res_ready.sem, 1)
                e.wait_ge(*res_ready(it, 2))
                V.tensor_tensor(x2[:], res[:], x1[:], ALU.add).then_inc(x2_ready.sem, 1)

            steps = {"ln0s": ln_stats_of(0), "ln1s": ln_stats_of(1), "ln2s": ln_stats_of(2), "ln0n": ln(0), "ln1n": ln(1), "ln2n": ln(2),
                     "ln0_T": ln_low(0), "ln1_T": ln_low(1), "ln2_T": ln_low(2),
                     "self_nm": nm_out("self"), "x_nm": nm_out("x"), "self_y": y_low("self"), "x_y": y_low("x"),
                     "qkv": qkv, "ctx_kv": ctx_kv, "ctx_split": norm("ctx_kv", kn, K_NORM),
                     "x_split": lambda it: (norm("xq", res, Q_NORM)(it), cut_rest(e, V, "xq", it)),
                     **{st: move(st, V.tensor_copy, e, 0) for st in ("self_T", "ctx_T", "x_T")},
                     "self_max": row_max("self"), "x_max": row_max("x"), "self_attn": attn("self"), "x_attn": attn("x"),
                     "self_o": out_tokens("self"), "x_o": out_tokens("x"), "self_proj": self_proj, "xq": xq, "x_proj": x_proj, "stored": stored}

            def router(it, k):
                lg = FR.bank(("router", 1))[:, 0:TT * E].rearrange("p (t e) -> p t e", e=E)
                wide = lambda ap: ap.unsqueeze(2).to_broadcast([P, TT, E])
                if k == 0:
                    e.wait_ge(*FR.ready(it, ("router", 1)))
                elif k in (5, 6):
                    carry(*gate_step(it, k))
                else:
                    e.wait_ge(*gate_step(it, k))
                if k == 0:
                    ins = V.tensor_reduce(gm[:, 0], lg, AX.X, ALU.max)
                elif k == 1:
                    ins = V.tensor_tensor(gt[:, 0], lg, wide(gm[:, 0]), ALU.subtract)
                elif k == 2:
                    e.wait_ge(*gate_exp(it, 1))
                    ins = V.tensor_reduce(gm[:, 1], gt[:, 1], AX.X, ALU.add)
                elif k == 3:
                    ins = V.reciprocal(gm[:, 2], gm[:, 1])
                elif k == 4:
                    ins = V.tensor_tensor(gt[:, 2], gt[:, 1], wide(gm[:, 2]), ALU.mult)
                elif k == 5:
                    for t in range(TT):
                        ins = V.max(top[:, t], gt[:, 2, t])
                elif k == 6:
                    for t in range(TT):
                        ins = V.max_index(topi[:, t], top[:, t], gt[:, 2, t])
                elif k == 7:
                    ins = V.tensor_copy(topf[:], topi[:])
                elif k == 8:
                    for j in range(2):
                        ins = V.tensor_tensor(gt[:, 3 + j], iota_e[:].unsqueeze(1).to_broadcast([P, TT, E]),
                                              topf[:, :, j:j + 1].to_broadcast([P, TT, E]), ALU.is_equal)
                elif k == 9:
                    ins = V.tensor_tensor(gt[:, 3], gt[:, 3], gt[:, 4], ALU.add)
                elif k == 10:
                    ins = V.tensor_tensor(gt[:, 5], gt[:, 3], gt[:, 2], ALU.mult)
                elif k == 11:
                    ins = V.tensor_copy(cp[:, :, 0], gt[:, 5])
                elif k == 12:
                    ins = V.tensor_tensor(gt[:, 4], gt[:, 5], cp[:, :, 0], ALU.subtract)
                elif k == 13:
                    ins = V.tensor_copy(cp[:, :, 1], gt[:, 4])
                else:
                    ins = V.tensor_tensor(cp[:, :, 2], gt[:, 4], cp[:, :, 1], ALU.subtract)
                ins.then_inc(gate_step.sem if k < NR - 1 else cp_ready.sem, 1)

            steps["router"] = router

            def ffn(it, n):
                if n == 3:
                    e.wait_ge(*FR.ready(it, ("router", 2)))
                    V.tensor_copy(cpT, FR.bank(("router", 2))[0:3 * E, 0:P].bitcast(BF16)).then_inc(cpT_ready.sem, 1)
                if n < NCH:
                    c = CHUNKS[n]
                    r = P if c < NCH - 1 else FLAST
                    ps = FR.bank(("gu", n))
                    slot = act[0:r, n % 2]
                    if n == 0:
                        e.wait_ge(*FR.ready(it, ("gu", 0)))
                        V.tensor_copy(lgT[FLAST:FLAST + E, :], ps[FLAST:FLAST + E, 0:S]).then_inc(lgT_ready.sem, 1)
                    e.wait_ge(*tanh_ready(it, n + 1))
                    V.scalar_tensor_tensor(slot, slot, 1.0, ps[0:r, 0:S], ALU.add, ALU.mult).then_inc(fa_ready.sem, 1)
                    e.wait_ge(*fa_ready(it, n + 1))
                    V.scalar_tensor_tensor(slot, slot, 0.5, ps[0:r, S:2 * S], ALU.mult, ALU.mult).then_inc(fb_ready.sem, 1)
                if n == NCH + LAG - 1:
                    e.wait_ge(*down_done(it, NCH))
                    V.tensor_tensor(x2[:], two(Y[:]), x2[:], ALU.add).then_inc(x3_ready.sem, 1)

            one_one = np.array([0x3f803f80], np.uint32).view(np.float32).item()
            V.memset(V_s[:], 0.0)
            V.memset(V_x[:], 0.0).then_inc(dve_const, 1)
            e.wait_ge(dve_const, 1)
            V.memset(V_s[:, :, :, HD:HD + 1], 1.0)
            V.memset(V_x[:, :, :, HD:HD + 1], 1.0)
            V.memset(QT[SW:P].bitcast(F32), 0.0)
            V.memset(KT_s[SW:P].bitcast(F32), one_one).then_inc(dve_const, 1)
            program(e, PLAN["vector"], steps, ffn, between=lambda: V.memset(KT_x[SW:P].bitcast(F32), one_one).then_inc(dve_const, 1))

        @block.tensor
        def _(e):
            def product(out, lhs, lcols, rhs, rcols, chunks, first=True, rows_=P):
                todo = [(c, i, j) for c in chunks for i, j in ((0, 0), (0, 1), (1, 0))]
                for n, (c, i, j) in enumerate(todo):
                    ins = e.matmul(out, lhs[i][0:rows_, c, lcols], rhs[j][0:rows_, c, rcols], start=first and n == 0, stop=n == len(todo) - 1,
                                   skip_group_check=True)
                return ins

            def tile(t):
                return slice(t * P, (t + 1) * P)

            def diagonal(ps):
                return ps[:, 0:3 * P].rearrange("p (b k) -> p b k", k=P)[:, 0:3:2]

            def weights(it, n):
                if isinstance(it, int) and it == 0:
                    e.wait_ge(wl_ready, n)

            def values_bank_free(it):
                if not first(it):
                    e.wait_ge(*oT_ready(it - 1, 4))

            def ln(k):
                ring = (H, G, R)[k]

                def step(it):
                    key = (f"ln{k}_T", 0)
                    e.wait_ge(*xn_ready[k](it, 1))
                    if k == 0:
                        values_bank_free(it)
                    if k == 0 and isinstance(it, int) and it == 0:
                        e.wait_ge(ident_loaded, 16)
                    ring.wait_free(e, it, key)
                    for c in range(KC):
                        for t in range(TT):
                            ins = e.transpose(two(ring.bank(key)[:])[:, c, tile(t)], xn[:, t, c * P:(c + 1) * P], ident[:])
                    ins.then_inc(ring.ready_sem, 1)
                return step

            def qkv(it):
                weights(it, 1)
                e.wait_ge(*xh_ready[0](it, 1))
                e.wait_ge(*xl_ready[0](it, 1))
                for t in range(TT):
                    key = ("qkv", t)
                    H.wait_free(e, it, key)
                    product(H.bank(key)[:, 0:QKV], xT, tile(t), wqkv, slice(0, QKV), range(KC)).then_inc(H.ready_sem, 1)

            def ctx_kv(it):
                weights(it, 3)
                e.wait_ge(*ch_ready(it, 1))
                e.wait_ge(*cl_ready(it, 1))
                for t in range(TT):
                    key = ("ctx_kv", t)
                    G.wait_free(e, it, key)
                    product(G.bank(key)[:], cT, tile(t), wkv, slice(0, 2 * D), range(KC)).then_inc(G.ready_sem, 1)

            def unstack(st, cuts):
                def step(it):
                    i = 0
                    for which in cuts:
                        _, stk, nh, _ = CUT[which]
                        e.wait_ge(*low_ready[which](it, TT))
                        for h0 in range(0, nh, 4):
                            key = (st, i)
                            G.wait_free(e, it, key)
                            ps = G.bank(key)[0:SW, :].bitcast(BF16).rearrange("p (h s) -> p h s", s=S)
                            for h in range(4):
                                for t in range(TT):
                                    ins = e.transpose(ps[:, h, tile(t)], stk[:, t, h0 + h, :], identb[:])
                            ins.then_inc(G.ready_sem, 1)
                            i += 1
                return step

            def self_max(it, g):
                e.wait_ge(*QT_ready[g % 2](it, g // 2 + 1))
                if g == 0:
                    e.wait_ge(*KTs_ready(it, 1))
                for h in range(4 * g, 4 * g + 4):
                    key = (f"self_max{g}", h % 4)
                    ps = G.bank(key)
                    G.wait_free(e, it, key)
                    e.matmul(diagonal(ps), identb[:], mask_q[:].unsqueeze(1).to_broadcast([P, 2, P]),
                             start=True, stop=False, skip_group_check=True)
                    e.matmul(ps[:, 0:P], QT[0:SW, h, 0:P], KT_s[0:SW, h // GQ, 0:P], start=False, stop=False, skip_group_check=True)
                    e.matmul(ps[:, P:3 * P], QT[0:SW, h, P:S], KT_s[0:SW, h // GQ, :], start=False, stop=True, skip_group_check=True)\
                        .then_inc(G.ready_sem, 1)

            def x_max(it, g):
                e.wait_ge(*QT_ready[g % 2](it, g // 2 + 3))
                e.wait_ge(*KTx_ready[g % 2](it, g // 2 + 1))
                for h in range(4 * g, 4 * g + 4):
                    key = (f"x_max{g}", h % 4)
                    G.wait_free(e, it, key)
                    for t in range(TT):
                        ins = e.matmul(G.bank(key)[:, t * S:(t + 1) * S], QT[0:SW, h, tile(t)], KT_x[0:SW, h, :], start=True, stop=True,
                                       skip_group_check=True)
                    ins.then_inc(G.ready_sem, 1)

            def attn(kind):
                st = kind + "_attn"
                k = 0 if kind == "self" else 1

                def values(it, g):
                    if kind == "self" and g == 0 and not first(it):
                        e.wait_ge(*xl_ready[2](it - 1, 1))
                    if kind == "x" and g == 0 and not (isinstance(it, int) and it == B - 1):
                        e.wait_ge(*v_self(it + 1, TT))
                    O.wait_free(e, it, (st, g))
                    out = O.bank((st, g))
                    for kt in range(TT):
                        for j in range(4):
                            h = 4 * g + j
                            if kt == 0:
                                e.wait_ge(*exp_ready(it, k * NH + h + 1))
                            v = V_s[:, kt, h // GQ, :] if kind == "self" else V_x[:, kt, h, :]
                            p = prob[:, (k * NH + h) % PSLOTS, :]
                            if kind == "self" and kt == 1:
                                o, p = out[VW * j:VW * (j + 1), P:S], p[:, S:S + P]
                            else:
                                o, p = out[VW * j:VW * (j + 1), 0:S], p[:, kt * S:(kt + 1) * S]
                            ins = e.matmul(o, v, p, start=kt == 0, stop=kt == TT - 1, skip_group_check=True, tile_position=(0, VW * j))
                    ins.then_inc(O.ready_sem, 1)

                def maxima(it):
                    key = (kind + "_nm", 0)
                    e.wait_ge(*nmp_ready(it, k + 1))
                    G.wait_free(e, it, key)
                    ps = G.bank(key)[0:3 * NH, 0:S]
                    for t in range(TT):
                        ins = e.matmul(ps[:, tile(t)], nmp[:, t].rearrange("p r h -> p (r h)"), identb[:], start=True, stop=True,
                                       skip_group_check=True)
                    ins.then_inc(G.ready_sem, 1)

                def step(it, group):
                    if group == 0:
                        if kind == "x" and first(it):
                            e.wait_ge(dve_const, 3)
                        e.wait_ge(*(v_self, v_ctx)[k](it, TT))
                        e.wait_ge(*nm_placed(it, 16 * (k + 1)))
                    for h in range(4 * group, 4 * group + 4):
                        key = (f"{st}{group}", h % 4)
                        ps = G.bank(key)
                        G.wait_free(e, it, key)
                        if kind == "self":
                            kT = KT_s[:, h // GQ]
                            e.matmul(diagonal(ps), identb[:], mask_k[:].unsqueeze(1).to_broadcast([P, 2, P]),
                                     start=True, stop=False, skip_group_check=True)
                            e.matmul(ps[:, 0:S], kT[:, 0:P], QT[:, h, :], start=False, stop=False, skip_group_check=True)
                            ins = e.matmul(ps[:, S:S + P], kT[:, P:S], QT[:, h, P:S], start=False, stop=True, skip_group_check=True)
                        else:
                            kT = KT_x[:, h]
                            e.matmul(ps[:, 0:S], kT[:, 0:P], QT[:, h, :], start=True, stop=True, skip_group_check=True)
                            ins = e.matmul(ps[:, S:2 * S], kT[:, P:S], QT[:, h, :], start=True, stop=True, skip_group_check=True)
                        ins.then_inc(G.ready_sem, 1)
                        if h % 4 == 1 and h > 4:
                            values(it, h // 4 - 1)
                    if group == 3:
                        values(it, 3)
                return maxima, step

            def to_tokens(kind):
                ring = R if kind == "x" else G

                k = 0 if kind == "self" else 1

                def step(it):
                    e.wait_ge(*oT_ready(it, 4 * (k + 1)))
                    for t in range(TT):
                        key = (kind + "_o", t)
                        ring.wait_free(e, it, key)
                        for g in range(4):
                            ins = e.transpose(ring.bank(key)[:, g * P:(g + 1) * P], oT[:, g, tile(t)], ident[:])
                        ins.then_inc(ring.ready_sem, 1)
                return step

            def y_transposed(kind):
                ring = R if kind == "x" else G

                k = 0 if kind == "self" else 1

                def step(it):
                    key = (kind + "_y", 0)
                    ring.wait_free(e, it, key)
                    e.wait_ge(*y_ready(it, (k + 1) * TT))
                    for c in range(KC):
                        for t in range(TT):
                            ins = e.transpose(two(ring.bank(key)[:])[:, c, tile(t)], xn[:, t, c * P:(c + 1) * P], ident[:])
                    ins.then_inc(ring.ready_sem, 1)
                return step

            def project(st, lhs, rhs, n, waits):
                ring = R if st == "x_proj" else G

                def step(it):
                    if st == "x_proj":
                        e.wait_ge(wl_ready, n)
                    weights(it, n)
                    for w, k in waits:
                        e.wait_ge(*w(it, k))
                    ring.wait_free(e, it, (st, 0))
                    for t in range(TT):
                        ins = product(two(ring.bank((st, 0))[:])[:, t], lhs, tile(t), rhs, slice(0, D), range(KC))
                    ins.then_inc(ring.ready_sem, 1)
                return step

            (self_nm, self_attn), (x_nm, x_attn) = attn("self"), attn("x")
            steps = {"ln0_T": ln(0), "ln1_T": ln(1), "ln2_T": ln(2), "qkv": qkv, "ctx_kv": ctx_kv,
                     "self_T": unstack("self_T", ("k", "q")), "ctx_T": unstack("ctx_T", ("ck",)), "x_T": unstack("x_T", ("xq",)),
                     "self_max": self_max, "x_max": x_max, "self_nm": self_nm, "x_nm": x_nm,
                     "self_attn": self_attn, "x_attn": x_attn, "self_o": to_tokens("self"), "x_o": to_tokens("x"),
                     "self_y": y_transposed("self"), "x_y": y_transposed("x"),
                     "self_proj": project("self_proj", xT, wp, 4, [(yh_ready, 1), (yl_ready, 1)]),
                     "xq": project("xq", xT, wq, 5, [(xh_ready[1], 1), (xl_ready[1], 1)]),
                     "x_proj": project("x_proj", xT, wo, 6, [(yh_ready, 2), (yl_ready, 2)])}

            def ffn(it, n):
                if n == 0:
                    e.wait_ge(wl_ready, NPIECE)
                    e.wait_ge(*xh_ready[2](it, 1))
                    e.wait_ge(*xl_ready[2](it, 1))
                if n == 3:
                    e.wait_ge(*cp_ready(it, 1))
                    FR.wait_free(e, it, ("router", 2))
                    for t in range(TT):
                        ins = e.transpose(FR.bank(("router", 2))[0:3 * E, 0:P].bitcast(BF16)[:, tile(t)],
                                          cp[:, t].rearrange("p r e -> p (r e)"), identb[:])
                    ins.then_inc(FR.ready_sem, 1)
                if n < NCH:
                    c = CHUNKS[n]
                    key = ("gu", n)
                    last = c == NCH - 1
                    FR.wait_free(e, it, key)
                    gc, uc = slice(c * P, GW if last else (c + 1) * P), slice(c * P, FT if last else (c + 1) * P)
                    ps = FR.bank(key)
                    product(ps[0:FLAST + E if last else P, 0:S], wg, gc, fT, slice(0, S), range(KC))
                    product(ps[0:FLAST if last else P, S:2 * S], wu, uc, fT, slice(0, S), range(KC)).then_inc(FR.ready_sem, 1)
                if n == 1:
                    e.wait_ge(*lgT_ready(it, 1))
                    FR.wait_free(e, it, ("router", 1))
                    for t in range(TT):
                        ins = e.matmul(FR.bank(("router", 1))[:, t * E:(t + 1) * E], lgT[FLAST:FLAST + E, tile(t)],
                                       ident[FLAST:FLAST + E, FLAST:FLAST + E], start=True, stop=True, skip_group_check=True)
                    ins.then_inc(FR.ready_sem, 1)
                if n < NCH and CHUNKS[n] < NEC and CHUNKS[n] % 2 == 0:
                    j = CHUNKS[n] // 2
                    FR.wait_free(e, it, ("cb", j))
                    e.wait_ge(*cpT_ready(it, 1))
                    for i in range(2 * j, min(2 * j + 2, NEC)):
                        ins = e.matmul(FR.bank(("cb", j))[:, i % 2 * S:(i % 2 + 1) * S], sel_exp[:, i, :], cpT, start=True, stop=True,
                                       skip_group_check=True)
                    ins.then_inc(FR.ready_sem, 1)
                if n >= LAG:
                    m = n - LAG
                    c = CHUNKS[m]
                    r = P if c < NCH - 1 else FLAST
                    e.wait_ge(*ah_ready(it, m + 1))
                    e.wait_ge(*al_ready(it, m + 1))
                    for t in range(TT):
                        for i, (ai, wi) in enumerate(((0, 0), (0, 1), (1, 0))):
                            ins = e.matmul(two(Y[:])[:, t], act_p[ai][0:r, m % 2, tile(t)], wd[wi][0:r, c, :],
                                           start=m == 0 and t == 0 and i == 0, stop=m == NCH - 1 and i == 2, skip_group_check=True)
                    ins.then_inc(down_done.sem, 1)

            def constants():
                e.wait_ge(const_loaded, 16 * NCONST)
                e.wait_ge(dve_const, 2)

            program(e, PLAN["tensor"], steps, ffn, between=constants)


_OUT = ((B, S, D), "float32")


def _constants(np):
    p = np.arange(P)
    pos = np.arange(S, dtype=np.float32)
    inv = (1.0 / np.float32(10000.0) ** (np.arange(0, HD, 2, dtype=np.float32) / np.float32(HD))).astype(np.float32)
    angle = (pos[:, None] * inv[None, :]).astype(np.float32)
    cos, sin = np.cos(angle), np.sin(angle)
    by_tile = lambda t: np.ascontiguousarray(t.reshape(TT, P, HD).transpose(1, 0, 2).astype(np.float32))
    sel_exp = np.zeros((3, E, NEC * P), np.float32)
    for e in range(E):
        sel_exp[:, e, e * F:(e + 1) * F] = 1.0
    return {"rope_c": by_tile(np.repeat(cos, 2, axis=1)), "rope_s": by_tile(np.stack([-sin, sin], axis=-1).reshape(S, HD)),
            "ident": np.eye(P, dtype=np.float32), "identb": np.eye(P, dtype=np.float32),
            "mask_q": np.where(p[None, :] <= p[:, None], 0.0, MASKED).astype(np.float32),
            "mask_k": np.where(p[:, None] <= p[None, :], 0.0, MASKED).astype(np.float32),
            "sel_exp": sel_exp.reshape(3 * E, NEC, P),
            "iota_e": np.tile(np.arange(E, dtype=np.float32), (P, 1))}


_BF16 = ("identb", "mask_q", "mask_k", "sel_exp")


def kernel(**inputs):
    import ml_dtypes as _ml_dtypes
    import numpy as _np
    import concourse.bacc as _bacc
    from concourse.bass_utils import run_bass_kernel_spmd as _run

    g = {n: _np.asarray(v) for n, v in inputs.items()}
    gu, sgu = g["L0_ffn_gate_up_weights"], g["L0_ffn_shared_gate_up"]
    lay = {
        "x": g["x"],
        "ctxT": g["ctx_2048"].reshape(B, S, KC, P).transpose(0, 3, 2, 1),
        "w_attn": g["L0_attn_w_attn"], "w_proj": g["L0_attn_w_proj"],
        **{n: g["L0_xattn_" + n].T for n in ("q_w", "k_img_w", "v_img_w", "o_w")},
        "wg": _np.concatenate([gu[:, :F].reshape(E * F, D), sgu[:FS], g["L0_ffn_gate_weight"]]).T,
        "wu": _np.concatenate([gu[:, F:].reshape(E * F, D), sgu[FS:]]).T,
        "wd": _np.concatenate([g["L0_ffn_down_weights"].transpose(0, 2, 1).reshape(E * F, D), g["L0_ffn_shared_down"].T]),
        "rows": _np.stack([g["L0_xattn_" + n] for n in ("q_b", "k_img_b", "v_img_b", "o_b", "norm_q_w", "norm_k_img_w")]
                          + [g["L0_attn_norm_w"]]),
        **_constants(_np)}
    nc = _bacc.Bacc("TRN2", target_bir_lowering=False, num_devices=1)
    arrays, aps = {}, {}
    for name, v in lay.items():
        v = _np.array(v, dtype=_ml_dtypes.bfloat16) if name in _BF16 else _np.ascontiguousarray(v)
        arrays["in_" + name] = v
        aps[name] = nc.dram_tensor("in_" + name, v.shape, mybir.dt.from_np(v.dtype), kind="ExternalInput").ap()
    aps["out"] = nc.dram_tensor("out_0", _OUT[0], F32, kind="ExternalOutput").ap()
    build(nc, aps)
    r = _run(nc, [arrays], core_ids=[0])
    return r.results[0]["out_0"]
```
